# Optimizing a Trainium2 kernel written in Bass

```python
import numpy as np
import jax
import jax.numpy as jnp

def _softmax(x, axis=-1):
    return jax.nn.softmax(x, axis=axis)

def _gelu(x):
    return jax.nn.gelu(x, approximate=True)

def _silu(x):
    return jax.nn.silu(x)

def _sigmoid(x):
    return jax.nn.sigmoid(x)

def _layernorm(x, axis=-1, eps=1e-05):
    m = jnp.mean(x, axis=axis, keepdims=True)
    v = jnp.var(x, axis=axis, keepdims=True)
    return (x - m) / jnp.sqrt(v + eps)

def _scatter_add(tgt, idx, src, axis=0):
    return tgt.at[idx].add(src)

def _segment_sum(src, seg, n):
    return jax.ops.segment_sum(src, seg, n)
kernel_name = 'mk_gnn_resnorm_d2_gnn_r32_f313f8'

def setup_inputs(seed: int=0):
    np.random.seed(seed)
    _w = jnp.asarray

    def _rec_inputs():
        import jax
        import jax.numpy as jnp
        _gk = jax.random.key(seed)
        x = -0.0001006 + 1 * jax.random.normal(jax.random.fold_in(_gk, 1), (50000, 96), jnp.float32)
        src = jax.random.randint(jax.random.fold_in(_gk, 2), (50000,), 0, 50000, jnp.int32)
        dst = jax.random.randint(jax.random.fold_in(_gk, 3), (50000,), 0, 50000, jnp.int32)
        _o = jnp.argsort(dst, stable=True)
        src = src[_o]
        dst = dst[_o]
        return (x, src, dst)
    x, src, dst = _rec_inputs()

    def _L0_gnn_setup():
        import jax, jax.numpy as jnp
        import numpy as np
        N_NODES = 50000
        N_EDGES = 25000
        D_MODEL = 96
        HEADS = 4
        key = jax.random.key(seed)
        ks = jax.random.split(key, 6)
        scale = 1.0 / np.sqrt(D_MODEL)
        return {'embeds': jax.random.normal(ks[0], (N_NODES, D_MODEL), dtype=jnp.float32), 'qW': jax.random.normal(ks[1], (D_MODEL, D_MODEL), dtype=jnp.float32) * scale, 'kW': jax.random.normal(ks[2], (D_MODEL, D_MODEL), dtype=jnp.float32) * scale, 'vW': jax.random.normal(ks[3], (D_MODEL, D_MODEL), dtype=jnp.float32) * scale, 'rows': jax.random.randint(ks[4], (N_EDGES,), 0, N_NODES, dtype=jnp.int32), 'cols': jax.random.randint(ks[5], (N_EDGES,), 0, N_NODES, dtype=jnp.int32)}
    _L0_gnn_all = _L0_gnn_setup()
    _L0_gnn_in = {k: v for k, v in _L0_gnn_all.items() if k in ('qW', 'kW', 'vW')}
    del _L0_gnn_all

    def _L1_gnn_setup():
        import jax, jax.numpy as jnp
        import numpy as np
        N_NODES = 50000

        def mish(y):
            return y * jnp.tanh(jax.nn.softplus(y))

        def gcn_conv(x, edge_index, W, b):
            n = x.shape[0]
            loop = jnp.arange(n, dtype=edge_index.dtype)
            src = jnp.concatenate([edge_index[0], loop])
            dst = jnp.concatenate([edge_index[1], loop])
            h = x @ W
            deg = jax.ops.segment_sum(jnp.ones_like(dst, dtype=h.dtype), dst, num_segments=n)
            dinv = jnp.where(deg > 0, jax.lax.rsqrt(deg), 0.0)
            norm = dinv[src] * dinv[dst]
            msg = h[src] * norm[:, None]
            agg = jax.ops.segment_sum(msg, dst, num_segments=n)
            return agg + b
        key = jax.random.key(seed)
        ks = jax.random.split(key, 5)
        d_in, d_out = (96, 96)
        x = jax.random.normal(ks[0], (N_NODES, d_in), dtype=jnp.float32)
        edge_index = jax.random.randint(ks[1], (2, 25000), 0, N_NODES, dtype=jnp.int64)
        W_gcn = jax.random.normal(ks[2], (d_in, d_out), dtype=jnp.float32) / np.sqrt(d_in)
        b_gcn = jnp.zeros((d_out,), dtype=jnp.float32)
        W_lin = jax.random.normal(ks[3], (d_in, d_out), dtype=jnp.float32) / np.sqrt(d_in)
        b_lin = jnp.zeros((d_out,), dtype=jnp.float32)
        return {'x': x, 'edge_index': edge_index, 'W_gcn': W_gcn, 'b_gcn': b_gcn, 'W_lin': W_lin, 'b_lin': b_lin}
    _L1_gnn_all = _L1_gnn_setup()
    _L1_gnn_in = {k: v for k, v in _L1_gnn_all.items() if k in ('W_gcn', 'b_gcn', 'W_lin', 'b_lin')}
    del _L1_gnn_all
    return {'x': x, 'src': src, 'dst': dst, 'L0_gnn_qW': _L0_gnn_in['qW'], 'L0_gnn_kW': _L0_gnn_in['kW'], 'L0_gnn_vW': _L0_gnn_in['vW'], 'L1_gnn_W_gcn': _L1_gnn_in['W_gcn'], 'L1_gnn_b_gcn': _L1_gnn_in['b_gcn'], 'L1_gnn_W_lin': _L1_gnn_in['W_lin'], 'L1_gnn_b_lin': _L1_gnn_in['b_lin']}

def reference(x, src, dst, L0_gnn_qW, L0_gnn_kW, L0_gnn_vW, L1_gnn_W_gcn, L1_gnn_b_gcn, L1_gnn_W_lin, L1_gnn_b_lin):
    import jax
    import jax.numpy as jnp

    def _L0_gnn_ref(embeds, qW, kW, vW, rows, cols):
        import jax, jax.numpy as jnp
        import numpy as np
        N_NODES = 50000
        N_EDGES = 25000
        D_MODEL = 96
        HEADS = 4
        nvar, d = embeds.shape
        dh = d // HEADS
        e = rows.shape[0]
        q = (embeds[rows] @ qW).reshape(e, HEADS, dh)
        k = (embeds[cols] @ kW).reshape(e, HEADS, dh)
        v = (embeds[cols] @ vW).reshape(e, HEADS, dh)
        scores = jnp.clip(jnp.einsum('ehd,ehd->eh', q, k), -10.0, 10.0)
        exp_s = jnp.exp(scores)
        norms = jax.ops.segment_sum(exp_s, rows, num_segments=nvar)[rows]
        w = exp_s / (norms + 1e-08)
        res = jax.ops.segment_sum(w[:, :, None] * v, rows, num_segments=nvar).reshape(nvar, d)
        return embeds + res

    def _L1_gnn_ref(x, edge_index, W_gcn, b_gcn, W_lin, b_lin):
        import jax, jax.numpy as jnp
        import numpy as np
        N_NODES = 50000

        def mish(y):
            return y * jnp.tanh(jax.nn.softplus(y))

        def gcn_conv(x, edge_index, W, b):
            n = x.shape[0]
            loop = jnp.arange(n, dtype=edge_index.dtype)
            src = jnp.concatenate([edge_index[0], loop])
            dst = jnp.concatenate([edge_index[1], loop])
            h = x @ W
            deg = jax.ops.segment_sum(jnp.ones_like(dst, dtype=h.dtype), dst, num_segments=n)
            dinv = jnp.where(deg > 0, jax.lax.rsqrt(deg), 0.0)
            norm = dinv[src] * dinv[dst]
            msg = h[src] * norm[:, None]
            agg = jax.ops.segment_sum(msg, dst, num_segments=n)
            return agg + b
        x_gcn = gcn_conv(x, edge_index, W_gcn, b_gcn)
        x_skip = x @ W_lin + b_lin
        return mish(x_gcn + x_skip)
    edge_index = jnp.stack([src, dst])
    x = _layernorm(x + _L0_gnn_ref(x, L0_gnn_qW, L0_gnn_kW, L0_gnn_vW, src, dst), axis=-1)
    x = _layernorm(x + _L1_gnn_ref(x, edge_index, L1_gnn_W_gcn, L1_gnn_b_gcn, L1_gnn_W_lin, L1_gnn_b_lin), axis=-1)
    return x

_drawn_inputs = setup_inputs


def setup_inputs(seed=0):
    import zlib

    import numpy as np

    out = dict(_drawn_inputs(seed))
    spreads = {'L1_gnn_b_gcn': (0.0, 0.1), 'L1_gnn_b_lin': (0.0, 0.1)}
    factors = {}
    for name, (base, spread) in spreads.items():
        noise = np.random.default_rng([zlib.crc32(name.encode()), seed]).standard_normal(out[name].shape)
        drawn = base * np.exp(spread * noise) if base else spread * noise
        out[name] = jnp.asarray(drawn.astype(out[name].dtype))
    for name, factor in factors.items():
        out[name] = (out[name] * factor).astype(out[name].dtype)
    return out
```

```python
import concourse.bass as bass
from concourse import mybir
from contextlib import ExitStack

F32 = mybir.dt.float32
F16 = mybir.dt.float16
I32 = mybir.dt.int32
ALU = mybir.AluOpType
ACT = mybir.ActivationFunctionType
AX = mybir.AxisListType.X


class Steps:

    def __init__(self, eng, sem, per, i):
        self.eng, self.sem, self.per, self.i, self.k = eng, sem, per, i, 0

    def done(self, ins):
        self.k += 1
        ins.then_inc(self.sem, 1)
        self.eng.wait_ge(self.sem, self.i * self.per + self.k)

    def end(self):
        assert self.k == self.per, (self.k, self.per)


def gnn(nc, x, src, dst, qW, kW, vW, gW, gb, lW, lb, out):
    N, D = x.shape
    E = src.shape[0]
    H = 4
    DH = D // H
    P = 128
    ET = -(-E // P)
    ET += ET % 2
    LASTE = E - (P - 1) * ET
    NT = -(-N // P)
    LASTN = N - (NT - 1) * P
    A = D + H
    DUMP = N
    ROWS = N + P + (-(N + P)) % P
    EPS_LN = 1e-5

    with ExitStack() as ctx:
        def sb(name, shape, dt=F32):
            return ctx.enter_context(nc.sbuf_tensor(name, shape, dt))

        def ps(name, shape, dt=F32):
            return ctx.enter_context(nc.psum_tensor(name, shape, dt))

        def sem(name):
            return ctx.enter_context(nc.semaphore(name))

        sums0 = nc.dram_tensor("sums0", (ROWS, A), F32).ap()
        sums1 = nc.dram_tensor("sums1", (ROWS, D), F32).ap()
        x1_rows = nc.dram_tensor("x1_rows", (N, D), F32).ap()
        x1s_rows = nc.dram_tensor("x1s_rows", (N, D), F32).ap()

        src_i = sb("src_i", [P, ET], I32)
        dst_i = sb("dst_i", [P, ET], I32)
        src_f = sb("src_f", [P, ET])
        dst_f = sb("dst_f", [P, ET])
        q_w = sb("q_w", [D, D])
        kv_w = sb("kv_w", [D, 2 * D])
        g_w = sb("g_w", [D, D])
        l_w = sb("l_w", [D, D])
        bias2 = sb("bias2", [2, D])
        ones = sb("ones", [P, P])
        ident = sb("ident", [P, P])
        below = sb("below", [P, P])
        dump = sb("dump", [P, 1])
        zero = sb("zero", [P, 25 * A])
        dinv = sb("dinv", [P, NT])
        eps = sb("eps", [P, 1])

        with ExitStack() as c1:
            s_ld = sem("s_loaded")
            s_w = sem("s_weights")
            s_zero = sem("s_zero_tile")
            s_z = sem("s_sums_zeroed")
            s_pad = sem("s_pads_set")
            s_c = sem("s_constants")
            dump_i = sb("dump_i", [P, 1], I32)
            block = c1.enter_context(nc.Block())

            @block.sync
            def _(sp):
                sp.wait_ge(s_pad, 2)
                for t, s in ((src_i, src), (dst_i, dst)):
                    sp.dma_start(t[0:P - 1, :], s[0:(P - 1) * ET].rearrange("(p t) -> p t", t=ET)).then_inc(s_ld, 16)
                    sp.dma_start(t[P - 1:P, 0:LASTE], s[(P - 1) * ET:E].rearrange("(p t) -> p t", p=1)).then_inc(s_ld, 16)
                for t, s in ((q_w[:, :], qW), (kv_w[:, 0:D], kW), (kv_w[:, D:2 * D], vW), (g_w[:, :], gW), (l_w[:, :], lW)):
                    sp.dma_start(t, s).then_inc(s_w, 16)
                for r, s in enumerate((gb, lb)):
                    sp.dma_start(bias2[r:r + 1, :], s.rearrange("(a n) -> a n", a=1)).then_inc(s_w, 16)
                sp.wait_ge(s_w, 16 * 7)
                sp.wait_ge(s_ld, 16 * 4)

            @block.scalar
            def _(act):
                act.wait_ge(s_zero, 1)
                n = 0
                for tab, w in ((sums0, A), (sums1, D)):
                    flat = tab.rearrange("r w -> (r w)").rearrange("(p f) -> p f", p=P)
                    step = 25 * A
                    for c in range(0, flat.shape[1], step):
                        m = min(step, flat.shape[1] - c)
                        act.dma_start(flat[:, c:c + m], zero[:, 0:m]).then_inc(s_z, 16)
                        n += 1
                act.wait_ge(s_z, 16 * n)

            @block.gpsimd
            def _(pool):
                pool.memset(ident[:, :], 0.0).then_inc(s_c, 1)
                pool.memset(below[:, :], 0.0).then_inc(s_c, 1)
                pool.iota(dump_i[:, :], pattern=[[0, 1]], base=DUMP, channel_multiplier=1).then_inc(s_c, 1)
                pool.wait_ge(s_c, 3)
                pool.affine_select(out=ident[:, :], in_=ident[:, :], compare_op=ALU.not_equal, fill=1.0,
                                   base=0, pattern=[[-1, P]], channel_multiplier=1).then_inc(s_c, 1)
                pool.affine_select(out=below[:, :], in_=below[:, :], compare_op=ALU.is_ge, fill=1.0,
                                   base=0, pattern=[[1, P]], channel_multiplier=-1).then_inc(s_c, 1)
                pool.wait_ge(s_c, 5)

            @block.vector
            def _(dve):
                dve.memset(src_i[:, :], DUMP + P - 1).then_inc(s_pad, 1)
                dve.memset(dst_i[:, :], DUMP + P - 1).then_inc(s_pad, 1)
                dve.memset(zero[:, :], 0.0).then_inc(s_zero, 1)
                dve.memset(eps[:, :], EPS_LN).then_inc(s_zero, 1)
                dve.memset(ones[:, :], 1.0).then_inc(s_zero, 1)
                dve.wait_ge(s_c, 3)
                dve.tensor_copy(dump[:, :], dump_i[:, :]).then_inc(s_zero, 1)
                dve.wait_ge(s_ld, 16 * 4)
                dve.tensor_copy(src_f[:, :], src_i[:, :]).then_inc(s_pad, 1)
                dve.tensor_copy(dst_f[:, :], dst_i[:, :]).then_inc(s_pad, 1)
                dve.wait_ge(s_pad, 4)
                dve.tensor_scalar_min(src_i[:, :], src_f[:, :], float(N - 1)).then_inc(s_pad, 1)
                dve.tensor_scalar_min(dst_i[:, :], dst_f[:, :], float(N - 1)).then_inc(s_pad, 1)
                dve.wait_ge(s_pad, 6)
                dve.wait_ge(s_zero, 4)

        with ExitStack() as c2:
            hi_i = c2.enter_context(nc.sbuf_tensor("hi_i", [P, ET], I32))
            lo_i = c2.enter_context(nc.sbuf_tensor("lo_i", [P, ET], I32))
            hi_f = c2.enter_context(nc.sbuf_tensor("hi_f", [P, ET], F32))
            lo_f = c2.enter_context(nc.sbuf_tensor("lo_f", [P, ET], F32))
            cols_i = c2.enter_context(nc.sbuf_tensor("cols_i", [P, NT], I32))
            cols = c2.enter_context(nc.sbuf_tensor("cols", [P, NT], F16))
            hot_hi = c2.enter_context(nc.sbuf_tensor("hot_hi", [P, 2, NT], F16))
            hot_lo = c2.enter_context(nc.sbuf_tensor("hot_lo", [P, 2, P], F16))
            logdeg = c2.enter_context(nc.sbuf_tensor("logdeg", [P, NT], F32))
            deg = c2.enter_context(nc.psum_tensor("deg", [P, NT], F32))
            s_iota = sem("s_iota")
            s_hot = sem("s_one_hots")
            s_cnt = sem("s_counted")
            s_k = sem("s_keys_split")
            s_log = sem("s_logdeg")
            block = c2.enter_context(nc.Block())

            @block.gpsimd
            def _(pool):
                pool.iota(cols_i[:, :], pattern=[[1, NT]], base=0, channel_multiplier=0).then_inc(s_iota, 1)

            @block.vector
            def _(dve):
                dve.wait_ge(s_iota, 1)
                dve.tensor_copy(cols[:, :], cols_i[:, :]).then_inc(s_k, 1)
                dve.tensor_copy(lo_i[:, :], dst_f[:, :]).then_inc(s_k, 1)
                dve.wait_ge(s_k, 2)
                dve.tensor_single_scalar(hi_i[:, :], lo_i[:, :], 7, ALU.arith_shift_right).then_inc(s_k, 1)
                dve.wait_ge(s_k, 3)
                dve.tensor_single_scalar(lo_i[:, :], lo_i[:, :], P - 1, ALU.bitwise_and).then_inc(s_k, 1)
                dve.wait_ge(s_k, 4)
                dve.tensor_copy(hi_f[:, :], hi_i[:, :]).then_inc(s_k, 1)
                dve.tensor_copy(lo_f[:, :], lo_i[:, :]).then_inc(s_k, 1)
                dve.wait_ge(s_k, 6)
                for b in range(2):
                    dve.tensor_scalar(hot_hi[:, b, :], cols[:, :], hi_f[:, b:b + 1], None, ALU.is_equal).then_inc(s_hot, 1)
                    dve.tensor_scalar(hot_lo[:, b, :], cols[:, 0:P], lo_f[:, b:b + 1], None, ALU.is_equal).then_inc(s_hot, 1)
                with dve.Fori(1, ET // 2) as i:
                    for b in range(2):
                        dve.wait_ge(s_cnt, i * 2 + b - 1)
                        dve.tensor_scalar(hot_hi[:, b, :], cols[:, :], hi_f[:, bass.ds(i * 2 + b, 1)], None, ALU.is_equal).then_inc(s_hot, 1)
                        dve.tensor_scalar(hot_lo[:, b, :], cols[:, 0:P], lo_f[:, bass.ds(i * 2 + b, 1)], None, ALU.is_equal).then_inc(s_hot, 1)

            @block.tensor
            def _(pe):
                for t in range(2):
                    pe.wait_ge(s_hot, 2 * t + 2)
                    pe.matmul(deg[:, :], hot_lo[:, t, :], hot_hi[:, t, :], start=(t == 0), stop=False, skip_group_check=True).then_inc(s_cnt, 1)
                with pe.Fori(1, ET // 2) as i:
                    for b in range(2):
                        pe.wait_ge(s_hot, i * 4 + 2 * b + 2)
                        pe.matmul(deg[:, :], hot_lo[:, b, :], hot_hi[:, b, :], start=False, stop=(b == 1), skip_group_check=True).then_inc(s_cnt, 1)

            @block.scalar
            def _(act):
                act.wait_ge(s_cnt, ET)
                act.activation(logdeg[:, :], deg[:, :], ACT.Ln, bias=ones[:, 0:1]).then_inc(s_log, 1)
                act.wait_ge(s_log, 1)
                act.activation(dinv[:, :], logdeg[:, :], ACT.Exp, scale=-0.5).then_inc(s_log, 1)
                act.wait_ge(s_log, 2)

        with ExitStack() as c3:
            def tsb(name, shape, dt=F32):
                return c3.enter_context(nc.sbuf_tensor(name, shape, dt))

            def bank(name):
                return c3.enter_context(nc.psum_tensor(name, [P, 512], F32))

            gs = tsb("e_gs", [P, 1], I32)
            gd = tsb("e_gd", [P, 1], I32)
            key = tsb("e_key", [P, 1])
            off = tsb("e_off", [P, 1])
            tidx = tsb("e_tidx", [P, 1], I32)
            rank = tsb("e_rank", [P, 1])
            move = tsb("e_move", [P, 1])
            rows = tsb("e_rows", [P, 2, D])
            rowsT = tsb("e_rowsT", [D, 2, P])
            same = tsb("e_same", [P, P])
            junk = tsb("e_junk", [P, P])
            q_sb = tsb("e_q", [P, D])
            prod = tsb("e_prod", [P, D])
            score = tsb("e_score", [P, H])
            contrib = tsb("e_contrib", [P, A])
            total = tsb("e_total", [P, A])
            pT = bank("e_pT")[:, 0:2 * P].rearrange("p (a b) -> p a b", a=2)
            pkey = bank("e_pkey")[:, 0:P]
            pq = bank("e_pq")[:, 0:D]
            pkv = bank("e_pkv")[:, 0:2 * D]
            ptot = bank("e_ptot")[:, 0:A]

            for layer in range(2):
                W = A if layer == 0 else D
                table = sums0 if layer == 0 else sums1
                key_all = src_f if layer == 0 else dst_f
                with ExitStack() as c4:
                    L = f"l{layer}_"
                    s_st = sem(L + "s_staged")
                    s_rows = sem(L + "s_rows")
                    s_T = sem(L + "s_transposed")
                    s_Tc = sem(L + "s_transposed_copied")
                    s_qkv = sem(L + "s_qkv")
                    s_q = sem(L + "s_q_copied")
                    s_dve = sem(L + "s_dve_steps")
                    s_sc = sem(L + "s_scores")
                    s_e = sem(L + "s_exp")
                    s_con = sem(L + "s_contrib")
                    s_tot = sem(L + "s_totals")
                    s_totc = sem(L + "s_totals_copied")
                    s_add = sem(L + "s_added")
                    s_carry = sem(L + "s_carry")
                    block = c4.enter_context(nc.Block())
                    DVE_STEPS = 13 if layer == 0 else 8

                    @block.vector
                    def _(dve):
                        with dve.Fori(0, ET) as i:
                            st = Steps(dve, s_dve, DVE_STEPS, i)
                            dve.wait_ge(s_add, i * 16)
                            dve.tensor_copy(gs[:, :], src_i[:, bass.ds(i, 1)]).then_inc(s_st, 1)
                            dve.tensor_copy(gd[:, :], dst_i[:, bass.ds(i, 1)]).then_inc(s_st, 1)
                            dve.tensor_copy(key[:, :], key_all[:, bass.ds(i, 1)]).then_inc(s_st, 1)
                            dve.wait_ge(s_st, i * 3 + 3)
                            st.done(dve.tensor_tensor(off[:, :], dump[:, :], key[:, :], ALU.subtract))
                            dve.wait_ge(s_T, i + 1)
                            st.done(dve.tensor_scalar(same[:, :], pkey[:, :], key[:, 0:1], None, ALU.is_equal))
                            st.done(dve.tensor_tensor(junk[:, :], same[:, :], below[:, :], ALU.mult))
                            st.done(dve.tensor_reduce(rank[:, :], junk[:, :], AX, ALU.add))
                            st.done(dve.tensor_scalar(rank[:, :], rank[:, :], 0.0, None, ALU.is_gt))
                            st.done(dve.tensor_tensor(move[:, :], rank[:, :], off[:, :], ALU.mult))
                            st.done(dve.tensor_tensor(tidx[:, :], key[:, :], move[:, :], ALU.add))
                            if layer == 0:
                                dve.wait_ge(s_qkv, i + 1)
                                dve.wait_ge(s_q, i + 1)
                                st.done(dve.tensor_tensor(prod[:, :], q_sb[:, :], pkv[:, 0:D], ALU.mult))
                                st.done(dve.tensor_reduce(score[:, :], prod[:, :].rearrange("p (h d) -> p h d", h=H), AX, ALU.add))
                                st.done(dve.tensor_scalar(score[:, :], score[:, :], 10.0, -10.0, ALU.min, ALU.max))
                                dve.sem_inc(s_sc, 1)
                                dve.wait_ge(s_e, i + 1)
                                e_b = contrib[:, D:A].unsqueeze(2).to_broadcast([P, H, DH])
                                st.done(dve.tensor_tensor(contrib[:, 0:D].rearrange("p (h d) -> p h d", h=H),
                                                          pkv[:, D:2 * D].rearrange("p (h d) -> p h d", h=H), e_b, ALU.mult))
                                st.done(dve.tensor_copy(junk[:, 0:1], rank[:, :]))
                            dve.sem_inc(s_con, 1)
                            dve.wait_ge(s_tot, i + 1)
                            st.done(dve.tensor_copy(total[:, 0:W], ptot[:, 0:W]))
                            dve.sem_inc(s_totc, 1)
                            st.end()

                    @block.gpsimd
                    def _(pool):
                        with pool.Fori(0, ET) as i:
                            pool.wait_ge(s_st, i * 3 + 3)
                            pool.sem_inc(s_carry, 1)
                            if layer == 0:
                                pool.indirect_dma_start(rows[:, 0, :], None, x[:, :],
                                                        bass.IndirectOffsetOnAxis(ap=gs[:, 0:1], axis=0)).then_inc(s_rows, 16)
                                pool.indirect_dma_start(rows[:, 1, :], None, x[:, :],
                                                        bass.IndirectOffsetOnAxis(ap=gd[:, 0:1], axis=0)).then_inc(s_rows, 16)
                            else:
                                pool.indirect_dma_start(rows[:, 0, :], None, x1s_rows[:, :],
                                                        bass.IndirectOffsetOnAxis(ap=gs[:, 0:1], axis=0)).then_inc(s_rows, 16)
                            pool.wait_ge(s_totc, i + 1)
                            pool.sem_inc(s_carry, 1)
                            pool.indirect_dma_start(table[:, :], bass.IndirectOffsetOnAxis(ap=tidx[:, 0:1], axis=0),
                                                    total[:, 0:W], None, compute_op=ALU.add).then_inc(s_add, 16)
                        pool.wait_ge(s_add, 16 * ET)

                    @block.tensor
                    def _(pe):
                        with pe.Fori(0, ET) as i:
                            pe.wait_ge(s_st, i * 3 + 3)
                            t = pe.transpose(pkey[:, :], key[:, 0:1].to_broadcast([P, P]), ident[:, :])
                            if layer == 0:
                                pe.wait_ge(s_rows, i * 32 + 32)
                                pe.sem_inc(s_carry, 1)
                                pe.transpose(pT[0:D, 0, :], rows[:, 0, :], ident[:, :])
                                t = pe.transpose(pT[0:D, 1, :], rows[:, 1, :], ident[:, :])
                            t.then_inc(s_T, 1)
                            if layer == 0:
                                pe.wait_ge(s_Tc, i + 1)
                                pe.sem_inc(s_carry, 1)
                                pe.matmul(pq[:, :], rowsT[:, 0, :], q_w[:, :], start=True, stop=True)
                                pe.matmul(pkv[:, :], rowsT[:, 1, :], kv_w[:, :], start=True, stop=True).then_inc(s_qkv, 1)
                            pe.wait_ge(s_con, i + 1)
                            if layer == 1:
                                pe.wait_ge(s_rows, i * 16 + 16)
                            pe.sem_inc(s_carry, 1)
                            pe.matmul(ptot[:, 0:W], same[:, :], contrib[:, 0:W] if layer == 0 else rows[:, 0, :],
                                      start=True, stop=True).then_inc(s_tot, 1)

                    if layer == 0:
                        @block.scalar
                        def _(act):
                            with act.Fori(0, ET) as i:
                                act.wait_ge(s_T, i + 1)
                                act.activation(rowsT[:, :, :], pT[0:D, 0:2, :], ACT.Copy).then_inc(s_Tc, 1)
                                act.wait_ge(s_qkv, i + 1)
                                act.activation(q_sb[:, :], pq[:, :], ACT.Copy).then_inc(s_q, 1)
                                act.wait_ge(s_sc, i + 1)
                                act.activation(contrib[:, D:A], score[:, :], ACT.Exp).then_inc(s_e, 1)

                if layer == 0:
                    dense(nc, ctx, locals(), 0)
        dense(nc, ctx, locals(), 1)


def dense(nc, ctx, v, layer):
    N, D, H, DH, P, NT, A, LASTN = (v[k] for k in ("N", "D", "H", "DH", "P", "NT", "A", "LASTN"))
    x, out, sums0, sums1, x1_rows, x1s_rows = (v[k] for k in ("x", "out", "sums0", "sums1", "x1_rows", "x1s_rows"))
    ident, ones, eps, dinv, g_w, l_w, bias2 = (v[k] for k in ("ident", "ones", "eps", "dinv", "g_w", "l_w", "bias2"))
    with ExitStack() as c:
        L = f"d{layer}_"

        def tsb(name, shape, dt=F32):
            return c.enter_context(nc.sbuf_tensor(L + name, shape, dt))

        def sem(name):
            return c.enter_context(nc.semaphore(L + name))

        xin = tsb("xin", [P, D])
        acc = tsb("acc", [P, A])
        agg = tsb("agg", [P, D])
        own = tsb("own", [P, D])
        rec = tsb("rec", [P, H])
        h = tsb("h", [P, D])
        stats = tsb("stats", [P, 6])
        mv = tsb("mv", [P, 2])
        lnv = tsb("lnv", [P, 1])
        rstd = tsb("rstd", [P, 1])
        y1 = tsb("y1", [P, D])
        y2 = tsb("y2", [P, D])
        rT = tsb("rT", [D, 2, P])
        num = tsb("num", [P, D])
        den = tsb("den", [P, D])
        pT = c.enter_context(nc.psum_tensor(L + "pT", [P, 512], F32))[0:D, 0:2 * P].rearrange("p (a b) -> p a b", a=2)
        py = c.enter_context(nc.psum_tensor(L + "py", [P, 512], F32))[:, 0:D]
        s_in = sem("s_in")
        s_dve = sem("s_dve_steps")
        s_var = sem("s_var")
        s_rstd = sem("s_rstd")
        s_y = sem("s_y")
        s_out = sem("s_out")
        s_act = sem("s_act_steps")
        s_agg = sem("s_agg")
        s_T = sem("s_T")
        s_Tc = sem("s_Tc")
        s_lin = sem("s_lin")
        s_e = sem("s_exp")
        s_cap = sem("s_cap")
        s_carry = sem("s_carry")
        s_bn = sem("s_bn")
        block = c.enter_context(nc.Block())
        full = NT - 1
        INS = 2 if layer == 0 else 3
        OUTS = 2 if layer == 0 else 1
        DVE_STEPS = 9 if layer == 0 else 12

        def loop(eng, body):
            with eng.Fori(0, full) as i:
                body(i, P)
            body(full, LASTN)

        @block.sync
        def _(sp):
            def body(i, n):
                at = bass.ds(i * P, n)
                sp.wait_ge(s_out, i * OUTS * 16)
                if layer == 0:
                    sp.dma_start(xin[0:n, :], x[at, :]).then_inc(s_in, 16)
                    sp.dma_start(acc[0:n, :], sums0[at, :]).then_inc(s_in, 16)
                else:
                    sp.dma_start(xin[0:n, :], x1_rows[at, :]).then_inc(s_in, 16)
                    sp.dma_start(own[0:n, :], x1s_rows[at, :]).then_inc(s_in, 16)
                    sp.dma_start(acc[0:n, 0:D], sums1[at, :]).then_inc(s_in, 16)
                sp.wait_ge(s_y, i + 1)
                if layer == 0:
                    sp.dma_start(x1_rows[at, :], y1[0:n, :]).then_inc(s_out, 16)
                    sp.dma_start(x1s_rows[at, :], y2[0:n, :]).then_inc(s_out, 16)
                else:
                    sp.dma_start(out[at, :], y1[0:n, :]).then_inc(s_out, 16)
            loop(sp, body)
            sp.wait_ge(s_out, NT * OUTS * 16)

        @block.vector
        def _(dve):
            def body(i, n):
                st = Steps(dve, s_dve, DVE_STEPS, i)
                dve.wait_ge(s_in, (i + 1) * INS * 16)
                if layer == 0:
                    st.done(dve.tensor_scalar(rec[0:n, :], acc[0:n, D:A], 1e-8, None, ALU.add))
                    st.done(dve.reciprocal(rec[0:n, :], rec[0:n, :]))
                    st.done(dve.tensor_tensor(h[0:n, :].rearrange("p (h d) -> p h d", h=H),
                                              acc[0:n, 0:D].rearrange("p (h d) -> p h d", h=H),
                                              rec[0:n, :].unsqueeze(2).to_broadcast([n, H, DH]), ALU.mult))
                    st.done(dve.scalar_tensor_tensor(h[0:n, :], xin[0:n, :], 2.0, h[0:n, :], ALU.mult, ALU.add))
                else:
                    st.done(dve.tensor_tensor(agg[0:n, :], acc[0:n, 0:D], own[0:n, :], ALU.add))
                    st.done(dve.tensor_scalar(agg[0:n, :], agg[0:n, :], dinv[0:n, bass.ds(i, 1)], None, ALU.mult))
                    dve.sem_inc(s_agg, 1)
                    dve.wait_ge(s_lin, i + 1)
                    st.done(dve.tensor_scalar(h[0:n, :], py[0:n, :], 20.0, None, ALU.min))
                    dve.sem_inc(s_cap, 1)
                    dve.wait_ge(s_e, i + 1)
                    st.done(dve.scalar_tensor_tensor(num[0:n, :], y2[0:n, :], 2.0, y2[0:n, :], ALU.add, ALU.mult))
                    st.done(dve.tensor_scalar(den[0:n, :], num[0:n, :], 2.0, None, ALU.add))
                    st.done(dve.reciprocal(den[0:n, :], den[0:n, :]))
                    st.done(dve.tensor_tensor(num[0:n, :], num[0:n, :], den[0:n, :], ALU.mult))
                    st.done(dve.tensor_tensor(num[0:n, :], num[0:n, :], py[0:n, :], ALU.mult))
                    st.done(dve.tensor_tensor(h[0:n, :], num[0:n, :], xin[0:n, :], ALU.add))
                st.done(dve.bn_stats(stats[0:n, :], h[0:n, :]))
                dve.sem_inc(s_bn, 1)
                st.done(dve.bn_aggr(mv[0:n, :], stats[0:n, :]))
                dve.sem_inc(s_var, 1)
                dve.wait_ge(s_rstd, i + 1)
                st.done(dve.tensor_scalar(y1[0:n, :], h[0:n, :], mv[0:n, 0:1], rstd[0:n, :], ALU.subtract, ALU.mult))
                if layer == 0:
                    st.done(dve.tensor_scalar(y2[0:n, :], y1[0:n, :], dinv[0:n, bass.ds(i, 1)], None, ALU.mult))
                    st.done(dve.tensor_copy(lnv[0:n, :], rstd[0:n, :]))
                dve.sem_inc(s_y, 1)
                st.end()
            loop(dve, body)

        if layer == 1:
            @block.tensor
            def _(pe):
                def body(i, n):
                    pe.wait_ge(s_agg, i + 1)
                    pe.sem_inc(s_carry, 1)
                    pe.transpose(pT[:, 0, 0:n], agg[0:n, :], ident[0:n, 0:n])
                    pe.transpose(pT[:, 1, 0:n], xin[0:n, :], ident[0:n, 0:n]).then_inc(s_T, 1)
                    pe.wait_ge(s_Tc, i + 1)
                    pe.sem_inc(s_carry, 1)
                    pe.matmul(py[0:n, :], rT[:, 0, 0:n], g_w[:, :], start=True, stop=False)
                    pe.matmul(py[0:n, :], rT[:, 1, 0:n], l_w[:, :], start=False, stop=False)
                    pe.matmul(py[0:n, :], ones[0:2, 0:n], bias2[:, :], start=False, stop=True).then_inc(s_lin, 1)
                loop(pe, body)

        @block.scalar
        def _(act):
            def body(i, n):
                if layer == 1:
                    act.wait_ge(s_T, i + 1)
                    act.activation(rT[:, :, 0:n], pT[:, :, 0:n], ACT.Copy).then_inc(s_Tc, 1)
                    act.wait_ge(s_cap, i + 1)
                    act.activation(y2[0:n, :], h[0:n, :], ACT.Exp).then_inc(s_e, 1)
                act.wait_ge(s_var, i + 1)
                act.activation(lnv[0:n, :], mv[0:n, 1:2], ACT.Ln, bias=eps[0:n, :]).then_inc(s_act, 1)
                act.wait_ge(s_act, i + 1)
                act.activation(rstd[0:n, :], lnv[0:n, :], ACT.Exp, scale=-0.5).then_inc(s_rstd, 1)
            loop(act, body)


def kernel(**inputs):
    import numpy as np
    import concourse.bacc as bacc
    from concourse.bass_utils import run_bass_kernel_spmd
    nc = bacc.Bacc("TRN2", target_bir_lowering=False, num_devices=1)
    names = ("x", "src", "dst", "L0_gnn_qW", "L0_gnn_kW", "L0_gnn_vW",
             "L1_gnn_W_gcn", "L1_gnn_b_gcn", "L1_gnn_W_lin", "L1_gnn_b_lin")
    arrays, aps = {}, []
    for n in names:
        a = np.ascontiguousarray(inputs[n])
        arrays["in_" + n] = a
        aps.append(nc.dram_tensor("in_" + n, a.shape, mybir.dt.from_np(a.dtype), kind="ExternalInput").ap())
    out = nc.dram_tensor("out", inputs["x"].shape, F32, kind="ExternalOutput").ap()
    gnn(nc, *aps, out)
    r = run_bass_kernel_spmd(nc, [arrays], core_ids=[0])
    return r.results[0]["out"]
```

```python
import concourse.bass as bass
from concourse import mybir
from contextlib import ExitStack

F32 = mybir.dt.float32
F16 = mybir.dt.float16
I32 = mybir.dt.int32
ALU = mybir.AluOpType
ACT = mybir.ActivationFunctionType
AX = mybir.AxisListType.X

P = 128
QUAD = 4
EPS_LN = 1e-5
EPS_NORM = 1e-8
LIMIT = 10.0
ROUND = 1.5 * 2 ** 23
ACT_SET = "natural_log_exp_and_others"


class Shared:
    pass


class Steps:

    def __init__(self, eng, sem, per, i):
        self.eng, self.sem, self.per, self.i, self.k = eng, sem, per, i, 0

    def done(self, ins):
        self.k += 1
        ins.then_inc(self.sem, 1)
        self.eng.wait_ge(self.sem, self.i * self.per + self.k)

    def end(self):
        assert self.k == self.per, (self.k, self.per)


class Chain:

    def __init__(self, eng, sem):
        self.eng, self.sem, self.k = eng, sem, 0

    def done(self, ins):
        self.k += 1
        ins.then_inc(self.sem, 1)
        self.eng.wait_ge(self.sem, self.k)


def wait(eng, sem, value):
    if not (isinstance(value, int) and value <= 0):
        eng.wait_ge(sem, value)


def after(eng, sem, u, back=0):
    wait(eng, sem, u + 1 - back)


def landed(eng, sems, slot, h, per, back=0):
    wait(eng, sems[slot], (h + 1 - back) * per)


def pipeline(eng, n, ring, stages, head=1):
    def at(u, k, s, lag):
        return u - lag, (s - lag) % ring, k + (s - lag) // ring

    for u in range(ring * head):
        for lag, f in stages:
            if u >= lag:
                f(*at(u, u // ring, u % ring, lag))
    with eng.Fori(head, n // ring - 1) as k:
        for s in range(ring):
            for lag, f in stages:
                f(*at(k * ring + s, k, s, lag))
    most = max(lag for lag, _ in stages)
    for u in range(n - ring, n + most):
        for lag, f in stages:
            if u - lag < n:
                f(*at(u, u // ring, u % ring, lag))


def cut_into_integers(dve, ch, out, a, n):
    ch.done(dve.tensor_scalar(out, a, 1.0 / n, -(n - 1) / (2.0 * n), ALU.mult, ALU.add))
    ch.done(dve.tensor_scalar(out, out, ROUND, -ROUND, ALU.add, ALU.add))


def slots_by_block(nc, e, tag, key, other):
    ET, NB, NPB = e.ET, e.NB, e.NPB
    OV = NB
    HI, LO = 32, 16
    CH = 4
    LK = 14
    with ExitStack() as c:
        def sb(name, shape, dt=F32):
            return c.enter_context(nc.sbuf_tensor(tag + name, shape, dt))

        def sem(name):
            return c.enter_context(nc.semaphore(tag + name))

        b = sb("b", [P, ET])
        val_hi = sb("val_hi", [P, ET])
        val_lo = sb("val_lo", [P, ET])
        rank = sb("rank", [P, ET])
        base = sb("base", [P, ET])
        bhl = sb("bhl", [P, 2, ET])
        t1 = sb("t1", [P, ET])
        t2 = sb("t2", [P, ET])
        ov16 = sb("ov16", [P, ET], F16)
        ovb16 = sb("ovb16", [P, ET], F16)

        with ExitStack() as c1:
            hot = c1.enter_context(nc.sbuf_tensor(tag + "hot", [P, ET, 64], F16))
            hotT = c1.enter_context(nc.sbuf_tensor(tag + "hotT", [P, ET // 2, P], F16))
            hist = c1.enter_context(nc.sbuf_tensor(tag + "hist", [HI, ET, LO], F32))
            seen = c1.enter_context(nc.sbuf_tensor(tag + "seen", [P, ET + 2, LO], F16))
            turned = c1.enter_context(nc.sbuf_tensor(tag + "turned", [P, 2, CH // 2, P], F16))
            near = c1.enter_context(nc.sbuf_tensor(tag + "near", [P, 2, CH, P], F16))
            prod = c1.enter_context(nc.sbuf_tensor(tag + "prod", [P, 2, LK, LO], F32))
            s_prep = sem("s_prep")
            s_seen0 = sem("s_seen_zeroed")
            with nc.Block() as block:
                @block.gpsimd
                def _(pool):
                    pool.memset(seen[:, :, :], 0.0).then_inc(s_seen0, 1)
                    pool.memset(hot[:, :, 48:64], 0.0).then_inc(s_seen0, 1)
                    pool.wait_ge(s_seen0, 2)

                @block.vector
                def _(dve):
                    ch = Chain(dve, s_prep)
                    q, r, lo, j = t1[:, :], t2[:, :], rank[:, :], base[:, :]
                    cut_into_integers(dve, ch, q, key, QUAD * NPB)
                    ch.done(dve.scalar_tensor_tensor(r, q, -float(QUAD * NPB), key, ALU.mult, ALU.add))
                    cut_into_integers(dve, ch, lo, r, QUAD)
                    ch.done(dve.scalar_tensor_tensor(j, lo, -float(QUAD), r, ALU.mult, ALU.add))
                    ch.done(dve.scalar_tensor_tensor(b[:, :], q, float(QUAD), j, ALU.mult, ALU.add))
                    ch.done(dve.tensor_scalar(q, b[:, :], float(NB), 1000.0, ALU.is_ge, ALU.mult))
                    ch.done(dve.tensor_tensor(b[:, :], b[:, :], q, ALU.add))
                    ch.done(dve.scalar_tensor_tensor(r, other, float(P), lo, ALU.mult, ALU.add))
                    ch.done(dve.tensor_scalar(r, r, 1.0, None, ALU.add))
                    ch.done(dve.tensor_scalar(val_hi[:, :], r, 1.0 / 4096, None, ALU.mult))
                    ch.done(dve.tensor_scalar(val_hi[:, :], val_hi[:, :], ROUND, -ROUND, ALU.add, ALU.add))
                    ch.done(dve.scalar_tensor_tensor(val_lo[:, :], val_hi[:, :], -4096.0, r, ALU.mult, ALU.add))
                    cut_into_integers(dve, ch, bhl[:, 0, :], b[:, :], LO)
                    ch.done(dve.scalar_tensor_tensor(bhl[:, 1, :], bhl[:, 0, :], -float(LO), b[:, :], ALU.mult, ALU.add))
                    ch.done(dve.tensor_tensor(hot[:, :, 0:HI], e.iota[:, 0:HI].unsqueeze(1).to_broadcast([P, ET, HI]),
                                              bhl[:, 0, :].unsqueeze(2).to_broadcast([P, ET, HI]), ALU.is_equal))
                    ch.done(dve.tensor_tensor(hot[:, :, HI:HI + LO], e.iota[:, 0:LO].unsqueeze(1).to_broadcast([P, ET, LO]),
                                              bhl[:, 1, :].unsqueeze(2).to_broadcast([P, ET, LO]), ALU.is_equal))

            with ExitStack() as c2:
                def bank(name, dt=F32):
                    return c2.enter_context(nc.psum_tensor(tag + name, [P, 2048 // (4 if dt == F32 else 2)], dt))

                pT = [bank(f"pT{i}", F16) for i in range(2)]
                pH = [bank(f"pH{i}") for i in range(2)]
                pS = [[bank(f"pS{i}{j}") for j in range(2)] for i in range(2)]
                s_T = sem("s_T")
                s_Tc = sem("s_T_copied")
                s_H = sem("s_hist")
                s_Hc = sem("s_hist_copied")
                s_same = sem("s_same")
                s_near = sem("s_near")
                s_kept = sem("s_kept")
                s_red = sem("s_reduced")
                s_carry = sem("s_carry")
                NC = ET // CH
                block = c2.enter_context(nc.Block())

                def chunks(eng, stages):
                    pipeline(eng, NC, 2, stages)

                @block.tensor
                def _(pe):
                    def turn(u, s, h):
                        after(pe, s_Tc, u, 2)
                        pe.sem_inc(s_carry, 1)
                        for k in range(CH // 2):
                            m = pe.transpose(pT[s][:, k * P:(k + 1) * P],
                                             hot[:, bass.ds(u * CH + 2 * k, 2), :].rearrange("p a b -> p (a b)"), e.ident16[:, :])
                        m.then_inc(s_T, 1)
                        after(pe, s_Hc, u, 2)
                        pe.sem_inc(s_carry, 1)
                        for k in range(CH):
                            row = hot[:, bass.ds(u * CH + k, 1), :].rearrange("p a b -> p (a b)")
                            m = pe.matmul(pH[s][0:HI, k * LO:(k + 1) * LO], row[:, 0:HI], row[:, HI:HI + LO], start=True, stop=True)
                        m.then_inc(s_H, 1)

                    def same(u, s, h):
                        after(pe, s_near, u, 2)
                        after(pe, s_Tc, u)
                        pe.sem_inc(s_carry, 1)
                        for half in range(2):
                            pe.matmul(pS[s][half][:, 0:CH // 2 * P], e.ident16[:, :],
                                      e.not_before[:, :].unsqueeze(1).to_broadcast([P, CH // 2, P]),
                                      start=True, stop=False, skip_group_check=True)
                        for k in range(CH):
                            half = 64 * (k % 2)
                            t = turned[half:half + 48, s, k // 2, :]
                            m = pe.matmul(pS[s][k % 2][:, k // 2 * P:(k // 2 + 1) * P], t, t, start=False, stop=True, skip_group_check=True)
                        m.then_inc(s_same, 1)
                    chunks(pe, [(0, turn), (1, same)])

                @block.scalar
                def _(act):
                    def near_(u, s, h):
                        after(act, s_same, u)
                        after(act, s_red, u, 2)
                        for half in range(2):
                            m = act.activation(near[:, s, half:CH:2, :], pS[s][half][:, 0:CH // 2 * P].rearrange("p (a b) -> p a b", b=P),
                                               ACT.Relu, bias=e.minus_one[:, 0:1])
                        m.then_inc(s_near, 1)

                    def keep(u, s, h):
                        after(act, s_Tc, u)
                        act.activation(hotT[:, bass.ds(u * (CH // 2), CH // 2), :], turned[:, s, :, :], ACT.Copy).then_inc(s_kept, 1)
                    chunks(act, [(0, keep), (1, near_)])

                @block.vector
                def _(dve):
                    def copies(u, s, h):
                        after(dve, s_T, u)
                        after(dve, s_same, u, 2)
                        after(dve, s_kept, u, 2)
                        dve.tensor_copy(turned[:, s, :, :],
                                        pT[s][:, 0:CH // 2 * P].rearrange("p (a b) -> p a b", b=P)).then_inc(s_Tc, 1)
                        after(dve, s_H, u)
                        dve.tensor_copy(hist[:, bass.ds(u * CH, CH), :],
                                        pH[s][0:HI, 0:CH * LO].rearrange("p (a b) -> p a b", b=LO)).then_inc(s_Hc, 1)

                    def reduce(u, s, h):
                        after(dve, s_near, u)
                        dve.tensor_reduce(rank[:, bass.ds(u * CH, CH)], near[:, s, :, :], AX, ALU.add).then_inc(s_red, 1)
                    chunks(dve, [(0, copies), (1, reduce)])

            s_scan = sem("s_scanned")
            s_twice = sem("s_seen_copied")
            with nc.Block() as block:
                @block.vector
                def _(dve):
                    for l in range(LO):
                        dve.tensor_tensor_scan(seen[0:HI, 1:ET + 1, l], e.ones[0:HI, 0:1].to_broadcast([HI, ET]), hist[:, :, l],
                                               0.0, ALU.mult, ALU.add).then_inc(s_scan, 1)
                    dve.wait_ge(s_twice, 16)
                    dve.tensor_scalar(seen[0:HI, 1:ET + 1:2, :], seen[0:HI, 1:ET + 1:2, :], 0.0, None, ALU.mult).then_inc(s_scan, 1)
                    dve.tensor_scalar(seen[64:64 + HI, 0:ET + 1:2, :], seen[64:64 + HI, 0:ET + 1:2, :], 0.0, None, ALU.mult).then_inc(s_scan, 1)
                    dve.wait_ge(s_scan, LO + 2)

                @block.sync
                def _(sp):
                    sp.wait_ge(s_scan, LO)
                    sp.dma_start(seen[64:64 + HI, 0:ET + 1, :], seen[0:HI, 0:ET + 1, :]).then_inc(s_twice, 16)
                    sp.wait_ge(s_twice, 16)

            with ExitStack() as c2:
                pL = [c2.enter_context(nc.psum_tensor(f"{tag}pL{i}", [P, 512], F32)) for i in range(2)]
                s_look = sem("s_looked_up")
                s_pick = sem("s_picked")
                s_base = sem("s_base")
                s_carry2 = sem("s_carry2")
                block = c2.enter_context(nc.Block())

                @block.tensor
                def _(pe):
                    def look(u, s, h):
                        after(pe, s_pick, u, 2)
                        pe.sem_inc(s_carry2, 1)
                        for k in range(0, LK, 2):
                            m = pe.matmul(pL[s][:, k * LO:(k + 2) * LO],
                                          hotT[:, bass.ds(u * (LK // 2) + k // 2, 1), :].rearrange("p a b -> p (a b)"),
                                          seen[:, bass.ds(u * LK + k, 2), :].rearrange("p a b -> p (a b)"),
                                          start=True, stop=True)
                        m.then_inc(s_look, 1)
                    pipeline(pe, ET // LK, 2, [(0, look)])

                @block.vector
                def _(dve):
                    def pick(u, s, h):
                        after(dve, s_look, u)
                        after(dve, s_base, u, 2)
                        dve.tensor_tensor(prod[:, s, :, :], pL[s][:, 0:LK * LO].rearrange("p (a b) -> p a b", b=LO),
                                          hot[:, bass.ds(u * LK, LK), HI:HI + LO], ALU.mult).then_inc(s_pick, 1)

                    def add(u, s, h):
                        after(dve, s_pick, u)
                        dve.tensor_reduce(base[:, bass.ds(u * LK, LK)], prod[:, s, :, :], AX, ALU.add).then_inc(s_base, 1)
                    pipeline(dve, ET // LK, 2, [(0, pick), (1, add)])

        with ExitStack() as c1:
            pA = c1.enter_context(nc.psum_tensor(tag + "pA", [P, 512], F32))
            pB = c1.enter_context(nc.psum_tensor(tag + "pB", [P, 512], F32))
            s_ov = sem("s_ov")
            s_pre = sem("s_pre")
            block = c1.enter_context(nc.Block())
            OV_FOUND = 4

            @block.tensor
            def _(pe):
                pe.wait_ge(s_ov, OV_FOUND)
                pe.matmul(pA[:, 0:ET], e.earlier16[:, :], ov16[:, :], start=True, stop=True)
                pe.matmul(pB[:, 0:ET], e.ones16[:, :], ov16[:, :], start=True, stop=True).then_inc(s_pre, 1)

            @block.vector
            def _(dve):
                ch = Chain(dve, s_ov)
                ch.done(dve.tensor_tensor(rank[:, :], rank[:, :], base[:, :], ALU.add))
                ch.done(dve.tensor_scalar(t1[:, :], rank[:, :], float(P), None, ALU.is_ge))
                ch.done(dve.scalar_tensor_tensor(t1[:, :], b[:, :], float(NB), t1[:, :], ALU.is_lt, ALU.mult))
                ch.done(dve.tensor_copy(ov16[:, :], t1[:, :]))
                assert ch.k == OV_FOUND
                ch.done(dve.tensor_tensor(ovb16[:, :], t1[:, :], b[:, :], ALU.mult))
                dve.wait_ge(s_pre, 1)
                ch.done(dve.tensor_tensor_scan(t2[:, :], e.ones[:, 0:1].to_broadcast([P, ET]), pB[:, 0:ET], 0.0, ALU.mult, ALU.add))
                ch.done(dve.tensor_copy(e.over[:, e.over_at:e.over_at + 1], t2[:, ET - 1:ET]))
                ch.done(dve.tensor_tensor(t2[:, :], t2[:, :], pB[:, 0:ET], ALU.subtract))
                ch.done(dve.tensor_tensor(t2[:, :], t2[:, :], pA[:, 0:ET], ALU.add))
                ch.done(dve.tensor_tensor(t2[:, :], t2[:, :], rank[:, :], ALU.subtract))
                ch.done(dve.tensor_tensor(t2[:, :], t2[:, :], t1[:, :], ALU.mult))
                ch.done(dve.tensor_tensor(rank[:, :], rank[:, :], t2[:, :], ALU.add))
                ch.done(dve.tensor_scalar(t2[:, :], b[:, :], -1.0, float(OV), ALU.mult, ALU.add))
                ch.done(dve.tensor_tensor(t2[:, :], t2[:, :], t1[:, :], ALU.mult))
                ch.done(dve.tensor_tensor(b[:, :], b[:, :], t2[:, :], ALU.add))

        with ExitStack() as c1:
            W = NB + 1
            hot_b = c1.enter_context(nc.sbuf_tensor(tag + "hot_b", [P, 2, CH, W + 1], F16))
            hot_s = c1.enter_context(nc.sbuf_tensor(tag + "hot_s", [P, 2, CH, 2, P], F16))
            low = c1.enter_context(nc.sbuf_tensor(tag + "low", [P, W + 1], F32))
            value = c1.enter_context(nc.sbuf_tensor(tag + "value", [P, W + 1], F32))
            pTab = [c1.enter_context(nc.psum_tensor(f"{tag}pTab{i}", [P, 512], F32)) for i in range(2)]
            pOv = [c1.enter_context(nc.psum_tensor(f"{tag}pOv{i}", [P, 512], F32)) for i in range(2)]
            s_hot = sem("s_hot")
            s_tab = sem("s_tab")
            s_low = sem("s_low")
            s_dec = sem("s_dec")
            s_carry3 = sem("s_carry3")
            NC = ET // CH
            block = c1.enter_context(nc.Block())

            @block.vector
            def _(dve):
                def hots(u, s, h):
                    after(dve, s_tab, u, 2)
                    for k in range(CH):
                        t = bass.ds(u * CH + k, 1)
                        dve.tensor_scalar(hot_b[:, s, k, 0:W + 1], e.iota16[:, 0:W + 1], b[:, t], None, ALU.is_equal)
                        dve.tensor_scalar(hot_s[:, s, k, 0, :], e.iota16[:, 0:P], rank[:, t], val_hi[:, t], ALU.is_equal, ALU.mult)
                        m = dve.tensor_scalar(hot_s[:, s, k, 1, :], e.iota16[:, 0:P], rank[:, t], val_lo[:, t], ALU.is_equal, ALU.mult)
                    m.then_inc(s_hot, 1)
                pipeline(dve, NC, 2, [(0, hots)])
                ch = Chain(dve, s_dec)
                dve.wait_ge(s_low, 2)
                ch.done(dve.scalar_tensor_tensor(value[:, 0:W], pTab[0][:, 0:W], 4096.0, low[:, 0:W], ALU.mult, ALU.add))
                ch.done(dve.scalar_tensor_tensor(value[:, W:W + 1], pOv[0][:, 0:1], 4096.0, low[:, W:W + 1], ALU.mult, ALU.add))
                cut_into_integers(dve, ch, e.oth[:, :], value[:, 0:W], P)
                ch.done(dve.scalar_tensor_tensor(e.lo[:, :], e.oth[:, :], -float(P), value[:, 0:W], ALU.mult, ALU.add))
                ch.done(dve.tensor_scalar(e.lo[:, :], e.lo[:, :], -1.0, None, ALU.add))
                q, j = low[:, 1:2], low[:, 2:3]
                ch.done(dve.tensor_scalar(q, value[:, OV:OV + 1], 1.0, None, ALU.max))
                ch.done(dve.reciprocal(q, q))
                ch.done(dve.tensor_tensor(q, q, value[:, W:W + 1], ALU.mult))
                ch.done(dve.tensor_scalar(e.ov_b[:, :], q, ROUND, -ROUND, ALU.add, ALU.add))
                cut_into_integers(dve, ch, q, e.ov_b[:, :], QUAD)
                ch.done(dve.scalar_tensor_tensor(j, q, -float(QUAD), e.ov_b[:, :], ALU.mult, ALU.add))
                ch.done(dve.scalar_tensor_tensor(j, q, float(QUAD * NPB), j, ALU.mult, ALU.add))
                ch.done(dve.scalar_tensor_tensor(e.ov_key[:, :], e.lo[:, OV:OV + 1], float(QUAD), j, ALU.mult, ALU.add))
                ch.done(dve.tensor_scalar(e.ov_row[:, :], e.quad_start[:, :], -1.0, e.ov_key[:, 0:1], ALU.mult, ALU.add))

            @block.tensor
            def _(pe):
                def table(u, s, h):
                    after(pe, s_hot, u)
                    pe.sem_inc(s_carry3, 1)
                    for k in range(CH):
                        first = isinstance(u, int) and u == 0 and k == 0
                        last = isinstance(u, int) and u == NC - 1 and k == CH - 1
                        for part in range(2):
                            pe.matmul(pTab[part][:, 0:W], hot_s[:, s, k, part, :], hot_b[:, s, k, 0:W], start=first, stop=last,
                                      skip_group_check=True)
                            m = pe.matmul(pOv[part][:, 0:1], hot_s[:, s, k, part, :], ovb16[:, bass.ds(u * CH + k, 1)],
                                          start=first, stop=last, skip_group_check=True)
                    m.then_inc(s_tab, 1)
                pipeline(pe, NC, 2, [(0, table)])

            @block.scalar
            def _(act):
                act.wait_ge(s_tab, NC)
                act.activation(low[:, 0:W], pTab[1][:, 0:W], ACT.Copy).then_inc(s_low, 1)
                act.activation(low[:, W:W + 1], pOv[1][:, 0:1], ACT.Copy).then_inc(s_low, 1)


def degrees(nc, e, by_dst):
    NB, NPB, NQ = e.NB, e.NPB, e.NQ
    with ExitStack() as c:
        def sb(name, shape, dt=F32):
            return c.enter_context(nc.sbuf_tensor("deg_" + name, shape, dt))

        def sem(name):
            return c.enter_context(nc.semaphore("deg_" + name))

        hot = sb("hot", [P, 2, QUAD, NPB], F16)
        ov_lo = sb("ov_lo", [P, NPB], F16)
        ov_b = sb("ov_b", [P, NB], F16)
        log = sb("log", [NPB, NB])
        rows = sb("rows", [NQ, QUAD * NPB])
        pD = c.enter_context(nc.psum_tensor("deg_pD", [P, 512], F32))
        pR = c.enter_context(nc.psum_tensor("deg_pR", [P, 512], F32))
        s_ov = sem("s_ov_hot")
        s_hot = sem("s_hot")
        s_cnt = sem("s_counted")
        s_log = sem("s_log")
        s_turn = sem("s_turned")
        s_rows = sem("s_rows")
        s_out = sem("s_out")
        s_carry = sem("s_carry")
        block = c.enter_context(nc.Block())

        @block.vector
        def _(dve):
            dve.tensor_scalar(ov_lo[:, :], e.iota16[:, 0:NPB], by_dst.lo[:, NB:NB + 1], None, ALU.is_equal).then_inc(s_ov, 1)
            dve.tensor_scalar(ov_b[:, :], e.iota16[:, 0:NB], by_dst.ov_b[:, 0:1], None, ALU.is_equal).then_inc(s_ov, 1)

            def hots(u, s, h):
                after(dve, s_cnt, u, 2)
                for j in range(QUAD):
                    m = dve.tensor_scalar(hot[:, s, j, :], e.iota16[:, 0:NPB], by_dst.lo[:, bass.ds(u * QUAD + j, 1)], None, ALU.is_equal)
                m.then_inc(s_hot, 1)
            pipeline(dve, NQ, 2, [(0, hots)])

        @block.tensor
        def _(pe):
            pe.wait_ge(s_ov, 2)
            pe.matmul(pD[0:NPB, 0:NB], ov_lo[:, :], ov_b[:, :], start=True, stop=False, skip_group_check=True)

            def count(u, s, h):
                after(pe, s_hot, u)
                pe.sem_inc(s_carry, 1)
                for j in range(QUAD):
                    m = pe.matmul(pD[0:NPB, bass.ds(u * QUAD + j, 1)], hot[:, s, j, :], e.ones16[:, 0:1], start=False, stop=True,
                                  skip_group_check=True)
                m.then_inc(s_cnt, 1)
            pipeline(pe, NQ, 2, [(0, count)])
            pe.wait_ge(s_log, 2)
            for j in range(QUAD):
                m = pe.transpose(pR[0:NQ, j * NPB:(j + 1) * NPB], e.dinv_b[:, j * NQ:(j + 1) * NQ], e.ident[0:NPB, 0:NPB])
            m.then_inc(s_turn, 1)

        @block.scalar
        def _(act):
            act.wait_ge(s_cnt, NQ)
            act.activation(log[:, :], pD[0:NPB, 0:NB], ACT.Ln, bias=e.ones[0:NPB, 0:1]).then_inc(s_log, 1)
            act.wait_ge(s_log, 1)
            act.activation(e.dinv_b[:, :], log[:, :], ACT.Exp, scale=-0.5).then_inc(s_log, 1)
            act.wait_ge(s_turn, 1)
            act.activation(rows[:, :], pR[0:NQ, 0:QUAD * NPB], ACT.Copy).then_inc(s_rows, 1)
            act.wait_ge(s_rows, 1)
            act.dma_start(e.dinv_rows.rearrange("(j b) p -> b j p", j=QUAD), rows[:, :].rearrange("b (j p) -> b j p", j=QUAD)).then_inc(s_out, 16)
            act.wait_ge(s_out, 16)


def attention(nc, e, by_src):
    N, D, H, DH, A, R1 = e.N, e.D, e.H, e.DH, e.A, e.R1
    NB, NPB, NQ = e.NB, e.NPB, e.NQ
    QN = QUAD * NPB
    LASTP = (N - (NQ - 1) * QN) // QUAD
    with ExitStack() as c:
        def sb(name, shape, dt=F32):
            return c.enter_context(nc.sbuf_tensor("a_" + name, shape, dt))

        def sem(name):
            h = c.enter_context(nc.semaphore("a_" + name))
            e.spare.append(h.num)
            return h

        bank = [c.enter_context(nc.psum_tensor(f"a_bank{i}", [P, 512], F32)) for i in range(7)]
        pHot, pDst, pSrc, pQ, pK, pV, pAcc = bank
        ov_con = sb("ov_con", [P, A])

        with ExitStack() as c1:
            idx = c1.enter_context(nc.sbuf_tensor("ao_idx", [P, 2], I32))
            rows = c1.enter_context(nc.sbuf_tensor("ao_rows", [P, 2, D], F32))
            rowsT = c1.enter_context(nc.sbuf_tensor("ao_rowsT", [D, 2, P], F32))
            q_sb = c1.enter_context(nc.sbuf_tensor("ao_q", [P, D], F32))
            prod = c1.enter_context(nc.sbuf_tensor("ao_prod", [P, D], F32))
            score = c1.enter_context(nc.sbuf_tensor("ao_score", [P, H], F32))
            so_dve = sem("so_dve")
            so_rows = sem("so_rows")
            so_T = sem("so_T")
            so_Tc = sem("so_Tc")
            so_qkv = sem("so_qkv")
            so_q = sem("so_q")
            so_e = sem("so_e")
            block = c1.enter_context(nc.Block())

            @block.vector
            def _(dve):
                with dve.If(e.fast(dve)):
                    ch = Chain(dve, so_dve)
                    ch.done(dve.tensor_scalar(idx[:, 0:1], by_src.ov_key[:, :], 0.0, None, ALU.max))
                    ch.done(dve.tensor_copy(idx[:, 1:2], by_src.oth[:, NB:NB + 1]))
                    dve.wait_ge(so_q, 1)
                    dve.wait_ge(so_qkv, 1)
                    ch.done(dve.tensor_tensor(prod[:, :], q_sb[:, :], pK[:, 0:D], ALU.mult))
                    ch.done(dve.tensor_reduce(score[:, :], prod[:, :].rearrange("p (h d) -> p h d", h=H), AX, ALU.add))
                    ch.done(dve.tensor_scalar(score[:, :], score[:, :], LIMIT, -LIMIT, ALU.min, ALU.max))
                    dve.wait_ge(so_e, 1)
                    ch.done(dve.tensor_tensor(ov_con[:, 0:D].rearrange("p (h d) -> p h d", h=H),
                                              pV[:, 0:D].rearrange("p (h d) -> p h d", h=H),
                                              ov_con[:, D:A].unsqueeze(2).to_broadcast([P, H, DH]), ALU.mult))

            @block.gpsimd
            def _(pool):
                with pool.If(e.fast(pool)):
                    pool.wait_ge(so_dve, 2)
                    for k in range(2):
                        pool.indirect_dma_start(rows[:, k, :], None, e.x[:, :],
                                                bass.IndirectOffsetOnAxis(ap=idx[:, k:k + 1], axis=0)).then_inc(so_rows, 16)
                    pool.wait_ge(so_rows, 32)

            @block.tensor
            def _(pe):
                with pe.If(e.fast(pe)):
                    pe.wait_ge(so_rows, 32)
                    pe.transpose(pHot[0:D, 0:P], rows[:, 0, :], e.ident[:, :])
                    pe.transpose(pHot[0:D, P:2 * P], rows[:, 1, :], e.ident[:, :]).then_inc(so_T, 1)
                    pe.wait_ge(so_Tc, 1)
                    pe.matmul(pQ[:, 0:D], rowsT[:, 0, :], e.q_w[:, :], start=True, stop=True)
                    pe.matmul(pK[:, 0:D], rowsT[:, 1, :], e.kv_w[:, 0:D], start=True, stop=True)
                    pe.matmul(pV[:, 0:D], rowsT[:, 1, :], e.kv_w[:, D:2 * D], start=True, stop=True).then_inc(so_qkv, 1)

            @block.scalar
            def _(act):
                with act.If(e.fast(act)):
                    act.preload_act_table_set(ACT_SET)
                    act.wait_ge(so_T, 1)
                    act.activation(rowsT[:, :, :], pHot[0:D, 0:2 * P].rearrange("p (a b) -> p a b", a=2), ACT.Copy).then_inc(so_Tc, 1)
                    act.wait_ge(so_qkv, 1)
                    act.activation(q_sb[:, :], pQ[:, 0:D], ACT.Copy).then_inc(so_q, 1)
                    act.wait_ge(so_dve, 5)
                    act.activation(ov_con[:, D:A], score[:, :], ACT.Exp).then_inc(so_e, 1)

        RING = 4
        idx = [sb(f"idx{i}", [P, QUAD], I32) for i in range(RING)]
        dst_rows = [sb(f"dst_rows{i}", [P, QUAD, D]) for i in range(RING)]
        own = [sb(f"own{i}", [NPB, QUAD, D]) for i in range(RING)]
        hot = [sb(f"hot{i}", [P, QUAD, NPB]) for i in range(RING)]
        hot_ov = [sb(f"hot_ov{i}", [P, QUAD, NPB]) for i in range(RING)]
        hotT = sb("hotT", [NPB, QUAD, P])
        dstT = sb("dstT", [D, QUAD, P])
        srcT = sb("srcT", [D, QUAD, P])
        q_sb = sb("q_sb", [P, QUAD, D])
        prod = sb("prod", [P, QUAD, D])
        score = sb("score", [P, QUAD * H])
        con = [sb(f"con{i}", [P, QUAD, A]) for i in range(2)]
        rec = sb("rec", [NPB, QUAD, H])
        hid = [sb(f"hid{i}", [NPB, QUAD, D]) for i in range(2)]
        stats = sb("stats", [NPB, QUAD, 6])
        mv = [sb(f"mv{i}", [NPB, QUAD, 2]) for i in range(2)]
        lnv = sb("lnv", [NPB, QUAD])
        rstd = [sb(f"rstd{i}", [NPB, QUAD]) for i in range(2)]
        x1r = [sb(f"x1r{i}", [NPB, QUAD, R1]) for i in range(RING)]

        d_rows = [sem(f"d_rows{i}") for i in range(RING)]
        d_own = [sem(f"d_own{i}") for i in range(RING)]
        d_out = [sem(f"d_out{i}") for i in range(RING)]
        (s_idx, s_hot, s_hov, s_hotT, s_dstT, s_hotTc, s_dstTc, s_srcT, s_srcTc, s_q, s_qc, s_kv, s_prod, s_sc, s_clip, s_exp,
         s_con, s_acc, s_den, s_rec, s_num, s_hid, s_st, s_mv, s_lnv, s_rstd, s_x1, s_dcol, s_carry, s_const) = [
            sem("s_" + n) for n in ("idx hot hov hotT dstT hotTc dstTc srcT srcTc q qc kv prod sc clip exp con acc den rec num "
                                    "hid st mv lnv rstd x1 dcol carry const").split()]
        block = c.enter_context(nc.Block())

        def rows_of(t, u, n):
            return t[bass.ds(u * QN, QUAD * n), :].rearrange("(p j) d -> p j d", j=QUAD)

        def parts(u):
            return LASTP if isinstance(u, int) and u == NQ - 1 else NPB

        @block.sync
        def _(sp):
            def load(u, s, h):
                after(sp, s_hid, u, RING)
                n = parts(u)
                sp.dma_start(own[s][0:n, :, :], rows_of(e.x, u, n)).then_inc(d_own[s], 16)

            def store(u, s, h):
                after(sp, s_x1, u)
                after(sp, s_dcol, u)
                n = parts(u)
                sp.dma_start(rows_of(e.x1_rows, u, n), x1r[s][0:n, :, :]).then_inc(d_out[s], 16)
            with sp.If(e.fast(sp)):
                sp.wait_ge(s_const, 3 * RING)
                pipeline(sp, NQ, RING, [(0, load), (4, store)])
                for s in range(RING):
                    sp.wait_ge(d_out[s], 16 * (NQ // RING))

        @block.gpsimd
        def _(pool):
            def gather(u, s, h):
                after(pool, s_dstT, u, RING)
                after(pool, s_idx, u)
                pool.sem_inc(s_carry, 1)
                for j in range(QUAD):
                    pool.indirect_dma_start(dst_rows[s][:, j, :], None, e.x[:, :],
                                            bass.IndirectOffsetOnAxis(ap=idx[s][:, j:j + 1], axis=0)).then_inc(d_rows[s], 16)
            with pool.If(e.fast(pool)):
                pipeline(pool, NQ, RING, [(0, gather)], 2)

        @block.scalar
        def _(act):
            def index(u, s, h):
                landed(act, d_rows, s, h, 16 * QUAD, 1)
                act.activation(idx[s][:, :], by_src.oth[:, bass.ds(u * QUAD, QUAD)], ACT.Copy).then_inc(s_idx, 1)

            def turned(u, s, h):
                after(act, s_hotT, u)
                after(act, s_srcT, u, 1)
                act.activation(hotT[:, :, :], pHot[0:NPB, :].rearrange("p (a b) -> p a b", a=QUAD), ACT.Copy).then_inc(s_hotTc, 1)

            def exps(u, s, h):
                after(act, s_clip, u)
                after(act, s_acc, u, 2)
                act.activation(con[s % 2][:, :, D:A], score[:, :].rearrange("p (j h) -> p j h", j=QUAD), ACT.Exp).then_inc(s_exp, 1)

            def turned2(u, s, h):
                after(act, s_dstT, u)
                after(act, s_kv, u, 1)
                act.activation(dstT[:, :, :], pDst[0:D, :].rearrange("p (a b) -> p a b", a=QUAD), ACT.Copy).then_inc(s_dstTc, 1)

            def turned3(u, s, h):
                after(act, s_srcT, u)
                after(act, s_q, u, 1)
                act.activation(srcT[:, :, :], pSrc[0:D, :].rearrange("p (a b) -> p a b", a=QUAD), ACT.Copy).then_inc(s_srcTc, 1)

            def queries(u, s, h):
                after(act, s_q, u)
                after(act, s_prod, u, 1)
                act.activation(q_sb[:, :, :], pQ[:, 0:QUAD * D].rearrange("p (a b) -> p a b", a=QUAD), ACT.Copy).then_inc(s_qc, 1)

            def rstd_(u, s, h):
                after(act, s_mv, u)
                after(act, s_rstd, u, 1)
                act.activation(lnv[:, :], mv[s % 2][:, :, 1], ACT.Ln, bias=e.eps[0:NPB, 0:1]).then_inc(s_lnv, 1)
                landed(act, d_out, s, h, 16, 1)
                act.activation(x1r[s][:, :, D], e.dinv_b[:, bass.ds(u * QUAD, QUAD)], ACT.Copy).then_inc(s_dcol, 1)
                after(act, s_lnv, u)
                after(act, s_x1, u, 2)
                act.activation(rstd[s % 2][:, :], lnv[:, :], ACT.Exp, scale=-0.5).then_inc(s_rstd, 1)
            with act.If(e.fast(act)):
                act.wait_ge(s_const, 3 * RING)
                act.preload_act_table_set(ACT_SET)
                pipeline(act, NQ, RING, [(0, index), (1, turned), (2, exps), (1, turned2), (4, rstd_), (1, turned3), (1, queries)], 2)

        @block.vector
        def _(dve):
            def select(u, s, h):
                after(dve, s_acc, u, RING)
                dve.tensor_tensor(hot[s][:, :, :], e.iota[:, 0:NPB].unsqueeze(1).to_broadcast([P, QUAD, NPB]),
                                  by_src.lo[:, bass.ds(u * QUAD, QUAD)].unsqueeze(2).to_broadcast([P, QUAD, NPB]), ALU.is_equal).then_inc(s_hot, 1)
                dve.tensor_scalar(hot_ov[s][:, :, :], e.quad_rows[:, :, :], by_src.ov_row[:, bass.ds(u, 1)], None,
                                  ALU.is_equal).then_inc(s_hov, 1)

            def product(u, s, h):
                after(dve, s_qc, u)
                after(dve, s_kv, u)
                after(dve, s_sc, u, 1)
                dve.tensor_tensor(prod[:, :, :], q_sb[:, :, :], pK[:, 0:QUAD * D].rearrange("p (j d) -> p j d", j=QUAD), ALU.mult).then_inc(s_prod, 1)

            def sums(u, s, h):
                after(dve, s_acc, u)
                after(dve, s_num, u, 1)
                acc = pAcc[0:NPB, 0:QUAD * A].rearrange("p (j a) -> p j a", j=QUAD)
                dve.tensor_scalar(rec[:, :, :], acc[:, :, D:A], EPS_NORM, None, ALU.add).then_inc(s_den, 1)

            def score_(u, s, h):
                after(dve, s_prod, u)
                after(dve, s_exp, u, 1)
                dve.tensor_reduce(score[:, :], prod[:, :, :].rearrange("p j (h d) -> p (j h) d", h=H), AX, ALU.add).then_inc(s_sc, 1)

            def recip(u, s, h):
                after(dve, s_den, u)
                dve.reciprocal(rec[:, :, :], rec[:, :, :]).then_inc(s_rec, 1)

            def clip(u, s, h):
                after(dve, s_sc, u)
                dve.tensor_scalar(score[:, :], score[:, :], LIMIT, -LIMIT, ALU.min, ALU.max).then_inc(s_clip, 1)

            def norms(u, s, h):
                after(dve, s_rec, u)
                after(dve, s_x1, u, 2)
                acc = pAcc[0:NPB, 0:QUAD * A].rearrange("p (j a) -> p j a", j=QUAD)
                dve.tensor_tensor(hid[s % 2][:, :, :].rearrange("p j (h d) -> p j h d", h=H),
                                  acc[:, :, 0:D].rearrange("p j (h d) -> p j h d", h=H),
                                  rec[:, :, :].unsqueeze(3).to_broadcast([NPB, QUAD, H, DH]), ALU.mult).then_inc(s_num, 1)

            def contribute(u, s, h):
                after(dve, s_exp, u)
                dve.tensor_tensor(con[s % 2][:, :, 0:D].rearrange("p j (h d) -> p j h d", h=H),
                                  pV[:, 0:QUAD * D].rearrange("p (j h d) -> p j h d", j=QUAD, h=H),
                                  con[s % 2][:, :, D:A].unsqueeze(3).to_broadcast([P, QUAD, H, DH]), ALU.mult).then_inc(s_con, 1)

            def hidden(u, s, h):
                after(dve, s_num, u)
                landed(dve, d_own, s, h, 16)
                dve.scalar_tensor_tensor(hid[s % 2][:, :, :], own[s][:, :, :], 2.0, hid[s % 2][:, :, :], ALU.mult, ALU.add).then_inc(s_hid, 1)

            def norm(u, s, h):
                after(dve, s_rstd, u)
                landed(dve, d_out, s, h, 16, 1)
                for j in range(QUAD):
                    m = dve.tensor_scalar(x1r[s][:, j, 0:D], hid[s % 2][:, j, :], mv[s % 2][:, j, 0:1], rstd[s % 2][:, j:j + 1],
                                          ALU.subtract, ALU.mult)
                m.then_inc(s_x1, 1)

            def stat(u, s, h):
                after(dve, s_hid, u)
                after(dve, s_mv, u, 1)
                for j in range(QUAD):
                    m = dve.bn_stats(stats[:, j, :], hid[s % 2][:, j, :])
                m.then_inc(s_st, 1)
                after(dve, s_st, u)
                after(dve, s_rstd, u, 2)
                dve.sem_inc(s_carry, 1)
                for j in range(QUAD):
                    m = dve.bn_aggr(mv[s % 2][:, j, :], stats[:, j, :])
                m.then_inc(s_mv, 1)
            with dve.If(e.fast(dve)):
                for s in range(RING):
                    dve.memset(own[s][:, :, :], 0.0).then_inc(s_const, 1)
                    dve.memset(x1r[s][:, :, D + 1:D + 3], 1.0).then_inc(s_const, 1)
                    dve.memset(x1r[s][:, :, D + 3:R1], 0.0).then_inc(s_const, 1)
                pipeline(dve, NQ, RING, [(0, select), (2, product), (3, sums), (2, score_), (3, recip), (2, clip), (3, norms),
                                         (2, contribute), (3, hidden), (4, norm), (3, stat)], 2)

        @block.tensor
        def _(pe):
            def turn(u, s, h):
                after(pe, s_hot, u)
                after(pe, s_hotTc, u, 1)
                pe.sem_inc(s_carry, 1)
                for j in range(QUAD):
                    m = pe.transpose(pHot[0:NPB, j * P:(j + 1) * P], hot[s][:, j, :], e.ident[:, :])
                m.then_inc(s_hotT, 1)
                landed(pe, d_rows, s, h, 16 * QUAD)
                after(pe, s_dstTc, u, 1)
                pe.sem_inc(s_carry, 1)
                for j in range(QUAD):
                    m = pe.transpose(pDst[0:D, j * P:(j + 1) * P], dst_rows[s][:, j, :], e.ident[:, :])
                m.then_inc(s_dstT, 1)

            def source(u, s, h):
                after(pe, s_hotTc, u)
                after(pe, s_srcTc, u, 1)
                landed(pe, d_own, s, h, 16)
                pe.sem_inc(s_carry, 1)
                for j in range(QUAD):
                    m = pe.matmul(pSrc[0:D, j * P:(j + 1) * P], own[s][:, j, :], hotT[:, j, :], start=True, stop=True)
                m.then_inc(s_srcT, 1)

            def keys(u, s, h):
                after(pe, s_dstTc, u)
                after(pe, s_con, u, 1)
                pe.sem_inc(s_carry, 1)
                for j in range(QUAD):
                    pe.matmul(pK[:, j * D:(j + 1) * D], dstT[:, j, :], e.kv_w[:, 0:D], start=True, stop=True)
                    m = pe.matmul(pV[:, j * D:(j + 1) * D], dstT[:, j, :], e.kv_w[:, D:2 * D], start=True, stop=True)
                m.then_inc(s_kv, 1)

            def query(u, s, h):
                after(pe, s_srcTc, u)
                after(pe, s_qc, u, 1)
                pe.sem_inc(s_carry, 1)
                for j in range(QUAD):
                    m = pe.matmul(pQ[:, j * D:(j + 1) * D], srcT[:, j, :], e.q_w[:, :], start=True, stop=True)
                m.then_inc(s_q, 1)

            def gather_sums(u, s, h):
                after(pe, s_con, u)
                after(pe, s_hov, u)
                after(pe, s_num, u, 1)
                pe.sem_inc(s_carry, 1)
                for j in range(QUAD):
                    pe.matmul(pAcc[0:NPB, j * A:(j + 1) * A], hot_ov[s][:, j, :], ov_con[:, :], start=True, stop=False)
                    m = pe.matmul(pAcc[0:NPB, j * A:(j + 1) * A], hot[s][:, j, :], con[s % 2][:, j, :], start=False, stop=True)
                m.then_inc(s_acc, 1)
            with pe.If(e.fast(pe)):
                pe.wait_ge(s_const, 3 * RING)
                pipeline(pe, NQ, RING, [(1, turn), (1, source), (2, gather_sums), (1, keys), (1, query)], 2)


def convolution(nc, e, by_dst):
    N, D, R1 = e.N, e.D, e.R1
    NB, NPB, NQ = e.NB, e.NPB, e.NQ
    QN = QUAD * NPB
    LASTP = (N - (NQ - 1) * QN) // QUAD
    with ExitStack() as c:
        def sb(name, shape, dt=F32):
            return c.enter_context(nc.sbuf_tensor("c_" + name, shape, dt))

        def sem(name):
            h = c.enter_context(nc.semaphore("c_" + name))
            e.spare.append(h.num)
            return h

        bank = [c.enter_context(nc.psum_tensor(f"c_bank{i}", [P, 512], F32)) for i in range(5)]
        pOwn, pSum, pY = bank[0], bank[1:3], bank[3:5]
        RING = 4
        ov_idx = sb("ov_idx", [P, 1], I32)
        ov_rows = sb("ov_rows", [P, R1])
        idx = [sb(f"idx{i}", [P, QUAD], I32) for i in range(RING)]
        rows = [sb(f"rows{i}", [P, QUAD, R1]) for i in range(RING)]
        own = [sb(f"own{i}", [NPB, QUAD, R1]) for i in range(RING)]
        dinvr = [sb(f"dinvr{i}", [D, QN]) for i in range(RING)]
        hot = [sb(f"hot{i}", [P, QUAD, NPB]) for i in range(2)]
        hot_ov = [sb(f"hot_ov{i}", [P, QUAD, NPB]) for i in range(2)]
        own_s = [sb(f"own_s{i}", [NPB, QUAD, D]) for i in range(2)]
        ownT = [sb(f"ownT{i}", [R1, QN]) for i in range(2)]
        sumT = sb("sumT", [D, QN])
        cap = sb("cap", [NPB, QUAD * D])
        u_ = [sb(f"u{i}", [NPB, QUAD * D]) for i in range(2)]
        n_ = sb("n", [NPB, QUAD * D])
        r_ = sb("r", [NPB, QUAD * D])
        lg = sb("lg", [NPB, QUAD * D])
        hid = [sb(f"hid{i}", [NPB, QUAD, D]) for i in range(2)]
        stats = sb("stats", [NPB, QUAD, 6])
        mv = [sb(f"mv{i}", [NPB, QUAD, 2]) for i in range(2)]
        lnv = sb("lnv", [NPB, QUAD])
        rstd = [sb(f"rstd{i}", [NPB, QUAD]) for i in range(2)]
        res = [sb(f"res{i}", [NPB, QUAD, D]) for i in range(RING)]

        d_ov = sem("d_ov")
        d_rows = [sem(f"d_rows{i}") for i in range(RING)]
        d_own = [sem(f"d_own{i}") for i in range(RING)]
        d_out = [sem(f"d_out{i}") for i in range(RING)]
        (s_ovi, s_idx, s_hot, s_hov, s_own_s, s_ownT, s_ownTc, s_sum, s_sumc, s_y, s_cap, s_u, s_n, s_lg, s_r, s_t, s_ty, s_hid,
         s_st, s_mv, s_lnv, s_rstd, s_res, s_carry, s_const) = [
            sem("s_" + n) for n in ("ovi idx hot hov own_s ownT ownTc sum sumc y cap u n lg r t ty hid st mv lnv rstd res carry "
                                    "const").split()]
        block = c.enter_context(nc.Block())

        def rows_of(t, u, n):
            return t[bass.ds(u * QN, QUAD * n), :].rearrange("(p j) d -> p j d", j=QUAD)

        def parts(u):
            return LASTP if isinstance(u, int) and u == NQ - 1 else NPB

        @block.sync
        def _(sp):
            def load(u, s, h):
                after(sp, s_hid, u, RING)
                n = parts(u)
                sp.dma_start(own[s][0:n, :, :], rows_of(e.x1_rows, u, n)).then_inc(d_own[s], 16)
                sp.dma_start(dinvr[s][:, :], e.dinv_rows.rearrange("(q j) p -> q (j p)", j=QUAD)[bass.ds(u, 1), :].to_broadcast([D, QN]))\
                  .then_inc(d_own[s], 16)

            def store(u, s, h):
                after(sp, s_res, u)
                n = parts(u)
                sp.dma_start(rows_of(e.out, u, n), res[s][0:n, :, :]).then_inc(d_out[s], 16)
            with sp.If(e.fast(sp)):
                sp.wait_ge(s_const, RING)
                pipeline(sp, NQ, RING, [(0, load), (4, store)])
                for s in range(RING):
                    sp.wait_ge(d_out[s], 16 * (NQ // RING))

        @block.gpsimd
        def _(pool):
            def gather(u, s, h):
                after(pool, s_sum, u, RING)
                after(pool, s_idx, u)
                pool.sem_inc(s_carry, 1)
                for j in range(QUAD):
                    pool.indirect_dma_start(rows[s][:, j, :], None, e.x1_rows[:, :],
                                            bass.IndirectOffsetOnAxis(ap=idx[s][:, j:j + 1], axis=0)).then_inc(d_rows[s], 16)
            with pool.If(e.fast(pool)):
                pool.wait_ge(s_ovi, 1)
                pool.indirect_dma_start(ov_rows[:, :], None, e.x1_rows[:, :],
                                        bass.IndirectOffsetOnAxis(ap=ov_idx[:, 0:1], axis=0)).then_inc(d_ov, 16)
                pipeline(pool, NQ, RING, [(0, gather)], 2)

        @block.scalar
        def _(act):
            def index(u, s, h):
                landed(act, d_rows, s, h, 16 * QUAD, 1)
                act.activation(idx[s][:, :], by_dst.oth[:, bass.ds(u * QUAD, QUAD)], ACT.Copy).then_inc(s_idx, 1)

            def logs(u, s, h):
                after(act, s_n, u)
                after(act, s_r, u, 1)
                act.activation(lg[:, :], n_[:, :], ACT.Ln, bias=e.two[0:NPB, 0:1]).then_inc(s_lg, 1)

            def scale_own(u, s, h):
                landed(act, d_own, s, h, 32)
                after(act, s_sum, u, 2)
                for j in range(QUAD):
                    m = act.activation(own_s[s % 2][:, j, :], own[s][:, j, 0:D], ACT.Copy, scale=own[s][:, j, D:D + 1])
                m.then_inc(s_own_s, 1)

            def recips(u, s, h):
                after(act, s_lg, u)
                after(act, s_t, u, 1)
                act.activation(r_[:, :], lg[:, :], ACT.Exp, scale=-1.0).then_inc(s_r, 1)

            def turned(u, s, h):
                after(act, s_ownT, u)
                after(act, s_y, u, 2)
                act.activation(ownT[s % 2][:, :], pOwn[0:R1, 0:QN], ACT.Copy).then_inc(s_ownTc, 1)

            def capped(u, s, h):
                after(act, s_y, u)
                after(act, s_u, u, 1)
                act.activation(cap[:, :], pY[s % 2][0:NPB, 0:QUAD * D], ACT.Relu, bias=e.twenty[0:NPB, 0:1], scale=-1.0).then_inc(s_cap, 1)
                after(act, s_cap, u)
                after(act, s_n, u, 2)
                act.activation(u_[s % 2][:, :], cap[:, :], ACT.Exp, bias=e.twenty[0:NPB, 0:1], scale=-1.0).then_inc(s_u, 1)

            def rstd_(u, s, h):
                after(act, s_mv, u)
                after(act, s_rstd, u, 1)
                act.activation(lnv[:, :], mv[s % 2][:, :, 1], ACT.Ln, bias=e.eps[0:NPB, 0:1]).then_inc(s_lnv, 1)
                after(act, s_lnv, u)
                after(act, s_res, u, 2)
                act.activation(rstd[s % 2][:, :], lnv[:, :], ACT.Exp, scale=-0.5).then_inc(s_rstd, 1)
            with act.If(e.fast(act)):
                act.wait_ge(s_const, RING)
                act.preload_act_table_set(ACT_SET)
                pipeline(act, NQ, RING, [(0, index), (3, logs), (1, scale_own), (3, recips), (1, turned), (4, rstd_), (2, capped)], 2)

        @block.vector
        def _(dve):
            def poly(u, s, h):
                after(dve, s_u, u)
                after(dve, s_t, u, 1)
                dve.scalar_tensor_tensor(n_[:, :], u_[s % 2][:, :], 2.0, u_[s % 2][:, :], ALU.add, ALU.mult).then_inc(s_n, 1)

            def select(u, s, h):
                landed(dve, d_rows, s, h, 16 * QUAD)
                after(dve, s_sum, u, 2)
                for j in range(QUAD):
                    m = dve.tensor_scalar(hot[s % 2][:, j, :], e.iota[:, 0:NPB], by_dst.lo[:, bass.ds(u * QUAD + j, 1)],
                                          rows[s][:, j, D:D + 1], ALU.is_equal, ALU.mult)
                m.then_inc(s_hot, 1)
                dve.tensor_scalar(hot_ov[s % 2][:, :, :], e.quad_rows[:, :, :], by_dst.ov_row[:, bass.ds(u, 1)], ov_rows[:, D:D + 1],
                                  ALU.is_equal, ALU.mult).then_inc(s_hov, 1)

            def scaled(u, s, h):
                after(dve, s_sum, u)
                after(dve, s_y, u, 1)
                dve.tensor_tensor(sumT[:, :], pSum[s % 2][0:D, 0:QN], dinvr[s][:, :], ALU.mult).then_inc(s_sumc, 1)

            def ratio(u, s, h):
                after(dve, s_r, u)
                after(dve, s_ty, u, 1)
                dve.tensor_tensor(n_[:, :], n_[:, :], r_[:, :], ALU.mult).then_inc(s_t, 1)

            def mish(u, s, h):
                after(dve, s_t, u)
                after(dve, s_res, u, 2)
                dve.tensor_tensor(hid[s % 2][:, :, :].rearrange("p j d -> p (j d)"), n_[:, :], pY[s % 2][0:NPB, 0:QUAD * D], ALU.mult)\
                   .then_inc(s_ty, 1)

            def hidden(u, s, h):
                after(dve, s_ty, u)
                dve.tensor_tensor(hid[s % 2][:, :, :], hid[s % 2][:, :, :], own[s][:, :, 0:D], ALU.add).then_inc(s_hid, 1)

            def norm(u, s, h):
                after(dve, s_rstd, u)
                landed(dve, d_out, s, h, 16, 1)
                for j in range(QUAD):
                    m = dve.tensor_scalar(res[s][:, j, :], hid[s % 2][:, j, :], mv[s % 2][:, j, 0:1], rstd[s % 2][:, j:j + 1],
                                          ALU.subtract, ALU.mult)
                m.then_inc(s_res, 1)

            def stat(u, s, h):
                after(dve, s_hid, u)
                after(dve, s_mv, u, 1)
                for j in range(QUAD):
                    m = dve.bn_stats(stats[:, j, :], hid[s % 2][:, j, :])
                m.then_inc(s_st, 1)
                after(dve, s_st, u)
                after(dve, s_rstd, u, 2)
                dve.sem_inc(s_carry, 1)
                for j in range(QUAD):
                    m = dve.bn_aggr(mv[s % 2][:, j, :], stats[:, j, :])
                m.then_inc(s_mv, 1)
            with dve.If(e.fast(dve)):
                for s in range(RING):
                    dve.memset(own[s][:, :, :], 0.0).then_inc(s_const, 1)
                dve.tensor_copy(ov_idx[:, :], by_dst.oth[:, NB:NB + 1]).then_inc(s_ovi, 1)
                dve.wait_ge(d_ov, 16)
                pipeline(dve, NQ, RING, [(3, poly), (1, select), (2, scaled), (3, ratio), (4, norm), (3, mish), (3, hidden), (3, stat)], 2)

        @block.tensor
        def _(pe):
            def turn(u, s, h):
                landed(pe, d_own, s, h, 32)
                after(pe, s_ownTc, u, 1)
                pe.sem_inc(s_carry, 1)
                for j in range(QUAD):
                    m = pe.transpose(pOwn[0:R1, j * NPB:(j + 1) * NPB], own[s][:, j, :], e.ident[0:NPB, 0:NPB])
                m.then_inc(s_ownT, 1)

            def sums(u, s, h):
                after(pe, s_hov, u)
                after(pe, s_sumc, u, 2)
                after(pe, s_own_s, u)
                landed(pe, d_rows, s, h, 16 * QUAD)
                pe.sem_inc(s_carry, 1)
                pe.matmul(pSum[s % 2][0:D, 0:QN], ov_rows[:, 0:D], hot_ov[s % 2][:, :, :], start=True, stop=False, skip_group_check=True)
                for j in range(QUAD):
                    at = slice(j * NPB, (j + 1) * NPB)
                    pe.matmul(pSum[s % 2][0:D, at], rows[s][:, j, 0:D], hot[s % 2][:, j, :], start=False, stop=False, skip_group_check=True)
                    m = pe.matmul(pSum[s % 2][0:D, at], own_s[s % 2][:, j, :], e.ident[0:NPB, 0:NPB], start=False, stop=True,
                                  skip_group_check=True)
                m.then_inc(s_sum, 1)

            def linear(u, s, h):
                after(pe, s_sumc, u)
                after(pe, s_ownTc, u)
                after(pe, s_ty, u, 2)
                pe.sem_inc(s_carry, 1)
                for j in range(QUAD):
                    at = slice(j * NPB, (j + 1) * NPB)
                    pe.matmul(pY[s % 2][0:NPB, j * D:(j + 1) * D], sumT[:, at], e.g_w[:, :], start=True, stop=False)
                    m = pe.matmul(pY[s % 2][0:NPB, j * D:(j + 1) * D], ownT[s % 2][:, at], e.lin_w[:, :], start=False, stop=True)
                m.then_inc(s_y, 1)
            with pe.If(e.fast(pe)):
                pe.wait_ge(s_const, RING)
                pe.wait_ge(d_ov, 16)
                pipeline(pe, NQ, RING, [(1, turn), (1, sums), (2, linear)], 2)


def general(nc, e):
    N, D, H, DH, A, ET, NT, LASTN, DUMP, ROWS = e.N, e.D, e.H, e.DH, e.A, e.ET, e.NT, e.LASTN, e.DUMP, e.ROWS
    src_i, dst_i, src_f, dst_f, ident, below, dump, ones = e.src_i, e.dst_i, e.src_f, e.dst_f, e.ident, e.below, e.dump, e.ones
    with ExitStack() as ctx:
        def sem(name):
            return ctx.enter_context(nc.semaphore("g_" + name, num=e.spare.pop()))

        dinv = ctx.enter_context(nc.sbuf_tensor("g_dinv", [P, NT], F32))

        with ExitStack() as c1:
            zero = c1.enter_context(nc.sbuf_tensor("g_zero", [P, 25 * A], F32))
            s_zero = sem("s_zero_tile")
            s_z = sem("s_sums_zeroed")
            block = c1.enter_context(nc.Block())

            @block.vector
            def _(dve):
                with dve.If(e.slow(dve)):
                    dve.memset(zero[:, :], 0.0).then_inc(s_zero, 1)

            @block.scalar
            def _(act):
                with act.If(e.slow(act)):
                    act.wait_ge(s_zero, 1)
                    n = 0
                    for tab, w in ((e.sums0, A), (e.sums1, D)):
                        flat = tab.rearrange("r w -> (r w)").rearrange("(p f) -> p f", p=P)
                        step = 25 * A
                        for c in range(0, flat.shape[1], step):
                            m = min(step, flat.shape[1] - c)
                            act.dma_start(flat[:, c:c + m], zero[:, 0:m]).then_inc(s_z, 16)
                            n += 1
                    act.wait_ge(s_z, 16 * n)

        with ExitStack() as c2:
            hi_i = c2.enter_context(nc.sbuf_tensor("hi_i", [P, ET], I32))
            lo_i = c2.enter_context(nc.sbuf_tensor("lo_i", [P, ET], I32))
            hi_f = c2.enter_context(nc.sbuf_tensor("hi_f", [P, ET], F32))
            lo_f = c2.enter_context(nc.sbuf_tensor("lo_f", [P, ET], F32))
            cols_i = c2.enter_context(nc.sbuf_tensor("cols_i", [P, NT], I32))
            cols = c2.enter_context(nc.sbuf_tensor("cols", [P, NT], F16))
            hot_hi = c2.enter_context(nc.sbuf_tensor("hot_hi", [P, 2, NT], F16))
            hot_lo = c2.enter_context(nc.sbuf_tensor("hot_lo", [P, 2, P], F16))
            logdeg = c2.enter_context(nc.sbuf_tensor("logdeg", [P, NT], F32))
            deg = c2.enter_context(nc.psum_tensor("deg", [P, NT], F32))
            s_iota = sem("s_iota")
            s_hot = sem("s_one_hots")
            s_cnt = sem("s_counted")
            s_k = sem("s_keys_split")
            s_log = sem("s_logdeg")
            block = c2.enter_context(nc.Block())

            @block.gpsimd
            def _(pool):
                with pool.If(e.slow(pool)):
                    pool.iota(cols_i[:, :], pattern=[[1, NT]], base=0, channel_multiplier=0).then_inc(s_iota, 1)

            @block.vector
            def _(dve):
                with dve.If(e.slow(dve)):
                    dve.wait_ge(s_iota, 1)
                    dve.tensor_copy(cols[:, :], cols_i[:, :]).then_inc(s_k, 1)
                    dve.tensor_copy(lo_i[:, :], dst_f[:, :]).then_inc(s_k, 1)
                    dve.wait_ge(s_k, 2)
                    dve.tensor_single_scalar(hi_i[:, :], lo_i[:, :], 7, ALU.arith_shift_right).then_inc(s_k, 1)
                    dve.wait_ge(s_k, 3)
                    dve.tensor_single_scalar(lo_i[:, :], lo_i[:, :], P - 1, ALU.bitwise_and).then_inc(s_k, 1)
                    dve.wait_ge(s_k, 4)
                    dve.tensor_copy(hi_f[:, :], hi_i[:, :]).then_inc(s_k, 1)
                    dve.tensor_copy(lo_f[:, :], lo_i[:, :]).then_inc(s_k, 1)
                    dve.wait_ge(s_k, 6)
                    for b in range(2):
                        dve.tensor_scalar(hot_hi[:, b, :], cols[:, :], hi_f[:, b:b + 1], None, ALU.is_equal).then_inc(s_hot, 1)
                        dve.tensor_scalar(hot_lo[:, b, :], cols[:, 0:P], lo_f[:, b:b + 1], None, ALU.is_equal).then_inc(s_hot, 1)
                    with dve.Fori(1, ET // 2) as i:
                        for b in range(2):
                            dve.wait_ge(s_cnt, i * 2 + b - 1)
                            dve.tensor_scalar(hot_hi[:, b, :], cols[:, :], hi_f[:, bass.ds(i * 2 + b, 1)], None, ALU.is_equal).then_inc(s_hot, 1)
                            dve.tensor_scalar(hot_lo[:, b, :], cols[:, 0:P], lo_f[:, bass.ds(i * 2 + b, 1)], None, ALU.is_equal).then_inc(s_hot, 1)

            @block.tensor
            def _(pe):
                with pe.If(e.slow(pe)):
                    for t in range(2):
                        pe.wait_ge(s_hot, 2 * t + 2)
                        pe.matmul(deg[:, :], hot_lo[:, t, :], hot_hi[:, t, :], start=(t == 0), stop=False, skip_group_check=True).then_inc(s_cnt, 1)
                    with pe.Fori(1, ET // 2) as i:
                        for b in range(2):
                            pe.wait_ge(s_hot, i * 4 + 2 * b + 2)
                            pe.matmul(deg[:, :], hot_lo[:, b, :], hot_hi[:, b, :], start=False, stop=(b == 1), skip_group_check=True).then_inc(s_cnt, 1)

            @block.scalar
            def _(act):
                with act.If(e.slow(act)):
                    act.preload_act_table_set(ACT_SET)
                    act.wait_ge(s_cnt, ET)
                    act.activation(logdeg[:, :], deg[:, :], ACT.Ln, bias=ones[:, 0:1]).then_inc(s_log, 1)
                    act.wait_ge(s_log, 1)
                    act.activation(dinv[:, :], logdeg[:, :], ACT.Exp, scale=-0.5).then_inc(s_log, 1)
                    act.wait_ge(s_log, 2)

        with ExitStack() as c3:
            def tsb(name, shape, dt=F32):
                return c3.enter_context(nc.sbuf_tensor(name, shape, dt))

            def bank(name):
                return c3.enter_context(nc.psum_tensor(name, [P, 512], F32))

            gs = tsb("e_gs", [P, 1], I32)
            gd = tsb("e_gd", [P, 1], I32)
            key = tsb("e_key", [P, 1])
            off = tsb("e_off", [P, 1])
            tidx = tsb("e_tidx", [P, 1], I32)
            rank = tsb("e_rank", [P, 1])
            move = tsb("e_move", [P, 1])
            rows = tsb("e_rows", [P, 2, D])
            rowsT = tsb("e_rowsT", [D, 2, P])
            same = tsb("e_same", [P, P])
            junk = tsb("e_junk", [P, P])
            q_sb = tsb("e_q", [P, D])
            prod = tsb("e_prod", [P, D])
            score = tsb("e_score", [P, H])
            contrib = tsb("e_contrib", [P, A])
            total = tsb("e_total", [P, A])
            pT = bank("e_pT")[:, 0:2 * P].rearrange("p (a b) -> p a b", a=2)
            pkey = bank("e_pkey")[:, 0:P]
            pq = bank("e_pq")[:, 0:D]
            pkv = bank("e_pkv")[:, 0:2 * D]
            ptot = bank("e_ptot")[:, 0:A]

            for layer in range(2):
                W = A if layer == 0 else D
                table = e.sums0 if layer == 0 else e.sums1
                key_all = src_f if layer == 0 else dst_f
                with ExitStack() as c4:
                    L = f"l{layer}_"
                    s_st = sem(L + "s_staged")
                    s_rows = sem(L + "s_rows")
                    s_T = sem(L + "s_transposed")
                    s_Tc = sem(L + "s_transposed_copied")
                    s_qkv = sem(L + "s_qkv")
                    s_q = sem(L + "s_q_copied")
                    s_dve = sem(L + "s_dve_steps")
                    s_sc = sem(L + "s_scores")
                    s_e = sem(L + "s_exp")
                    s_con = sem(L + "s_contrib")
                    s_tot = sem(L + "s_totals")
                    s_totc = sem(L + "s_totals_copied")
                    s_add = sem(L + "s_added")
                    s_carry = sem(L + "s_carry")
                    block = c4.enter_context(nc.Block())
                    DVE_STEPS = 13 if layer == 0 else 8

                    @block.vector
                    def _(dve):
                        with dve.If(e.slow(dve)):
                            with dve.Fori(0, ET) as i:
                                st = Steps(dve, s_dve, DVE_STEPS, i)
                                dve.wait_ge(s_add, i * 16)
                                dve.tensor_copy(gs[:, :], src_i[:, bass.ds(i, 1)]).then_inc(s_st, 1)
                                dve.tensor_copy(gd[:, :], dst_i[:, bass.ds(i, 1)]).then_inc(s_st, 1)
                                dve.tensor_copy(key[:, :], key_all[:, bass.ds(i, 1)]).then_inc(s_st, 1)
                                dve.wait_ge(s_st, i * 3 + 3)
                                st.done(dve.tensor_tensor(off[:, :], dump[:, :], key[:, :], ALU.subtract))
                                dve.wait_ge(s_T, i + 1)
                                st.done(dve.tensor_scalar(same[:, :], pkey[:, :], key[:, 0:1], None, ALU.is_equal))
                                st.done(dve.tensor_tensor(junk[:, :], same[:, :], below[:, :], ALU.mult))
                                st.done(dve.tensor_reduce(rank[:, :], junk[:, :], AX, ALU.add))
                                st.done(dve.tensor_scalar(rank[:, :], rank[:, :], 0.0, None, ALU.is_gt))
                                st.done(dve.tensor_tensor(move[:, :], rank[:, :], off[:, :], ALU.mult))
                                st.done(dve.tensor_tensor(tidx[:, :], key[:, :], move[:, :], ALU.add))
                                if layer == 0:
                                    dve.wait_ge(s_qkv, i + 1)
                                    dve.wait_ge(s_q, i + 1)
                                    st.done(dve.tensor_tensor(prod[:, :], q_sb[:, :], pkv[:, 0:D], ALU.mult))
                                    st.done(dve.tensor_reduce(score[:, :], prod[:, :].rearrange("p (h d) -> p h d", h=H), AX, ALU.add))
                                    st.done(dve.tensor_scalar(score[:, :], score[:, :], 10.0, -10.0, ALU.min, ALU.max))
                                    dve.sem_inc(s_sc, 1)
                                    dve.wait_ge(s_e, i + 1)
                                    e_b = contrib[:, D:A].unsqueeze(2).to_broadcast([P, H, DH])
                                    st.done(dve.tensor_tensor(contrib[:, 0:D].rearrange("p (h d) -> p h d", h=H),
                                                              pkv[:, D:2 * D].rearrange("p (h d) -> p h d", h=H), e_b, ALU.mult))
                                    st.done(dve.tensor_copy(junk[:, 0:1], rank[:, :]))
                                dve.sem_inc(s_con, 1)
                                dve.wait_ge(s_tot, i + 1)
                                st.done(dve.tensor_copy(total[:, 0:W], ptot[:, 0:W]))
                                dve.sem_inc(s_totc, 1)
                                st.end()

                    @block.gpsimd
                    def _(pool):
                        with pool.If(e.slow(pool)):
                            with pool.Fori(0, ET) as i:
                                pool.wait_ge(s_st, i * 3 + 3)
                                pool.sem_inc(s_carry, 1)
                                if layer == 0:
                                    pool.indirect_dma_start(rows[:, 0, :], None, e.x[:, :],
                                                            bass.IndirectOffsetOnAxis(ap=gs[:, 0:1], axis=0)).then_inc(s_rows, 16)
                                    pool.indirect_dma_start(rows[:, 1, :], None, e.x[:, :],
                                                            bass.IndirectOffsetOnAxis(ap=gd[:, 0:1], axis=0)).then_inc(s_rows, 16)
                                else:
                                    pool.indirect_dma_start(rows[:, 0, :], None, e.x1s_plain[:, :],
                                                            bass.IndirectOffsetOnAxis(ap=gs[:, 0:1], axis=0)).then_inc(s_rows, 16)
                                pool.wait_ge(s_totc, i + 1)
                                pool.sem_inc(s_carry, 1)
                                pool.indirect_dma_start(table[:, :], bass.IndirectOffsetOnAxis(ap=tidx[:, 0:1], axis=0),
                                                        total[:, 0:W], None, compute_op=ALU.add).then_inc(s_add, 16)
                            pool.wait_ge(s_add, 16 * ET)

                    @block.tensor
                    def _(pe):
                        with pe.If(e.slow(pe)):
                            with pe.Fori(0, ET) as i:
                                pe.wait_ge(s_st, i * 3 + 3)
                                t = pe.transpose(pkey[:, :], key[:, 0:1].to_broadcast([P, P]), ident[:, :])
                                if layer == 0:
                                    pe.wait_ge(s_rows, i * 32 + 32)
                                    pe.sem_inc(s_carry, 1)
                                    pe.transpose(pT[0:D, 0, :], rows[:, 0, :], ident[:, :])
                                    t = pe.transpose(pT[0:D, 1, :], rows[:, 1, :], ident[:, :])
                                t.then_inc(s_T, 1)
                                if layer == 0:
                                    pe.wait_ge(s_Tc, i + 1)
                                    pe.sem_inc(s_carry, 1)
                                    pe.matmul(pq[:, :], rowsT[:, 0, :], e.q_w[:, :], start=True, stop=True)
                                    pe.matmul(pkv[:, :], rowsT[:, 1, :], e.kv_w[:, :], start=True, stop=True).then_inc(s_qkv, 1)
                                pe.wait_ge(s_con, i + 1)
                                if layer == 1:
                                    pe.wait_ge(s_rows, i * 16 + 16)
                                pe.sem_inc(s_carry, 1)
                                pe.matmul(ptot[:, 0:W], same[:, :], contrib[:, 0:W] if layer == 0 else rows[:, 0, :],
                                          start=True, stop=True).then_inc(s_tot, 1)

                    if layer == 0:
                        @block.scalar
                        def _(act):
                            with act.If(e.slow(act)):
                                act.preload_act_table_set(ACT_SET)
                                with act.Fori(0, ET) as i:
                                    act.wait_ge(s_T, i + 1)
                                    act.activation(rowsT[:, :, :], pT[0:D, 0:2, :], ACT.Copy).then_inc(s_Tc, 1)
                                    act.wait_ge(s_qkv, i + 1)
                                    act.activation(q_sb[:, :], pq[:, :], ACT.Copy).then_inc(s_q, 1)
                                    act.wait_ge(s_sc, i + 1)
                                    act.activation(contrib[:, D:A], score[:, :], ACT.Exp).then_inc(s_e, 1)

                if layer == 0:
                    dense(nc, e, dinv, 0)
        dense(nc, e, dinv, 1)



def dense(nc, e, dinv, layer):
    N, D, H, DH, NT, A, LASTN = e.N, e.D, e.H, e.DH, e.NT, e.A, e.LASTN
    ident, ones, eps, bias2 = e.ident, e.ones, e.eps, e.bias2
    with ExitStack() as c:
        L = f"d{layer}_"

        def tsb(name, shape, dt=F32):
            return c.enter_context(nc.sbuf_tensor(L + name, shape, dt))

        def sem(name):
            return c.enter_context(nc.semaphore(L + name, num=e.spare.pop()))

        xin = tsb("xin", [P, D])
        acc = tsb("acc", [P, A])
        agg = tsb("agg", [P, D])
        own = tsb("own", [P, D])
        rec = tsb("rec", [P, H])
        h = tsb("h", [P, D])
        stats = tsb("stats", [P, 6])
        mv = tsb("mv", [P, 2])
        lnv = tsb("lnv", [P, 1])
        rstd = tsb("rstd", [P, 1])
        y1 = tsb("y1", [P, D])
        y2 = tsb("y2", [P, D])
        rT = tsb("rT", [D, 2, P])
        num = tsb("num", [P, D])
        den = tsb("den", [P, D])
        pT = c.enter_context(nc.psum_tensor(L + "pT", [P, 512], F32))[0:D, 0:2 * P].rearrange("p (a b) -> p a b", a=2)
        py = c.enter_context(nc.psum_tensor(L + "py", [P, 512], F32))[:, 0:D]
        s_in = sem("s_in")
        s_dve = sem("s_dve_steps")
        s_var = sem("s_var")
        s_rstd = sem("s_rstd")
        s_y = sem("s_y")
        s_out = sem("s_out")
        s_act = sem("s_act_steps")
        s_agg = sem("s_agg")
        s_T = sem("s_T")
        s_Tc = sem("s_Tc")
        s_lin = sem("s_lin")
        s_e = sem("s_exp")
        s_cap = sem("s_cap")
        s_carry = sem("s_carry")
        s_bn = sem("s_bn")
        block = c.enter_context(nc.Block())
        full = NT - 1
        INS = 2 if layer == 0 else 3
        OUTS = 2 if layer == 0 else 1
        DVE_STEPS = 9 if layer == 0 else 12

        def loop(eng, body):
            with eng.Fori(0, full) as i:
                body(i, P)
            body(full, LASTN)

        @block.sync
        def _(sp):
            with sp.If(e.slow(sp)):
                def body(i, n):
                    at = bass.ds(i * P, n)
                    sp.wait_ge(s_out, i * OUTS * 16)
                    if layer == 0:
                        sp.dma_start(xin[0:n, :], e.x[at, :]).then_inc(s_in, 16)
                        sp.dma_start(acc[0:n, :], e.sums0[at, :]).then_inc(s_in, 16)
                    else:
                        sp.dma_start(xin[0:n, :], e.x1_plain[at, :]).then_inc(s_in, 16)
                        sp.dma_start(own[0:n, :], e.x1s_plain[at, :]).then_inc(s_in, 16)
                        sp.dma_start(acc[0:n, 0:D], e.sums1[at, :]).then_inc(s_in, 16)
                    sp.wait_ge(s_y, i + 1)
                    if layer == 0:
                        sp.dma_start(e.x1_plain[at, :], y1[0:n, :]).then_inc(s_out, 16)
                        sp.dma_start(e.x1s_plain[at, :], y2[0:n, :]).then_inc(s_out, 16)
                    else:
                        sp.dma_start(e.out[at, :], y1[0:n, :]).then_inc(s_out, 16)
                loop(sp, body)
                sp.wait_ge(s_out, NT * OUTS * 16)

        @block.vector
        def _(dve):
            with dve.If(e.slow(dve)):
                def body(i, n):
                    st = Steps(dve, s_dve, DVE_STEPS, i)
                    dve.wait_ge(s_in, (i + 1) * INS * 16)
                    if layer == 0:
                        st.done(dve.tensor_scalar(rec[0:n, :], acc[0:n, D:A], 1e-8, None, ALU.add))
                        st.done(dve.reciprocal(rec[0:n, :], rec[0:n, :]))
                        st.done(dve.tensor_tensor(h[0:n, :].rearrange("p (h d) -> p h d", h=H),
                                                  acc[0:n, 0:D].rearrange("p (h d) -> p h d", h=H),
                                                  rec[0:n, :].unsqueeze(2).to_broadcast([n, H, DH]), ALU.mult))
                        st.done(dve.scalar_tensor_tensor(h[0:n, :], xin[0:n, :], 2.0, h[0:n, :], ALU.mult, ALU.add))
                    else:
                        st.done(dve.tensor_tensor(agg[0:n, :], acc[0:n, 0:D], own[0:n, :], ALU.add))
                        st.done(dve.tensor_scalar(agg[0:n, :], agg[0:n, :], dinv[0:n, bass.ds(i, 1)], None, ALU.mult))
                        dve.sem_inc(s_agg, 1)
                        dve.wait_ge(s_lin, i + 1)
                        st.done(dve.tensor_scalar(h[0:n, :], py[0:n, :], 20.0, None, ALU.min))
                        dve.sem_inc(s_cap, 1)
                        dve.wait_ge(s_e, i + 1)
                        st.done(dve.scalar_tensor_tensor(num[0:n, :], y2[0:n, :], 2.0, y2[0:n, :], ALU.add, ALU.mult))
                        st.done(dve.tensor_scalar(den[0:n, :], num[0:n, :], 2.0, None, ALU.add))
                        st.done(dve.reciprocal(den[0:n, :], den[0:n, :]))
                        st.done(dve.tensor_tensor(num[0:n, :], num[0:n, :], den[0:n, :], ALU.mult))
                        st.done(dve.tensor_tensor(num[0:n, :], num[0:n, :], py[0:n, :], ALU.mult))
                        st.done(dve.tensor_tensor(h[0:n, :], num[0:n, :], xin[0:n, :], ALU.add))
                    st.done(dve.bn_stats(stats[0:n, :], h[0:n, :]))
                    dve.sem_inc(s_bn, 1)
                    st.done(dve.bn_aggr(mv[0:n, :], stats[0:n, :]))
                    dve.sem_inc(s_var, 1)
                    dve.wait_ge(s_rstd, i + 1)
                    st.done(dve.tensor_scalar(y1[0:n, :], h[0:n, :], mv[0:n, 0:1], rstd[0:n, :], ALU.subtract, ALU.mult))
                    if layer == 0:
                        st.done(dve.tensor_scalar(y2[0:n, :], y1[0:n, :], dinv[0:n, bass.ds(i, 1)], None, ALU.mult))
                        st.done(dve.tensor_copy(lnv[0:n, :], rstd[0:n, :]))
                    dve.sem_inc(s_y, 1)
                    st.end()
                loop(dve, body)

        if layer == 1:
            @block.tensor
            def _(pe):
                with pe.If(e.slow(pe)):
                    def body(i, n):
                        pe.wait_ge(s_agg, i + 1)
                        pe.sem_inc(s_carry, 1)
                        pe.transpose(pT[:, 0, 0:n], agg[0:n, :], ident[0:n, 0:n])
                        pe.transpose(pT[:, 1, 0:n], xin[0:n, :], ident[0:n, 0:n]).then_inc(s_T, 1)
                        pe.wait_ge(s_Tc, i + 1)
                        pe.sem_inc(s_carry, 1)
                        pe.matmul(py[0:n, :], rT[:, 0, 0:n], e.g_w[:, :], start=True, stop=False)
                        pe.matmul(py[0:n, :], rT[:, 1, 0:n], e.lin_w[0:D, :], start=False, stop=False)
                        pe.matmul(py[0:n, :], ones[0:2, 0:n], bias2[:, :], start=False, stop=True).then_inc(s_lin, 1)
                    loop(pe, body)

        @block.scalar
        def _(act):
            with act.If(e.slow(act)):
                def body(i, n):
                    if layer == 1:
                        act.wait_ge(s_T, i + 1)
                        act.activation(rT[:, :, 0:n], pT[:, :, 0:n], ACT.Copy).then_inc(s_Tc, 1)
                        act.wait_ge(s_cap, i + 1)
                        act.activation(y2[0:n, :], h[0:n, :], ACT.Exp).then_inc(s_e, 1)
                    act.wait_ge(s_var, i + 1)
                    act.activation(lnv[0:n, :], mv[0:n, 1:2], ACT.Ln, bias=eps[0:n, :]).then_inc(s_act, 1)
                    act.wait_ge(s_act, i + 1)
                    act.activation(rstd[0:n, :], lnv[0:n, :], ACT.Exp, scale=-0.5).then_inc(s_rstd, 1)
                act.preload_act_table_set(ACT_SET)
                loop(act, body)


def gnn(nc, x, src, dst, qW, kW, vW, gW, gb, lW, lb, out):
    N, D = x.shape
    E = src.shape[0]
    H = 4
    NPB = 108
    NQ = -(-N // (QUAD * NPB))
    NB = NQ * QUAD
    ET = -(-E // P)
    ET += -ET % 28
    LASTE = E - (P - 1) * ET
    NT = -(-N // P)
    A = D + H
    R1 = D + 4
    DUMP = N
    ROWS = N + P + (-(N + P)) % P
    assert NB + 2 <= 512 and ET <= 512 and N < 2 ** 16 and NPB < P and NQ % 4 == 0
    assert (N - (NQ - 1) * QUAD * NPB) % QUAD == 0

    with ExitStack() as ctx:
        def sb(name, shape, dt=F32):
            return ctx.enter_context(nc.sbuf_tensor(name, shape, dt))

        def sem(name):
            return ctx.enter_context(nc.semaphore(name))

        e = Shared()
        e.N, e.D, e.H, e.DH, e.A, e.R1 = N, D, H, D // H, A, R1
        e.NB, e.NPB, e.NQ, e.ET, e.NT, e.LASTN, e.DUMP, e.ROWS = NB, NPB, NQ, ET, NT, N - (NT - 1) * P, DUMP, ROWS
        e.x, e.out, e.spare = x, out, []
        e.sums0 = nc.dram_tensor("sums0", (ROWS, A), F32).ap()
        e.sums1 = nc.dram_tensor("sums1", (ROWS, D), F32).ap()
        e.x1_plain = nc.dram_tensor("x1_plain", (N, D), F32).ap()
        e.x1s_plain = nc.dram_tensor("x1s_plain", (N, D), F32).ap()
        e.x1_rows = nc.dram_tensor("x1_rows", (N, R1), F32).ap()
        e.dinv_rows = nc.dram_tensor("dinv_rows", (NB, NPB), F32).ap()

        e.src_i = sb("src_i", [P, ET], I32)
        e.dst_i = sb("dst_i", [P, ET], I32)
        e.src_f = sb("src_f", [P, ET])
        e.dst_f = sb("dst_f", [P, ET])
        e.q_w = sb("q_w", [D, D])
        e.kv_w = sb("kv_w", [D, 2 * D])
        e.g_w = sb("g_w", [D, D])
        e.lin_w = sb("lin_w", [R1, D])
        e.bias2 = sb("bias2", [2, D])
        e.ones = sb("ones", [P, P])
        e.ones16 = sb("ones16", [P, P], F16)
        e.ident = sb("ident", [P, P])
        e.ident16 = sb("ident16", [P, P], F16)
        e.below = sb("below", [P, P])
        e.earlier16 = sb("earlier16", [P, P], F16)
        e.not_before = sb("not_before", [P, P], F16)
        e.dump = sb("dump", [P, 1])
        e.iota = sb("iota", [P, P])
        e.iota16 = sb("iota16", [P, NB + 2], F16)
        e.quad_rows = sb("quad_rows", [P, QUAD, NPB])
        e.quad_start = sb("quad_start", [P, NQ])
        e.eps, e.minus_one, e.two, e.twenty = [sb(n, [P, 1]) for n in ("eps", "minus_one", "two", "twenty")]
        e.over = sb("over", [P, 2])
        e.flag = sb("flag", [P, 1], I32)
        e.dinv_b = sb("dinv_b", [NPB, NB])
        tables = []
        for t in ("src", "dst"):
            v = Shared()
            v.oth, v.lo = sb(t + "_oth", [P, NB + 1]), sb(t + "_lo", [P, NB + 1])
            v.ov_b, v.ov_key, v.ov_row = sb(t + "_ov_b", [P, 1]), sb(t + "_ov_key", [P, 1]), sb(t + "_ov_row", [P, NQ])
            tables.append(v)
        e.fast = lambda eng: eng.value_load(e.flag[0:1, 0:1], min_val=0, max_val=1) < 1
        e.slow = lambda eng: eng.value_load(e.flag[0:1, 0:1], min_val=0, max_val=1) > 0

        with ExitStack() as c1:
            s_ld, s_w, s_pad, s_c, s_d, s_lin = [c1.enter_context(nc.semaphore(n)) for n in
                                                 ("s_edges", "s_weights", "s_pads_set", "s_pool_constants", "s_dve_constants", "s_lin")]
            ints = c1.enter_context(nc.sbuf_tensor("ints", [P, 512], I32))
            ints_q = c1.enter_context(nc.sbuf_tensor("ints_q", [P, QUAD, NPB], I32))
            ints_s = c1.enter_context(nc.sbuf_tensor("ints_s", [P, NQ], I32))
            ints_d = c1.enter_context(nc.sbuf_tensor("ints_d", [P, 1], I32))
            block = c1.enter_context(nc.Block())

            @block.sync
            def _(sp):
                sp.wait_ge(s_pad, 2)
                for t, s in ((e.src_i, src), (e.dst_i, dst)):
                    sp.dma_start(t[0:P - 1, :], s[0:(P - 1) * ET].rearrange("(p t) -> p t", t=ET)).then_inc(s_ld, 16)
                    sp.dma_start(t[P - 1:P, 0:LASTE], s[(P - 1) * ET:E].rearrange("(p t) -> p t", p=1)).then_inc(s_ld, 16)
                sp.wait_ge(s_lin, 1)
                for t, s in ((e.q_w[:, :], qW), (e.kv_w[:, 0:D], kW), (e.kv_w[:, D:2 * D], vW), (e.g_w[:, :], gW), (e.lin_w[0:D, :], lW)):
                    sp.dma_start(t, s).then_inc(s_w, 16)
                for r, s in enumerate((gb, lb)):
                    sp.dma_start(e.bias2[r:r + 1, :], s.rearrange("(a n) -> a n", a=1)).then_inc(s_w, 16)
                    sp.dma_start(e.lin_w[D + 1 + r:D + 2 + r, :], s.rearrange("(a n) -> a n", a=1)).then_inc(s_w, 16)
                sp.wait_ge(s_w, 16 * 9)
                sp.wait_ge(s_ld, 16 * 4)

            @block.gpsimd
            def _(pool):
                pool.iota(ints[:, :], pattern=[[1, 512]], base=0, channel_multiplier=0).then_inc(s_c, 1)
                pool.iota(ints_q[:, :, :], pattern=[[1, QUAD], [QUAD, NPB]], base=0, channel_multiplier=0).then_inc(s_c, 1)
                pool.iota(ints_s[:, :], pattern=[[QUAD * NPB, NQ]], base=0, channel_multiplier=0).then_inc(s_c, 1)
                pool.iota(ints_d[:, :], pattern=[[0, 1]], base=DUMP, channel_multiplier=1).then_inc(s_c, 1)
                for t in (e.ident, e.ident16, e.below, e.not_before):
                    pool.memset(t[:, :], 0.0).then_inc(s_c, 1)
                pool.memset(e.earlier16[:, :], 1.0).then_inc(s_c, 1)
                pool.wait_ge(s_c, 9)
                for t in (e.ident, e.ident16):
                    pool.affine_select(out=t[:, :], in_=t[:, :], compare_op=ALU.not_equal, fill=1.0,
                                       base=0, pattern=[[-1, P]], channel_multiplier=1).then_inc(s_c, 1)
                pool.affine_select(out=e.below[:, :], in_=e.below[:, :], compare_op=ALU.is_ge, fill=1.0,
                                   base=0, pattern=[[1, P]], channel_multiplier=-1).then_inc(s_c, 1)
                pool.affine_select(out=e.not_before[:, :], in_=e.not_before[:, :], compare_op=ALU.is_gt, fill=-2.0,
                                   base=0, pattern=[[-1, P]], channel_multiplier=1).then_inc(s_c, 1)
                pool.affine_select(out=e.earlier16[:, :], in_=e.earlier16[:, :], compare_op=ALU.is_gt, fill=0.0,
                                   base=0, pattern=[[1, P]], channel_multiplier=-1).then_inc(s_c, 1)
                pool.wait_ge(s_c, 14)

            @block.vector
            def _(dve):
                dve.memset(e.src_i[:, :], DUMP + P - 1).then_inc(s_pad, 1)
                dve.memset(e.dst_i[:, :], DUMP + P - 1).then_inc(s_pad, 1)
                dve.memset(e.lin_w[:, :], 0.0).then_inc(s_lin, 1)
                for t, v in ((e.ones, 1.0), (e.ones16, 1.0), (e.eps, EPS_LN), (e.minus_one, -1.0), (e.two, 2.0), (e.twenty, 20.0)):
                    dve.memset(t[:, :], v).then_inc(s_d, 1)
                dve.wait_ge(s_c, 4)
                dve.tensor_copy(e.dump[:, :], ints_d[:, :]).then_inc(s_d, 1)
                dve.tensor_copy(e.iota[:, :], ints[:, 0:P]).then_inc(s_d, 1)
                dve.tensor_copy(e.iota16[:, :], ints[:, 0:NB + 2]).then_inc(s_d, 1)
                dve.tensor_copy(e.quad_rows[:, :, :], ints_q[:, :, :]).then_inc(s_d, 1)
                dve.tensor_copy(e.quad_start[:, :], ints_s[:, :]).then_inc(s_d, 1)
                dve.wait_ge(s_ld, 16 * 4)
                dve.tensor_copy(e.src_f[:, :], e.src_i[:, :]).then_inc(s_pad, 1)
                dve.tensor_copy(e.dst_f[:, :], e.dst_i[:, :]).then_inc(s_pad, 1)
                dve.wait_ge(s_pad, 4)
                dve.tensor_scalar_min(e.src_i[:, :], e.src_f[:, :], float(N - 1)).then_inc(s_pad, 1)
                dve.tensor_scalar_min(e.dst_i[:, :], e.dst_f[:, :], float(N - 1)).then_inc(s_pad, 1)
                dve.wait_ge(s_pad, 6)
                dve.wait_ge(s_d, 11)

        for k, (t, key, other) in enumerate((("src", e.src_f, e.dst_f), ("dst", e.dst_f, e.src_f))):
            v = tables[k]
            e.oth, e.lo, e.ov_b, e.ov_key, e.ov_row, e.over_at = v.oth, v.lo, v.ov_b, v.ov_key, v.ov_row, k
            slots_by_block(nc, e, t + "_", key[:, :], other[:, :])
        with ExitStack() as c1:
            s_flag = c1.enter_context(nc.semaphore("s_flag"))
            block = c1.enter_context(nc.Block())

            @block.vector
            def _(dve):
                ch = Chain(dve, s_flag)
                ch.done(dve.tensor_tensor(e.over[:, 0:1], e.over[:, 0:1], e.over[:, 1:2], ALU.max))
                ch.done(dve.tensor_scalar(e.flag[:, :], e.over[:, 0:1], float(P), None, ALU.is_gt))

        degrees(nc, e, tables[1])
        attention(nc, e, tables[0])
        convolution(nc, e, tables[1])
        general(nc, e)


def kernel(**inputs):
    import numpy as np
    import concourse.bacc as bacc
    from concourse.bass_utils import run_bass_kernel_spmd
    nc = bacc.Bacc("TRN2", target_bir_lowering=False, num_devices=1)
    names = ("x", "src", "dst", "L0_gnn_qW", "L0_gnn_kW", "L0_gnn_vW",
             "L1_gnn_W_gcn", "L1_gnn_b_gcn", "L1_gnn_W_lin", "L1_gnn_b_lin")
    arrays, aps = {}, []
    for n in names:
        a = np.ascontiguousarray(inputs[n])
        arrays["in_" + n] = a
        aps.append(nc.dram_tensor("in_" + n, a.shape, mybir.dt.from_np(a.dtype), kind="ExternalInput").ap())
    out = nc.dram_tensor("out", inputs["x"].shape, F32, kind="ExternalOutput").ap()
    gnn(nc, *aps, out)
    r = run_bass_kernel_spmd(nc, [arrays], core_ids=[0])
    return r.results[0]["out"]
```

```python
import concourse.bass as bass
from concourse import mybir
from contextlib import ExitStack

F32 = mybir.dt.float32
F16 = mybir.dt.float16
I32 = mybir.dt.int32
ALU = mybir.AluOpType
ACT = mybir.ActivationFunctionType
AX = mybir.AxisListType.X

P = 128
QUAD = 4
EPS_LN = 1e-5
EPS_NORM = 1e-8
LIMIT = 10.0
ROUND = 1.5 * 2 ** 23
ACT_SET = "natural_log_exp_and_others"


class Shared:
    pass


class Steps:

    def __init__(self, eng, sem, per, i):
        self.eng, self.sem, self.per, self.i, self.k = eng, sem, per, i, 0

    def done(self, ins):
        self.k += 1
        ins.then_inc(self.sem, 1)
        self.eng.wait_ge(self.sem, self.i * self.per + self.k)

    def end(self):
        assert self.k == self.per, (self.k, self.per)


class Chain:

    def __init__(self, eng, e):
        self.eng, self.e, self.sem, self.k = eng, e, e.steps, e.steps_done

    def done(self, ins):
        self.k += 1
        self.e.steps_done = self.k
        ins.then_inc(self.sem, 1)
        self.eng.wait_ge(self.sem, self.k)


def wait(eng, sem, value):
    if not (isinstance(value, int) and value <= 0):
        eng.wait_ge(sem, value)


def after(eng, sem, u, back=0):
    wait(eng, sem, u + 1 - back)


def landed(eng, sems, slot, h, per, back=0):
    wait(eng, sems[slot], (h + 1 - back) * per)


def pipeline(eng, n, ring, stages, head=1):
    def at(u, k, s, lag):
        return u - lag, (s - lag) % ring, k + (s - lag) // ring

    rounds = (n - 1) // ring
    for u in range(ring * head):
        for lag, f in stages:
            if u >= lag:
                f(*at(u, u // ring, u % ring, lag))
    with eng.Fori(head, rounds) as k:
        for s in range(ring):
            for lag, f in stages:
                f(*at(k * ring + s, k, s, lag))
    most = max(lag for lag, _ in stages)
    for u in range(rounds * ring, n + most):
        for lag, f in stages:
            if u - lag < n:
                f(*at(u, u // ring, u % ring, lag))


def cut_into_integers(dve, ch, out, a, n):
    ch.done(dve.tensor_scalar(out, a, 1.0 / n, -(n - 1) / (2.0 * n), ALU.mult, ALU.add))
    ch.done(dve.tensor_scalar(out, out, ROUND, -ROUND, ALU.add, ALU.add))


def slots_by_block(nc, e, tag, key, other):
    ET, NB, NPB = e.ET, e.NB, e.NPB
    OV = NB
    HI, LO = 32, 16
    CH = 4
    LK = 14
    with ExitStack() as c:
        def sb(name, shape, dt=F32):
            return c.enter_context(nc.sbuf_tensor(tag + name, shape, dt))

        def sem(name):
            return c.enter_context(nc.semaphore(tag + name))

        b = sb("b", [P, ET])
        val_hi = sb("val_hi", [P, ET])
        val_lo = sb("val_lo", [P, ET])
        rank = sb("rank", [P, ET])
        base = sb("base", [P, ET])
        bhl = sb("bhl", [P, 2, ET])
        t1 = sb("t1", [P, ET])
        t2 = sb("t2", [P, ET])
        ov16 = sb("ov16", [P, ET], F16)
        ovb16 = sb("ovb16", [P, ET], F16)

        with ExitStack() as c1:
            hot = c1.enter_context(nc.sbuf_tensor(tag + "hot", [P, ET, 64], F16))
            hotT = c1.enter_context(nc.sbuf_tensor(tag + "hotT", [P, ET // 2, P], F16))
            hist = c1.enter_context(nc.sbuf_tensor(tag + "hist", [HI, ET, LO], F32))
            seen = c1.enter_context(nc.sbuf_tensor(tag + "seen", [P, ET + 2, LO], F16))
            turned = c1.enter_context(nc.sbuf_tensor(tag + "turned", [P, 4, CH // 2, P], F16))
            near = c1.enter_context(nc.sbuf_tensor(tag + "near", [P, 4, CH, P], F16))
            prod = c1.enter_context(nc.sbuf_tensor(tag + "prod", [P, 2, LK, LO], F32))
            s_seen0 = sem("s_seen_zeroed")
            with nc.Block() as block:
                @block.gpsimd
                def _(pool):
                    pool.memset(seen[:, :, :], 0.0).then_inc(s_seen0, 1)
                    pool.memset(hot[:, :, 48:64], 0.0).then_inc(s_seen0, 1)
                    pool.wait_ge(s_seen0, 2)

                @block.vector
                def _(dve):
                    ch = Chain(dve, e)
                    q, r, lo, j = t1[:, :], t2[:, :], rank[:, :], base[:, :]
                    cut_into_integers(dve, ch, q, key, QUAD * NPB)
                    ch.done(dve.scalar_tensor_tensor(r, q, -float(QUAD * NPB), key, ALU.mult, ALU.add))
                    cut_into_integers(dve, ch, lo, r, QUAD)
                    ch.done(dve.scalar_tensor_tensor(j, lo, -float(QUAD), r, ALU.mult, ALU.add))
                    ch.done(dve.scalar_tensor_tensor(b[:, :], q, float(QUAD), j, ALU.mult, ALU.add))
                    ch.done(dve.tensor_scalar(q, b[:, :], float(NB), 1000.0, ALU.is_ge, ALU.mult))
                    ch.done(dve.tensor_tensor(b[:, :], b[:, :], q, ALU.add))
                    ch.done(dve.scalar_tensor_tensor(r, other, float(P), lo, ALU.mult, ALU.add))
                    ch.done(dve.tensor_scalar(r, r, 1.0, None, ALU.add))
                    ch.done(dve.tensor_scalar(val_hi[:, :], r, 1.0 / 4096, None, ALU.mult))
                    ch.done(dve.tensor_scalar(val_hi[:, :], val_hi[:, :], ROUND, -ROUND, ALU.add, ALU.add))
                    ch.done(dve.scalar_tensor_tensor(val_lo[:, :], val_hi[:, :], -4096.0, r, ALU.mult, ALU.add))
                    cut_into_integers(dve, ch, bhl[:, 0, :], b[:, :], LO)
                    ch.done(dve.scalar_tensor_tensor(bhl[:, 1, :], bhl[:, 0, :], -float(LO), b[:, :], ALU.mult, ALU.add))
                    ch.done(dve.tensor_tensor(hot[:, :, 0:HI], e.iota[:, 0:HI].unsqueeze(1).to_broadcast([P, ET, HI]),
                                              bhl[:, 0, :].unsqueeze(2).to_broadcast([P, ET, HI]), ALU.is_equal))
                    ch.done(dve.tensor_tensor(hot[:, :, HI:HI + LO], e.iota[:, 0:LO].unsqueeze(1).to_broadcast([P, ET, LO]),
                                              bhl[:, 1, :].unsqueeze(2).to_broadcast([P, ET, LO]), ALU.is_equal))

            with ExitStack() as c2:
                def bank(name, dt=F32):
                    return c2.enter_context(nc.psum_tensor(tag + name, [P, 2048 // (4 if dt == F32 else 2)], dt))

                pT = [bank(f"pT{i}", F16) for i in range(2)]
                pH = [bank(f"pH{i}") for i in range(2)]
                pS = [[bank(f"pS{i}{j}") for j in range(2)] for i in range(2)]
                s_T = sem("s_T")
                s_Tc = sem("s_T_copied")
                s_H = sem("s_hist")
                s_Hc = sem("s_hist_copied")
                s_same = sem("s_same")
                s_near = sem("s_near")
                s_kept = sem("s_kept")
                s_red = sem("s_reduced")
                NC = ET // CH
                block = c2.enter_context(nc.Block())

                def chunks(eng, stages):
                    pipeline(eng, NC, 4, stages)

                @block.tensor
                def _(pe):
                    def turn(u, s, h):
                        after(pe, s_Tc, u, 2)
                        pe.sem_inc(e.carry, 1)
                        row = hot[:, bass.ds(u * CH, CH), :]
                        for k in range(CH // 2):
                            m = pe.transpose(pT[s % 2][:, k * P:(k + 1) * P], row[:, 2 * k:2 * k + 2, :].rearrange("p a b -> p (a b)"),
                                             e.ident16[:, :])
                        m.then_inc(s_T, 1)
                        after(pe, s_Hc, u, 2)
                        pe.sem_inc(e.carry, 1)
                        for k in range(CH):
                            m = pe.matmul(pH[s % 2][0:HI, k * LO:(k + 1) * LO], row[:, k, 0:HI], row[:, k, HI:HI + LO], start=True, stop=True)
                        m.then_inc(s_H, 1)

                    def same(u, s, h):
                        after(pe, s_near, u, 2)
                        after(pe, s_Tc, u)
                        pe.sem_inc(e.carry, 1)
                        for half in range(2):
                            pe.matmul(pS[s % 2][half][:, 0:CH // 2 * P], e.ident16[:, :],
                                      e.not_before[:, :].unsqueeze(1).to_broadcast([P, CH // 2, P]),
                                      start=True, stop=False, skip_group_check=True)
                        for k in range(CH):
                            half = 64 * (k % 2)
                            t = turned[half:half + 48, s, k // 2, :]
                            m = pe.matmul(pS[s % 2][k % 2][:, k // 2 * P:(k // 2 + 1) * P], t, t, start=False, stop=True, skip_group_check=True)
                        m.then_inc(s_same, 1)
                    chunks(pe, [(0, turn), (1, same)])

                @block.scalar
                def _(act):
                    def near_(u, s, h):
                        after(act, s_same, u)
                        after(act, s_red, u, 4)
                        for half in range(2):
                            m = act.activation(near[:, s, half:CH:2, :], pS[s % 2][half][:, 0:CH // 2 * P].rearrange("p (a b) -> p a b", b=P),
                                               ACT.Relu, bias=e.minus_one[:, 0:1])
                        m.then_inc(s_near, 1)

                    def keep(u, s, h):
                        after(act, s_Tc, u)
                        act.activation(hotT[:, bass.ds(u * (CH // 2), CH // 2), :], turned[:, s, :, :], ACT.Copy).then_inc(s_kept, 1)
                    chunks(act, [(0, keep), (1, near_)])

                @block.vector
                def _(dve):
                    def copies(u, s, h):
                        after(dve, s_T, u)
                        after(dve, s_same, u, 4)
                        after(dve, s_kept, u, 4)
                        dve.tensor_copy(turned[:, s, :, :],
                                        pT[s % 2][:, 0:CH // 2 * P].rearrange("p (a b) -> p a b", b=P)).then_inc(s_Tc, 1)
                        after(dve, s_H, u)
                        dve.tensor_copy(hist[:, bass.ds(u * CH, CH), :],
                                        pH[s % 2][0:HI, 0:CH * LO].rearrange("p (a b) -> p a b", b=LO)).then_inc(s_Hc, 1)

                    def reduce(u, s, h):
                        after(dve, s_near, u)
                        dve.tensor_reduce(rank[:, bass.ds(u * CH, CH)], near[:, s, :, :], AX, ALU.add).then_inc(s_red, 1)
                    chunks(dve, [(0, copies), (2, reduce)])

            s_scan = sem("s_scanned")
            s_twice = sem("s_seen_copied")
            with nc.Block() as block:
                @block.vector
                def _(dve):
                    for l in range(LO):
                        dve.tensor_tensor_scan(seen[0:HI, 1:ET + 1, l], e.ones[0:HI, 0:1].to_broadcast([HI, ET]), hist[:, :, l],
                                               0.0, ALU.mult, ALU.add).then_inc(s_scan, 1)
                    dve.wait_ge(s_twice, 16)
                    dve.tensor_scalar(seen[0:HI, 1:ET + 1:2, :], seen[0:HI, 1:ET + 1:2, :], 0.0, None, ALU.mult).then_inc(s_scan, 1)
                    dve.tensor_scalar(seen[64:64 + HI, 0:ET + 1:2, :], seen[64:64 + HI, 0:ET + 1:2, :], 0.0, None, ALU.mult).then_inc(s_scan, 1)
                    dve.wait_ge(s_scan, LO + 2)

                @block.sync
                def _(sp):
                    sp.wait_ge(s_scan, LO)
                    sp.dma_start(seen[64:64 + HI, 0:ET + 1, :], seen[0:HI, 0:ET + 1, :]).then_inc(s_twice, 16)
                    sp.wait_ge(s_twice, 16)

            with ExitStack() as c2:
                pL = [c2.enter_context(nc.psum_tensor(f"{tag}pL{i}", [P, 512], F32)) for i in range(2)]
                s_look = sem("s_looked_up")
                s_pick = sem("s_picked")
                s_base = sem("s_base")
                block = c2.enter_context(nc.Block())

                @block.tensor
                def _(pe):
                    def look(u, s, h):
                        after(pe, s_pick, u, 2)
                        pe.sem_inc(e.carry, 1)
                        ones_of = hotT[:, bass.ds(u * (LK // 2), LK // 2), :]
                        counts_of = seen[:, bass.ds(u * LK, LK), :]
                        for k in range(0, LK, 2):
                            m = pe.matmul(pL[s][:, k * LO:(k + 2) * LO], ones_of[:, k // 2, :],
                                          counts_of[:, k:k + 2, :].rearrange("p a b -> p (a b)"), start=True, stop=True)
                        m.then_inc(s_look, 1)
                    pipeline(pe, ET // LK, 2, [(0, look)])

                @block.vector
                def _(dve):
                    def pick(u, s, h):
                        after(dve, s_look, u)
                        after(dve, s_base, u, 2)
                        dve.tensor_tensor(prod[:, s, :, :], pL[s][:, 0:LK * LO].rearrange("p (a b) -> p a b", b=LO),
                                          hot[:, bass.ds(u * LK, LK), HI:HI + LO], ALU.mult).then_inc(s_pick, 1)

                    def add(u, s, h):
                        after(dve, s_pick, u)
                        dve.tensor_reduce(base[:, bass.ds(u * LK, LK)], prod[:, s, :, :], AX, ALU.add).then_inc(s_base, 1)
                    pipeline(dve, ET // LK, 2, [(0, pick), (1, add)])

        with ExitStack() as c1:
            pA = c1.enter_context(nc.psum_tensor(tag + "pA", [P, 512], F32))
            pB = c1.enter_context(nc.psum_tensor(tag + "pB", [P, 512], F32))
            s_pre = sem("s_pre")
            block = c1.enter_context(nc.Block())
            FOUND = e.steps_done + 4

            @block.tensor
            def _(pe):
                pe.wait_ge(e.steps, FOUND)
                pe.matmul(pA[:, 0:ET], e.earlier16[:, :], ov16[:, :], start=True, stop=True)
                pe.matmul(pB[:, 0:ET], e.ones16[:, :], ov16[:, :], start=True, stop=True).then_inc(s_pre, 1)

            @block.vector
            def _(dve):
                ch = Chain(dve, e)
                ch.done(dve.tensor_tensor(rank[:, :], rank[:, :], base[:, :], ALU.add))
                ch.done(dve.tensor_scalar(t1[:, :], rank[:, :], float(P), None, ALU.is_ge))
                ch.done(dve.scalar_tensor_tensor(t1[:, :], b[:, :], float(NB), t1[:, :], ALU.is_lt, ALU.mult))
                ch.done(dve.tensor_copy(ov16[:, :], t1[:, :]))
                assert ch.k == FOUND
                ch.done(dve.tensor_tensor(ovb16[:, :], t1[:, :], b[:, :], ALU.mult))
                dve.wait_ge(s_pre, 1)
                ch.done(dve.tensor_tensor_scan(t2[:, :], e.ones[:, 0:1].to_broadcast([P, ET]), pB[:, 0:ET], 0.0, ALU.mult, ALU.add))
                ch.done(dve.tensor_copy(e.over[:, e.over_at:e.over_at + 1], t2[:, ET - 1:ET]))
                ch.done(dve.tensor_tensor(t2[:, :], t2[:, :], pB[:, 0:ET], ALU.subtract))
                ch.done(dve.tensor_tensor(t2[:, :], t2[:, :], pA[:, 0:ET], ALU.add))
                ch.done(dve.tensor_tensor(t2[:, :], t2[:, :], rank[:, :], ALU.subtract))
                ch.done(dve.tensor_tensor(t2[:, :], t2[:, :], t1[:, :], ALU.mult))
                ch.done(dve.tensor_tensor(rank[:, :], rank[:, :], t2[:, :], ALU.add))
                ch.done(dve.tensor_scalar(t2[:, :], b[:, :], -1.0, float(OV), ALU.mult, ALU.add))
                ch.done(dve.tensor_tensor(t2[:, :], t2[:, :], t1[:, :], ALU.mult))
                ch.done(dve.tensor_tensor(b[:, :], b[:, :], t2[:, :], ALU.add))

        with ExitStack() as c1:
            W = NB + 1
            BY_ACT = {0: (0, 1), 1: (0, 1), 2: (0, 1)}
            hot_b = c1.enter_context(nc.sbuf_tensor(tag + "hot_b", [P, 4, CH, W + 1], F16))
            hot_s = c1.enter_context(nc.sbuf_tensor(tag + "hot_s", [P, 4, CH, 2, P], F16))
            slot = c1.enter_context(nc.sbuf_tensor(tag + "slot", [P, 4, len(BY_ACT), P], F16))
            low = c1.enter_context(nc.sbuf_tensor(tag + "low", [P, W + 1], F32))
            value = c1.enter_context(nc.sbuf_tensor(tag + "value", [P, W + 1], F32))
            pTab = [c1.enter_context(nc.psum_tensor(f"{tag}pTab{i}", [P, 512], F32)) for i in range(2)]
            pOv = [c1.enter_context(nc.psum_tensor(f"{tag}pOv{i}", [P, 512], F32)) for i in range(2)]
            s_hot = sem("s_hot")
            s_slot = sem("s_slot")
            s_scaled = sem("s_scaled")
            s_tab = sem("s_tab")
            s_low = sem("s_low")
            NC = ET // CH
            block = c1.enter_context(nc.Block())

            @block.vector
            def _(dve):
                def hots(u, s, h):
                    after(dve, s_tab, u, 4)
                    t = bass.ds(u * CH, CH)
                    b_of, rank_of, vals_of = b[:, t], rank[:, t], (val_hi[:, t], val_lo[:, t])
                    for k in BY_ACT:
                        m = dve.tensor_scalar(slot[:, s, k, :], e.iota16[:, 0:P], rank_of[:, k:k + 1], None, ALU.is_equal)
                    m.then_inc(s_slot, 1)
                    for k in range(CH):
                        m = dve.tensor_scalar(hot_b[:, s, k, 0:W + 1], e.iota16[:, 0:W + 1], b_of[:, k:k + 1], None, ALU.is_equal)
                        for part in range(2):
                            if part not in BY_ACT.get(k, ()):
                                m = dve.tensor_scalar(hot_s[:, s, k, part, :], e.iota16[:, 0:P], rank_of[:, k:k + 1], vals_of[part][:, k:k + 1],
                                                      ALU.is_equal, ALU.mult)
                    m.then_inc(s_hot, 1)
                pipeline(dve, NC, 4, [(0, hots)])
                ch = Chain(dve, e)
                dve.wait_ge(s_low, 2)
                ch.done(dve.scalar_tensor_tensor(value[:, 0:W], pTab[0][:, 0:W], 4096.0, low[:, 0:W], ALU.mult, ALU.add))
                ch.done(dve.scalar_tensor_tensor(value[:, W:W + 1], pOv[0][:, 0:1], 4096.0, low[:, W:W + 1], ALU.mult, ALU.add))
                cut_into_integers(dve, ch, e.oth[:, :], value[:, 0:W], P)
                ch.done(dve.scalar_tensor_tensor(e.lo[:, :], e.oth[:, :], -float(P), value[:, 0:W], ALU.mult, ALU.add))
                ch.done(dve.tensor_scalar(e.lo[:, :], e.lo[:, :], -1.0, None, ALU.add))
                q, j = low[:, 1:2], low[:, 2:3]
                ch.done(dve.tensor_scalar(q, value[:, OV:OV + 1], 1.0, None, ALU.max))
                ch.done(dve.reciprocal(q, q))
                ch.done(dve.tensor_tensor(q, q, value[:, W:W + 1], ALU.mult))
                ch.done(dve.tensor_scalar(e.ov_b[:, :], q, ROUND, -ROUND, ALU.add, ALU.add))
                cut_into_integers(dve, ch, q, e.ov_b[:, :], QUAD)
                ch.done(dve.scalar_tensor_tensor(j, q, -float(QUAD), e.ov_b[:, :], ALU.mult, ALU.add))
                ch.done(dve.scalar_tensor_tensor(j, q, float(QUAD * NPB), j, ALU.mult, ALU.add))
                ch.done(dve.scalar_tensor_tensor(e.ov_key[:, :], e.lo[:, OV:OV + 1], float(QUAD), j, ALU.mult, ALU.add))
                ch.done(dve.tensor_scalar(e.ov_row[:, :], e.quad_start[:, :], -1.0, e.ov_key[:, 0:1], ALU.mult, ALU.add))

            @block.tensor
            def _(pe):
                def table(u, s, h):
                    after(pe, s_hot, u)
                    after(pe, s_scaled, u)
                    pe.sem_inc(e.carry, 1)
                    beyond = ovb16[:, bass.ds(u * CH, CH)]
                    for k in range(CH):
                        first = isinstance(u, int) and u == 0 and k == 0
                        last = isinstance(u, int) and u == NC - 1 and k == CH - 1
                        for part in range(2):
                            pe.matmul(pTab[part][:, 0:W], hot_s[:, s, k, part, :], hot_b[:, s, k, 0:W], start=first, stop=last,
                                      skip_group_check=True)
                            m = pe.matmul(pOv[part][:, 0:1], hot_s[:, s, k, part, :], beyond[:, k:k + 1],
                                          start=first, stop=last, skip_group_check=True)
                    m.then_inc(s_tab, 1)
                pipeline(pe, NC, 4, [(0, table)])

            @block.scalar
            def _(act):
                def scaled(u, s, h):
                    after(act, s_slot, u)
                    after(act, s_tab, u, 4)
                    t = bass.ds(u * CH, CH)
                    vals_of = val_hi[:, t], val_lo[:, t]
                    for k, parts in BY_ACT.items():
                        for part in parts:
                            m = act.activation(hot_s[:, s, k, part, :], slot[:, s, k, :], ACT.Copy, scale=vals_of[part][:, k:k + 1])
                    m.then_inc(s_scaled, 1)
                pipeline(act, NC, 4, [(0, scaled)])
                act.wait_ge(s_tab, NC)
                act.activation(low[:, 0:W], pTab[1][:, 0:W], ACT.Copy).then_inc(s_low, 1)
                act.activation(low[:, W:W + 1], pOv[1][:, 0:1], ACT.Copy).then_inc(s_low, 1)


def degrees(nc, e, by_dst):
    NB, NPB, NQ = e.NB, e.NPB, e.NQ
    with ExitStack() as c:
        def sb(name, shape, dt=F32):
            return c.enter_context(nc.sbuf_tensor("deg_" + name, shape, dt))

        def sem(name):
            return c.enter_context(nc.semaphore("deg_" + name))

        QN = QUAD * NPB
        hot = sb("hot", [P, 4, QUAD, NPB], F16)
        band = sb("band", [P, 2 * NQ], F16)
        inside = sb("inside", [P, NQ])
        ov_quad = sb("ov_quad", [P, NQ], F16)
        ov_in = sb("ov_in", [P, NQ])
        ov_at = sb("ov_at", [P, 1])
        ov_hot = sb("ov_hot", [P, QN], F16)
        log = sb("log", [NQ, QN])
        rows = sb("rows", [NQ, QN])
        pD = c.enter_context(nc.psum_tensor("deg_pD", [P, 512], F32))
        pR = c.enter_context(nc.psum_tensor("deg_pR", [P, 512], F32))
        done = e.steps_done
        s_hot = sem("s_hot")
        s_cnt = sem("s_counted")
        s_log = sem("s_log")
        s_turn = sem("s_turned")
        s_out = sem("s_out")
        block = c.enter_context(nc.Block())

        @block.vector
        def _(dve):
            ch = Chain(dve, e)
            ch.done(dve.memset(band[:, :], 0.0))
            ch.done(dve.memset(band[:, NQ:NQ + 1], 1.0))
            ch.done(dve.tensor_scalar(inside[:, :], by_dst.ov_row[:, :], float(QN), None, ALU.is_lt))
            ch.done(dve.scalar_tensor_tensor(inside[:, :], by_dst.ov_row[:, :], 0.0, inside[:, :], ALU.is_ge, ALU.mult))
            ch.done(dve.tensor_copy(ov_quad[:, :], inside[:, :]))
            ch.done(dve.tensor_tensor(ov_in[:, :], inside[:, :], by_dst.ov_row[:, :], ALU.mult))
            ch.done(dve.tensor_reduce(ov_at[:, :], ov_in[:, :], AX, ALU.add))
            ch.done(dve.tensor_scalar(ov_hot[:, :], e.quad_rows[:, :, :].rearrange("p j n -> p (j n)"), ov_at[:, 0:1], None, ALU.is_equal))
            assert ch.k == done + 8

            def hots(u, s, h):
                after(dve, s_cnt, u, 4)
                dve.tensor_tensor(hot[:, s, :, :], e.iota16[:, 0:NPB].unsqueeze(1).to_broadcast([P, QUAD, NPB]),
                                  by_dst.lo[:, bass.ds(u * QUAD, QUAD)].unsqueeze(2).to_broadcast([P, QUAD, NPB]), ALU.is_equal)\
                   .then_inc(s_hot, 1)
            pipeline(dve, NQ, 4, [(0, hots)])

        @block.tensor
        def _(pe):
            pe.wait_ge(e.steps, done + 8)
            pe.matmul(pD[0:NQ, 0:QN], ov_quad[:, :], ov_hot[:, :], start=True, stop=False, skip_group_check=True)

            def count(u, s, h):
                after(pe, s_hot, u)
                pe.sem_inc(e.carry, 1)
                pe.matmul(pD[0:NQ, 0:QN], band[:, bass.ds(NQ - u, NQ)], hot[:, s, :, :].rearrange("p j n -> p (j n)"), start=False,
                          stop=isinstance(u, int) and u == NQ - 1, skip_group_check=True).then_inc(s_cnt, 1)
            pipeline(pe, NQ, 4, [(0, count)])
            pe.wait_ge(s_log, 2)
            for j in range(QUAD):
                m = pe.transpose(pR[0:NPB, j * NQ:(j + 1) * NQ], rows[:, j * NPB:(j + 1) * NPB], e.ident[0:NQ, 0:NQ])
            m.then_inc(s_turn, 1)

        @block.scalar
        def _(act):
            act.preload_act_table_set(ACT_SET)
            act.wait_ge(s_cnt, NQ)
            act.activation(log[:, :], pD[0:NQ, 0:QN], ACT.Ln, bias=e.ones[0:NQ, 0:1]).then_inc(s_log, 1)
            act.wait_ge(s_log, 1)
            act.activation(rows[:, :], log[:, :], ACT.Exp, scale=-0.5).then_inc(s_log, 1)
            act.wait_ge(s_log, 2)
            act.dma_start(e.dinv_rows.rearrange("(q j) p -> q (j p)", j=QUAD), rows[:, :]).then_inc(s_out, 16)
            act.wait_ge(s_turn, 1)
            act.activation(e.dinv_b[:, :].rearrange("p (q j) -> p j q", j=QUAD), pR[0:NPB, 0:NB].rearrange("p (j q) -> p j q", j=QUAD),
                           ACT.Copy).then_inc(s_log, 1)
            act.wait_ge(s_log, 3)
            act.wait_ge(s_out, 16)


def attention(nc, e, by_src):
    N, D, H, DH, A, R1 = e.N, e.D, e.H, e.DH, e.A, e.R1
    NB, NPB, NQ = e.NB, e.NPB, e.NQ
    QN = QUAD * NPB
    LASTP = (N - (NQ - 1) * QN) // QUAD
    with ExitStack() as c:
        def sb(name, shape, dt=F32):
            return c.enter_context(nc.sbuf_tensor("a_" + name, shape, dt))

        def sem(name):
            h = c.enter_context(nc.semaphore("a_" + name))
            e.spare.append(h.num)
            return h

        bank = [c.enter_context(nc.psum_tensor(f"a_bank{i}", [P, 512], F32)) for i in range(8)]
        pHot, pDst, pSrc, pQ, pK, pAcc = bank[:6]
        pV = bank[6:8]
        ov_con = sb("ov_con", [P, A])

        with ExitStack() as c1:
            idx = c1.enter_context(nc.sbuf_tensor("ao_idx", [P, 2], I32))
            rows = c1.enter_context(nc.sbuf_tensor("ao_rows", [P, 2, D], F32))
            rowsT = c1.enter_context(nc.sbuf_tensor("ao_rowsT", [D, 2, P], F32))
            q_sb = c1.enter_context(nc.sbuf_tensor("ao_q", [P, D], F32))
            prod = c1.enter_context(nc.sbuf_tensor("ao_prod", [P, D], F32))
            score = c1.enter_context(nc.sbuf_tensor("ao_score", [P, H], F32))
            done = e.steps_done
            so_rows = sem("so_rows")
            so_T = sem("so_T")
            so_Tc = sem("so_Tc")
            so_qkv = sem("so_qkv")
            so_q = sem("so_q")
            so_e = sem("so_e")
            block = c1.enter_context(nc.Block())

            @block.vector
            def _(dve):
                with dve.If(e.fast(dve)):
                    ch = Chain(dve, e)
                    ch.done(dve.tensor_scalar(idx[:, 0:1], by_src.ov_key[:, :], 0.0, None, ALU.max))
                    ch.done(dve.tensor_copy(idx[:, 1:2], by_src.oth[:, NB:NB + 1]))
                    dve.wait_ge(so_q, 1)
                    dve.wait_ge(so_qkv, 1)
                    ch.done(dve.tensor_tensor(prod[:, :], q_sb[:, :], pK[:, 0:D], ALU.mult))
                    ch.done(dve.tensor_reduce(score[:, :], prod[:, :].rearrange("p (h d) -> p h d", h=H), AX, ALU.add))
                    ch.done(dve.tensor_scalar(score[:, :], score[:, :], LIMIT, -LIMIT, ALU.min, ALU.max))
                    dve.wait_ge(so_e, 1)
                    ch.done(dve.tensor_tensor(ov_con[:, 0:D].rearrange("p (h d) -> p h d", h=H),
                                              pV[0][:, 0:D].rearrange("p (h d) -> p h d", h=H),
                                              ov_con[:, D:A].unsqueeze(2).to_broadcast([P, H, DH]), ALU.mult))

            @block.gpsimd
            def _(pool):
                with pool.If(e.fast(pool)):
                    pool.wait_ge(e.steps, done + 2)
                    for k in range(2):
                        pool.indirect_dma_start(rows[:, k, :], None, e.x[:, :],
                                                bass.IndirectOffsetOnAxis(ap=idx[:, k:k + 1], axis=0)).then_inc(so_rows, 16)
                    pool.wait_ge(so_rows, 32)

            @block.tensor
            def _(pe):
                with pe.If(e.fast(pe)):
                    pe.wait_ge(so_rows, 32)
                    pe.transpose(pHot[0:D, 0:P], rows[:, 0, :], e.ident[:, :])
                    pe.transpose(pHot[0:D, P:2 * P], rows[:, 1, :], e.ident[:, :]).then_inc(so_T, 1)
                    pe.wait_ge(so_Tc, 1)
                    pe.matmul(pQ[:, 0:D], rowsT[:, 0, :], e.q_w[:, :], start=True, stop=True)
                    pe.matmul(pK[:, 0:D], rowsT[:, 1, :], e.kv_w[:, 0:D], start=True, stop=True)
                    pe.matmul(pV[0][:, 0:D], rowsT[:, 1, :], e.kv_w[:, D:2 * D], start=True, stop=True).then_inc(so_qkv, 1)

            @block.scalar
            def _(act):
                with act.If(e.fast(act)):
                    act.preload_act_table_set(ACT_SET)
                    act.wait_ge(so_T, 1)
                    act.activation(rowsT[:, :, :], pHot[0:D, 0:2 * P].rearrange("p (a b) -> p a b", a=2), ACT.Copy).then_inc(so_Tc, 1)
                    act.wait_ge(so_qkv, 1)
                    act.activation(q_sb[:, :], pQ[:, 0:D], ACT.Copy).then_inc(so_q, 1)
                    act.wait_ge(e.steps, done + 5)
                    act.activation(ov_con[:, D:A], score[:, :], ACT.Exp).then_inc(so_e, 1)

        RING = 6
        idx = [sb(f"idx{i}", [P, QUAD], I32) for i in range(RING)]
        dst_rows = [sb(f"dst_rows{i}", [P, QUAD, D]) for i in range(RING)]
        own = [sb(f"own{i}", [NPB, QUAD, D]) for i in range(RING)]
        hot = [sb(f"hot{i}", [P, QUAD, NPB]) for i in range(RING)]
        hot_ov = [sb(f"hot_ov{i}", [P, QUAD, NPB]) for i in range(RING)]
        hotT = sb("hotT", [NPB, QUAD, P])
        dstT = sb("dstT", [D, QUAD, P])
        srcT = sb("srcT", [D, QUAD, P])
        q_sb = sb("q_sb", [P, QUAD, D])
        prod = sb("prod", [P, QUAD, D])
        score = sb("score", [P, QUAD * H])
        con = [sb(f"con{i}", [P, QUAD, A]) for i in range(3)]
        rec = sb("rec", [NPB, QUAD, H])
        hid = [sb(f"hid{i}", [NPB, QUAD, D]) for i in range(3)]
        shift = [sb(f"shift{i}", [NPB, QUAD]) for i in range(2)]
        stats = sb("stats", [NPB, QUAD, 6])
        mv = [sb(f"mv{i}", [NPB, QUAD, 2]) for i in range(2)]
        lnv = sb("lnv", [NPB, QUAD])
        rstd = [sb(f"rstd{i}", [NPB, QUAD]) for i in range(2)]
        x1r = [sb(f"x1r{i}", [NPB, QUAD, R1]) for i in range(RING)]

        d_rows = [sem(f"d_rows{i}") for i in range(RING)]
        d_own = [sem(f"d_own{i}") for i in range(RING)]
        d_out = [sem(f"d_out{i}") for i in range(RING)]
        (s_idx, s_hot, s_hov, s_hotT, s_dstT, s_hotTc, s_dstTc, s_srcT, s_srcTc, s_q, s_qc, s_kv, s_prod, s_sc, s_clip, s_exp,
         s_con, s_acc, s_den, s_rec, s_num, s_hid, s_st, s_mv, s_lnv, s_rstd, s_x1, s_shift, s_dcol, s_const) = [
            sem("s_" + n) for n in ("idx hot hov hotT dstT hotTc dstTc srcT srcTc q qc kv prod sc clip exp con acc den rec num "
                                    "hid st mv lnv rstd x1 shift dcol const").split()]
        block = c.enter_context(nc.Block())

        def rows_of(t, u, n):
            return t[bass.ds(u * QN, QUAD * n), :].rearrange("(p j) d -> p j d", j=QUAD)

        def parts(u):
            return LASTP if isinstance(u, int) and u == NQ - 1 else NPB

        @block.sync
        def _(sp):
            def load(u, s, h):
                after(sp, s_hid, u, RING)
                n = parts(u)
                sp.dma_start(own[s][0:n, :, :], rows_of(e.x, u, n)).then_inc(d_own[s], 16)

            def store(u, s, h):
                after(sp, s_x1, u)
                after(sp, s_dcol, u)
                n = parts(u)
                sp.dma_start(rows_of(e.x1_rows, u, n), x1r[s][0:n, :, :]).then_inc(d_out[s], 16)
            with sp.If(e.fast(sp)):
                sp.wait_ge(s_const, 3 * RING)
                pipeline(sp, NQ, RING, [(1, load), (9, store)], 3)
                for s in range(RING):
                    sp.wait_ge(d_out[s], 16 * len(range(s, NQ, RING)))

        @block.gpsimd
        def _(pool):
            def gather(u, s, h):
                after(pool, s_dstT, u, RING)
                after(pool, s_idx, u)
                pool.sem_inc(e.carry, 1)
                for j in range(QUAD):
                    pool.indirect_dma_start(dst_rows[s][:, j, :], None, e.x[:, :],
                                            bass.IndirectOffsetOnAxis(ap=idx[s][:, j:j + 1], axis=0)).then_inc(d_rows[s], 16)
            with pool.If(e.fast(pool)):
                pipeline(pool, NQ, RING, [(0, gather)], 3)

        @block.scalar
        def _(act):
            def index(u, s, h):
                landed(act, d_rows, s, h, 16 * QUAD, 1)
                act.activation(idx[s][:, :], by_src.oth[:, bass.ds(u * QUAD, QUAD)], ACT.Copy).then_inc(s_idx, 1)

            def turned(u, s, h):
                after(act, s_hotT, u)
                after(act, s_srcT, u, 1)
                act.activation(hotT[:, :, :], pHot[0:NPB, :].rearrange("p (a b) -> p a b", a=QUAD), ACT.Copy).then_inc(s_hotTc, 1)

            def exps(u, s, h):
                after(act, s_clip, u)
                after(act, s_acc, u, 3)
                act.activation(con[s % 3][:, :, D:A], score[:, :].rearrange("p (j h) -> p j h", j=QUAD), ACT.Exp).then_inc(s_exp, 1)

            def turned2(u, s, h):
                after(act, s_dstT, u)
                after(act, s_kv, u, 1)
                act.activation(dstT[:, :, :], pDst[0:D, :].rearrange("p (a b) -> p a b", a=QUAD), ACT.Copy).then_inc(s_dstTc, 1)

            def turned3(u, s, h):
                after(act, s_srcT, u)
                after(act, s_q, u, 1)
                act.activation(srcT[:, :, :], pSrc[0:D, :].rearrange("p (a b) -> p a b", a=QUAD), ACT.Copy).then_inc(s_srcTc, 1)

            def queries(u, s, h):
                after(act, s_q, u)
                after(act, s_prod, u, 1)
                act.activation(q_sb[:, :, :], pQ[:, 0:QUAD * D].rearrange("p (a b) -> p a b", a=QUAD), ACT.Copy).then_inc(s_qc, 1)

            def rstd_(u, s, h):
                after(act, s_mv, u)
                after(act, s_rstd, u, 1)
                act.activation(lnv[:, :], mv[s % 2][:, :, 1], ACT.Ln, bias=e.eps[0:NPB, 0:1]).then_inc(s_lnv, 1)
                landed(act, d_out, s, h, 16, 1)
                act.activation(x1r[s][:, :, D], e.dinv_b[:, bass.ds(u * QUAD, QUAD)], ACT.Copy).then_inc(s_dcol, 1)
                after(act, s_lnv, u)
                after(act, s_x1, u, 2)
                act.activation(rstd[s % 2][:, :], lnv[:, :], ACT.Exp, scale=-0.5).then_inc(s_rstd, 1)
            def norm(u, s, h):
                after(act, s_shift, u)
                landed(act, d_out, s, h, 16, 1)
                for j in range(QUAD):
                    m = act.activation(x1r[s][:, j, 0:D], hid[s % 3][:, j, :], ACT.Identity, bias=shift[s % 2][:, j:j + 1],
                                       scale=rstd[s % 2][:, j:j + 1])
                m.then_inc(s_x1, 1)
            with act.If(e.fast(act)):
                act.wait_ge(s_const, 3 * RING)
                act.preload_act_table_set(ACT_SET)
                pipeline(act, NQ, RING, [(0, index), (8, rstd_), (3, turned3), (2, turned), (2, turned2), (4, exps), (3, queries), (9, norm)], 3)

        @block.vector
        def _(dve):
            def select(u, s, h):
                after(dve, s_acc, u, RING)
                dve.tensor_tensor(hot[s][:, :, :], e.iota[:, 0:NPB].unsqueeze(1).to_broadcast([P, QUAD, NPB]),
                                  by_src.lo[:, bass.ds(u * QUAD, QUAD)].unsqueeze(2).to_broadcast([P, QUAD, NPB]), ALU.is_equal).then_inc(s_hot, 1)

            def beyond(u, s, h):
                after(dve, s_acc, u, RING)
                dve.tensor_scalar(hot_ov[s][:, :, :], e.quad_rows[:, :, :], by_src.ov_row[:, bass.ds(u, 1)], None,
                                  ALU.is_equal).then_inc(s_hov, 1)

            def product(u, s, h):
                after(dve, s_qc, u)
                after(dve, s_kv, u)
                after(dve, s_sc, u, 1)
                dve.tensor_tensor(prod[:, :, :], q_sb[:, :, :], pK[:, 0:QUAD * D].rearrange("p (j d) -> p j d", j=QUAD), ALU.mult).then_inc(s_prod, 1)

            def sums(u, s, h):
                after(dve, s_acc, u)
                after(dve, s_num, u, 1)
                acc = pAcc[0:NPB, 0:QUAD * A].rearrange("p (j a) -> p j a", j=QUAD)
                dve.tensor_scalar(rec[:, :, :], acc[:, :, D:A], EPS_NORM, None, ALU.add).then_inc(s_den, 1)

            def score_(u, s, h):
                after(dve, s_prod, u)
                after(dve, s_exp, u, 1)
                dve.tensor_reduce(score[:, :], prod[:, :, :].rearrange("p j (h d) -> p (j h) d", h=H), AX, ALU.add).then_inc(s_sc, 1)

            def recip(u, s, h):
                after(dve, s_den, u)
                dve.reciprocal(rec[:, :, :], rec[:, :, :]).then_inc(s_rec, 1)

            def clip(u, s, h):
                after(dve, s_sc, u)
                dve.tensor_scalar(score[:, :], score[:, :], LIMIT, -LIMIT, ALU.min, ALU.max).then_inc(s_clip, 1)

            def norms(u, s, h):
                after(dve, s_rec, u)
                after(dve, s_x1, u, 3)
                acc = pAcc[0:NPB, 0:QUAD * A].rearrange("p (j a) -> p j a", j=QUAD)
                dve.tensor_tensor(hid[s % 3][:, :, :].rearrange("p j (h d) -> p j h d", h=H),
                                  acc[:, :, 0:D].rearrange("p j (h d) -> p j h d", h=H),
                                  rec[:, :, :].unsqueeze(3).to_broadcast([NPB, QUAD, H, DH]), ALU.mult).then_inc(s_num, 1)

            def contribute(u, s, h):
                after(dve, s_exp, u)
                dve.tensor_tensor(con[s % 3][:, :, 0:D].rearrange("p j (h d) -> p j h d", h=H),
                                  pV[s % 2][:, 0:QUAD * D].rearrange("p (j h d) -> p j h d", j=QUAD, h=H),
                                  con[s % 3][:, :, D:A].unsqueeze(3).to_broadcast([P, QUAD, H, DH]), ALU.mult).then_inc(s_con, 1)

            def hidden(u, s, h):
                after(dve, s_num, u)
                landed(dve, d_own, s, h, 16)
                dve.scalar_tensor_tensor(hid[s % 3][:, :, :], own[s][:, :, :], 2.0, hid[s % 3][:, :, :], ALU.mult, ALU.add).then_inc(s_hid, 1)

            def shifts(u, s, h):
                after(dve, s_rstd, u)
                after(dve, s_x1, u, 2)
                dve.scalar_tensor_tensor(shift[s % 2][:, :], mv[s % 2][:, :, 0], -1.0, rstd[s % 2][:, :], ALU.mult, ALU.mult).then_inc(s_shift, 1)

            def stat(u, s, h):
                after(dve, s_hid, u)
                after(dve, s_mv, u, 1)
                for j in range(QUAD):
                    m = dve.bn_stats(stats[:, j, :], hid[s % 3][:, j, :])
                m.then_inc(s_st, 1)

            def aggregate(u, s, h):
                after(dve, s_st, u)
                after(dve, s_shift, u, 2)
                dve.sem_inc(e.carry, 1)
                for j in range(QUAD):
                    m = dve.bn_aggr(mv[s % 2][:, j, :], stats[:, j, :])
                m.then_inc(s_mv, 1)
            with dve.If(e.fast(dve)):
                for s in range(RING):
                    dve.memset(own[s][:, :, :], 0.0).then_inc(s_const, 1)
                    dve.memset(x1r[s][:, :, D + 1:D + 3], 1.0).then_inc(s_const, 1)
                    dve.memset(x1r[s][:, :, D + 3:R1], 0.0).then_inc(s_const, 1)
                pipeline(dve, NQ, RING, [(5, contribute), (4, product), (7, sums), (4, score_), (7, recip), (4, clip), (7, norms), (1, select),
                                         (7, hidden), (8, shifts), (7, stat), (1, beyond), (7, aggregate)], 3)

        @block.tensor
        def _(pe):
            def turn(u, s, h):
                after(pe, s_hot, u)
                after(pe, s_hotTc, u, 1)
                pe.sem_inc(e.carry, 1)
                for j in range(QUAD):
                    m = pe.transpose(pHot[0:NPB, j * P:(j + 1) * P], hot[s][:, j, :], e.ident[:, :])
                m.then_inc(s_hotT, 1)
                landed(pe, d_rows, s, h, 16 * QUAD)
                after(pe, s_dstTc, u, 1)
                pe.sem_inc(e.carry, 1)
                for j in range(QUAD):
                    m = pe.transpose(pDst[0:D, j * P:(j + 1) * P], dst_rows[s][:, j, :], e.ident[:, :])
                m.then_inc(s_dstT, 1)

            def source(u, s, h):
                after(pe, s_hotTc, u)
                after(pe, s_srcTc, u, 1)
                landed(pe, d_own, s, h, 16)
                pe.sem_inc(e.carry, 1)
                for j in range(QUAD):
                    m = pe.matmul(pSrc[0:D, j * P:(j + 1) * P], own[s][:, j, :], hotT[:, j, :], start=True, stop=True)
                m.then_inc(s_srcT, 1)

            def keys(u, s, h):
                after(pe, s_dstTc, u)
                after(pe, s_prod, u, 1)
                after(pe, s_con, u, 2)
                pe.sem_inc(e.carry, 1)
                for j in range(QUAD):
                    pe.matmul(pK[:, j * D:(j + 1) * D], dstT[:, j, :], e.kv_w[:, 0:D], start=True, stop=True)
                    m = pe.matmul(pV[s % 2][:, j * D:(j + 1) * D], dstT[:, j, :], e.kv_w[:, D:2 * D], start=True, stop=True)
                m.then_inc(s_kv, 1)

            def query(u, s, h):
                after(pe, s_srcTc, u)
                after(pe, s_qc, u, 1)
                pe.sem_inc(e.carry, 1)
                for j in range(QUAD):
                    m = pe.matmul(pQ[:, j * D:(j + 1) * D], srcT[:, j, :], e.q_w[:, :], start=True, stop=True)
                m.then_inc(s_q, 1)

            def gather_sums(u, s, h):
                after(pe, s_con, u)
                after(pe, s_hov, u)
                after(pe, s_num, u, 1)
                pe.sem_inc(e.carry, 1)
                for j in range(QUAD):
                    pe.matmul(pAcc[0:NPB, j * A:(j + 1) * A], hot_ov[s][:, j, :], ov_con[:, :], start=True, stop=False)
                    m = pe.matmul(pAcc[0:NPB, j * A:(j + 1) * A], hot[s][:, j, :], con[s % 3][:, j, :], start=False, stop=True)
                m.then_inc(s_acc, 1)
            with pe.If(e.fast(pe)):
                pe.wait_ge(s_const, 3 * RING)
                pipeline(pe, NQ, RING, [(3, source), (3, keys), (2, turn), (3, query), (6, gather_sums)], 3)


def convolution(nc, e, by_dst):
    N, D, R1 = e.N, e.D, e.R1
    NB, NPB, NQ = e.NB, e.NPB, e.NQ
    QN = QUAD * NPB
    LASTP = (N - (NQ - 1) * QN) // QUAD
    with ExitStack() as c:
        def sb(name, shape, dt=F32):
            return c.enter_context(nc.sbuf_tensor("c_" + name, shape, dt))

        def sem(name):
            h = c.enter_context(nc.semaphore("c_" + name))
            e.spare.append(h.num)
            return h

        bank = [c.enter_context(nc.psum_tensor(f"c_bank{i}", [P, 512], F32)) for i in range(6)]
        pOwn, pSum, pY = bank[0], bank[1:3], bank[3:6]
        RING = 6
        ov_idx = sb("ov_idx", [P, 1], I32)
        ov_rows = sb("ov_rows", [P, R1])
        idx = [sb(f"idx{i}", [P, QUAD], I32) for i in range(RING)]
        rows = [sb(f"rows{i}", [P, QUAD, R1]) for i in range(RING)]
        own = [sb(f"own{i}", [NPB, QUAD, R1]) for i in range(RING)]
        dinvr = [sb(f"dinvr{i}", [D, QN]) for i in range(RING)]
        hot = [sb(f"hot{i}", [P, QUAD, NPB]) for i in range(2)]
        hot_ov = [sb(f"hot_ov{i}", [P, QUAD, NPB]) for i in range(2)]
        own_s = [sb(f"own_s{i}", [NPB, QUAD, D]) for i in range(2)]
        ownT = [sb(f"ownT{i}", [R1, QN]) for i in range(3)]
        sumT = [sb(f"sumT{i}", [D, QN]) for i in range(2)]
        cap = sb("cap", [NPB, QUAD * D])
        u_ = [sb(f"u{i}", [NPB, QUAD * D]) for i in range(2)]
        n_ = [sb(f"n{i}", [NPB, QUAD * D]) for i in range(2)]
        r_ = [sb(f"r{i}", [NPB, QUAD * D]) for i in range(2)]
        lg = sb("lg", [NPB, QUAD * D])
        hid = [sb(f"hid{i}", [NPB, QUAD, D]) for i in range(3)]
        shift = [sb(f"shift{i}", [NPB, 2]) for i in range(2)]
        stats = sb("stats", [NPB, QUAD, 6])
        mv = [sb(f"mv{i}", [NPB, QUAD, 2]) for i in range(2)]
        lnv = sb("lnv", [NPB, QUAD])
        rstd = [sb(f"rstd{i}", [NPB, QUAD]) for i in range(2)]
        res = [sb(f"res{i}", [NPB, QUAD, D]) for i in range(RING)]

        d_ov = sem("d_ov")
        d_rows = [sem(f"d_rows{i}") for i in range(RING)]
        d_own = [sem(f"d_own{i}") for i in range(RING)]
        d_out = [sem(f"d_out{i}") for i in range(RING)]
        (s_ovi, s_idx, s_hot, s_hov, s_own_s, s_ownT, s_ownTc, s_sum, s_sumc, s_y, s_cap, s_u, s_n, s_lg, s_r, s_t, s_ty, s_hid,
         s_st, s_mv, s_lnv, s_rstd, s_res, s_res_a, s_shift, s_const) = [
            sem("s_" + n) for n in ("ovi idx hot hov own_s ownT ownTc sum sumc y cap u n lg r t ty hid st mv lnv rstd res res_a shift "
                                    "const").split()]
        block = c.enter_context(nc.Block())

        def rows_of(t, u, n):
            return t[bass.ds(u * QN, QUAD * n), :].rearrange("(p j) d -> p j d", j=QUAD)

        def parts(u):
            return LASTP if isinstance(u, int) and u == NQ - 1 else NPB

        @block.sync
        def _(sp):
            def load(u, s, h):
                after(sp, s_hid, u, RING)
                n = parts(u)
                sp.dma_start(own[s][0:n, :, :], rows_of(e.x1_rows, u, n)).then_inc(d_own[s], 16)
                sp.dma_start(dinvr[s][:, :], e.dinv_rows.rearrange("(q j) p -> q (j p)", j=QUAD)[bass.ds(u, 1), :].to_broadcast([D, QN]))\
                  .then_inc(d_own[s], 16)

            def store(u, s, h):
                after(sp, s_res, u)
                after(sp, s_res_a, u)
                n = parts(u)
                sp.dma_start(rows_of(e.out, u, n), res[s][0:n, :, :]).then_inc(d_out[s], 16)
            with sp.If(e.fast(sp)):
                sp.wait_ge(s_const, RING)
                pipeline(sp, NQ, RING, [(1, load), (8, store)], 3)
                for s in range(RING):
                    sp.wait_ge(d_out[s], 16 * len(range(s, NQ, RING)))

        @block.gpsimd
        def _(pool):
            def gather(u, s, h):
                after(pool, s_sum, u, RING)
                after(pool, s_idx, u)
                pool.sem_inc(e.carry, 1)
                for j in range(QUAD):
                    pool.indirect_dma_start(rows[s][:, j, :], None, e.x1_rows[:, :],
                                            bass.IndirectOffsetOnAxis(ap=idx[s][:, j:j + 1], axis=0)).then_inc(d_rows[s], 16)
            with pool.If(e.fast(pool)):
                pool.wait_ge(s_ovi, 1)
                pool.indirect_dma_start(ov_rows[:, :], None, e.x1_rows[:, :],
                                        bass.IndirectOffsetOnAxis(ap=ov_idx[:, 0:1], axis=0)).then_inc(d_ov, 16)
                pipeline(pool, NQ, RING, [(0, gather)], 3)

        @block.scalar
        def _(act):
            def index(u, s, h):
                landed(act, d_rows, s, h, 16 * QUAD, 1)
                act.activation(idx[s][:, :], by_dst.oth[:, bass.ds(u * QUAD, QUAD)], ACT.Copy).then_inc(s_idx, 1)

            def logs(u, s, h):
                after(act, s_n, u)
                after(act, s_r, u, 1)
                act.activation(lg[:, :], n_[s % 2][:, :], ACT.Ln, bias=e.two[0:NPB, 0:1]).then_inc(s_lg, 1)

            def scale_own(u, s, h):
                landed(act, d_own, s, h, 32)
                after(act, s_sum, u, 2)
                for j in range(QUAD):
                    m = act.activation(own_s[s % 2][:, j, :], own[s][:, j, 0:D], ACT.Copy, scale=own[s][:, j, D:D + 1])
                m.then_inc(s_own_s, 1)

            def recips(u, s, h):
                after(act, s_lg, u)
                after(act, s_t, u, 2)
                act.activation(r_[s % 2][:, :], lg[:, :], ACT.Exp, scale=-1.0).then_inc(s_r, 1)

            def turned(u, s, h):
                after(act, s_ownT, u)
                after(act, s_y, u, 3)
                act.activation(ownT[s % 3][:, :], pOwn[0:R1, 0:QN], ACT.Copy).then_inc(s_ownTc, 1)

            def capped(u, s, h):
                after(act, s_y, u)
                after(act, s_u, u, 1)
                act.activation(cap[:, :], pY[s % 3][0:NPB, 0:QUAD * D], ACT.Relu, bias=e.twenty[0:NPB, 0:1], scale=-1.0).then_inc(s_cap, 1)

            def exps(u, s, h):
                after(act, s_cap, u)
                after(act, s_n, u, 2)
                act.activation(u_[s % 2][:, :], cap[:, :], ACT.Exp, bias=e.twenty[0:NPB, 0:1], scale=-1.0).then_inc(s_u, 1)

            def variance(u, s, h):
                after(act, s_mv, u)
                after(act, s_rstd, u, 1)
                act.activation(lnv[:, :], mv[s % 2][:, :, 1], ACT.Ln, bias=e.eps[0:NPB, 0:1]).then_inc(s_lnv, 1)

            def rstd_(u, s, h):
                after(act, s_lnv, u)
                after(act, s_res, u, 2)
                after(act, s_res_a, u, 2)
                act.activation(rstd[s % 2][:, :], lnv[:, :], ACT.Exp, scale=-0.5).then_inc(s_rstd, 1)
            def norm(u, s, h):
                after(act, s_shift, u)
                landed(act, d_out, s, h, 16, 1)
                for j in range(2):
                    m = act.activation(res[s][:, j, :], hid[s % 3][:, j, :], ACT.Identity, bias=shift[s % 2][:, j:j + 1],
                                       scale=rstd[s % 2][:, j:j + 1])
                m.then_inc(s_res_a, 1)
            with act.If(e.fast(act)):
                act.wait_ge(s_const, RING)
                act.preload_act_table_set(ACT_SET)
                pipeline(act, NQ, RING, [(7, variance), (0, index), (7, rstd_), (2, scale_own), (5, logs), (4, capped), (2, turned), (5, recips),
                                         (4, exps), (8, norm)], 3)

        @block.vector
        def _(dve):
            def poly(u, s, h):
                after(dve, s_u, u)
                after(dve, s_ty, u, 2)
                dve.scalar_tensor_tensor(n_[s % 2][:, :], u_[s % 2][:, :], 2.0, u_[s % 2][:, :], ALU.add, ALU.mult).then_inc(s_n, 1)

            def select(u, s, h):
                landed(dve, d_rows, s, h, 16 * QUAD)
                after(dve, s_sum, u, 2)
                rows_in = by_dst.lo[:, bass.ds(u * QUAD, QUAD)]
                for j in range(QUAD):
                    m = dve.tensor_scalar(hot[s % 2][:, j, :], e.iota[:, 0:NPB], rows_in[:, j:j + 1],
                                          rows[s][:, j, D:D + 1], ALU.is_equal, ALU.mult)
                m.then_inc(s_hot, 1)

            def beyond(u, s, h):
                after(dve, s_sum, u, 2)
                dve.tensor_scalar(hot_ov[s % 2][:, :, :], e.quad_rows[:, :, :], by_dst.ov_row[:, bass.ds(u, 1)], ov_rows[:, D:D + 1],
                                  ALU.is_equal, ALU.mult).then_inc(s_hov, 1)

            def scaled(u, s, h):
                after(dve, s_sum, u)
                after(dve, s_y, u, 2)
                dve.tensor_tensor(sumT[s % 2][:, :], pSum[s % 2][0:D, 0:QN], dinvr[s][:, :], ALU.mult).then_inc(s_sumc, 1)

            def ratio(u, s, h):
                after(dve, s_r, u)
                dve.tensor_tensor(n_[s % 2][:, :], n_[s % 2][:, :], r_[s % 2][:, :], ALU.mult).then_inc(s_t, 1)

            def mish(u, s, h):
                after(dve, s_t, u)
                after(dve, s_res, u, 3)
                after(dve, s_res_a, u, 3)
                dve.tensor_tensor(hid[s % 3][:, :, :].rearrange("p j d -> p (j d)"), n_[s % 2][:, :], pY[s % 3][0:NPB, 0:QUAD * D], ALU.mult)\
                   .then_inc(s_ty, 1)

            def hidden(u, s, h):
                after(dve, s_ty, u)
                dve.tensor_tensor(hid[s % 3][:, :, :], hid[s % 3][:, :, :], own[s][:, :, 0:D], ALU.add).then_inc(s_hid, 1)

            def norm(u, s, h):
                after(dve, s_rstd, u)
                after(dve, s_res_a, u, 2)
                dve.scalar_tensor_tensor(shift[s % 2][:, :], mv[s % 2][:, 0:2, 0], -1.0, rstd[s % 2][:, 0:2], ALU.mult, ALU.mult)\
                   .then_inc(s_shift, 1)
                landed(dve, d_out, s, h, 16, 1)
                for j in range(2, QUAD):
                    m = dve.tensor_scalar(res[s][:, j, :], hid[s % 3][:, j, :], mv[s % 2][:, j, 0:1], rstd[s % 2][:, j:j + 1],
                                          ALU.subtract, ALU.mult)
                m.then_inc(s_res, 1)

            def stat(u, s, h):
                after(dve, s_hid, u)
                after(dve, s_mv, u, 1)
                for j in range(QUAD):
                    m = dve.bn_stats(stats[:, j, :], hid[s % 3][:, j, :])
                m.then_inc(s_st, 1)

            def aggregate(u, s, h):
                after(dve, s_st, u)
                after(dve, s_rstd, u, 2)
                after(dve, s_res, u, 2)
                dve.sem_inc(e.carry, 1)
                for j in range(QUAD):
                    m = dve.bn_aggr(mv[s % 2][:, j, :], stats[:, j, :])
                m.then_inc(s_mv, 1)
            with dve.If(e.fast(dve)):
                for s in range(RING):
                    dve.memset(own[s][:, :, :], 0.0).then_inc(s_const, 1)
                dve.tensor_copy(ov_idx[:, :], by_dst.oth[:, NB:NB + 1]).then_inc(s_ovi, 1)
                dve.wait_ge(d_ov, 16)
                pipeline(dve, NQ, RING, [(2, select), (6, ratio), (5, poly), (6, mish), (3, scaled), (6, hidden), (7, norm), (6, stat), (2, beyond), (6, aggregate)], 3)

        @block.tensor
        def _(pe):
            def turn(u, s, h):
                landed(pe, d_own, s, h, 32)
                after(pe, s_ownTc, u, 1)
                pe.sem_inc(e.carry, 1)
                for j in range(QUAD):
                    m = pe.transpose(pOwn[0:R1, j * NPB:(j + 1) * NPB], own[s][:, j, :], e.ident[0:NPB, 0:NPB])
                m.then_inc(s_ownT, 1)

            def sums(u, s, h):
                after(pe, s_hot, u)
                after(pe, s_hov, u)
                after(pe, s_sumc, u, 2)
                after(pe, s_own_s, u)
                landed(pe, d_rows, s, h, 16 * QUAD)
                pe.sem_inc(e.carry, 1)
                pe.matmul(pSum[s % 2][0:D, 0:QN], ov_rows[:, 0:D], hot_ov[s % 2][:, :, :], start=True, stop=False, skip_group_check=True)
                for j in range(QUAD):
                    at = slice(j * NPB, (j + 1) * NPB)
                    pe.matmul(pSum[s % 2][0:D, at], rows[s][:, j, 0:D], hot[s % 2][:, j, :], start=False, stop=False, skip_group_check=True)
                    m = pe.matmul(pSum[s % 2][0:D, at], own_s[s % 2][:, j, :], e.ident[0:NPB, 0:NPB], start=False, stop=True,
                                  skip_group_check=True)
                m.then_inc(s_sum, 1)

            def linear(u, s, h):
                after(pe, s_sumc, u)
                after(pe, s_ownTc, u)
                after(pe, s_ty, u, 3)
                pe.sem_inc(e.carry, 1)
                for j in range(QUAD):
                    at = slice(j * NPB, (j + 1) * NPB)
                    pe.matmul(pY[s % 3][0:NPB, j * D:(j + 1) * D], sumT[s % 2][:, at], e.g_w[:, :], start=True, stop=False)
                    m = pe.matmul(pY[s % 3][0:NPB, j * D:(j + 1) * D], ownT[s % 3][:, at], e.lin_w[:, :], start=False, stop=True)
                m.then_inc(s_y, 1)
            with pe.If(e.fast(pe)):
                pe.wait_ge(s_const, RING)
                pe.wait_ge(d_ov, 16)
                pipeline(pe, NQ, RING, [(4, linear), (2, turn), (2, sums)], 3)


def general(nc, e):
    N, D, H, DH, A, ET, NT, LASTN, DUMP, ROWS = e.N, e.D, e.H, e.DH, e.A, e.ET, e.NT, e.LASTN, e.DUMP, e.ROWS
    src_i, dst_i, src_f, dst_f, ident, below, dump, ones = e.src_i, e.dst_i, e.src_f, e.dst_f, e.ident, e.below, e.dump, e.ones
    with ExitStack() as ctx:
        def sem(name):
            return ctx.enter_context(nc.semaphore("g_" + name, num=e.spare.pop()))

        dinv = ctx.enter_context(nc.sbuf_tensor("g_dinv", [P, NT], F32))

        with ExitStack() as c1:
            zero = c1.enter_context(nc.sbuf_tensor("g_zero", [P, 25 * A], F32))
            s_zero = sem("s_zero_tile")
            s_z = sem("s_sums_zeroed")
            block = c1.enter_context(nc.Block())

            @block.vector
            def _(dve):
                with dve.If(e.slow(dve)):
                    dve.memset(zero[:, :], 0.0).then_inc(s_zero, 1)

            @block.scalar
            def _(act):
                with act.If(e.slow(act)):
                    act.wait_ge(s_zero, 1)
                    n = 0
                    for tab, w in ((e.sums0, A), (e.sums1, D)):
                        flat = tab.rearrange("r w -> (r w)").rearrange("(p f) -> p f", p=P)
                        step = 25 * A
                        for c in range(0, flat.shape[1], step):
                            m = min(step, flat.shape[1] - c)
                            act.dma_start(flat[:, c:c + m], zero[:, 0:m]).then_inc(s_z, 16)
                            n += 1
                    act.wait_ge(s_z, 16 * n)

        with ExitStack() as c2:
            hi_i = c2.enter_context(nc.sbuf_tensor("hi_i", [P, ET], I32))
            lo_i = c2.enter_context(nc.sbuf_tensor("lo_i", [P, ET], I32))
            hi_f = c2.enter_context(nc.sbuf_tensor("hi_f", [P, ET], F32))
            lo_f = c2.enter_context(nc.sbuf_tensor("lo_f", [P, ET], F32))
            cols_i = c2.enter_context(nc.sbuf_tensor("cols_i", [P, NT], I32))
            cols = c2.enter_context(nc.sbuf_tensor("cols", [P, NT], F16))
            hot_hi = c2.enter_context(nc.sbuf_tensor("hot_hi", [P, 2, NT], F16))
            hot_lo = c2.enter_context(nc.sbuf_tensor("hot_lo", [P, 2, P], F16))
            logdeg = c2.enter_context(nc.sbuf_tensor("logdeg", [P, NT], F32))
            deg = c2.enter_context(nc.psum_tensor("deg", [P, NT], F32))
            s_iota = sem("s_iota")
            s_hot = sem("s_one_hots")
            s_cnt = sem("s_counted")
            s_k = sem("s_keys_split")
            s_log = sem("s_logdeg")
            block = c2.enter_context(nc.Block())

            @block.gpsimd
            def _(pool):
                with pool.If(e.slow(pool)):
                    pool.iota(cols_i[:, :], pattern=[[1, NT]], base=0, channel_multiplier=0).then_inc(s_iota, 1)

            @block.vector
            def _(dve):
                with dve.If(e.slow(dve)):
                    dve.wait_ge(s_iota, 1)
                    dve.tensor_copy(cols[:, :], cols_i[:, :]).then_inc(s_k, 1)
                    dve.tensor_copy(lo_i[:, :], dst_f[:, :]).then_inc(s_k, 1)
                    dve.wait_ge(s_k, 2)
                    dve.tensor_single_scalar(hi_i[:, :], lo_i[:, :], 7, ALU.arith_shift_right).then_inc(s_k, 1)
                    dve.wait_ge(s_k, 3)
                    dve.tensor_single_scalar(lo_i[:, :], lo_i[:, :], P - 1, ALU.bitwise_and).then_inc(s_k, 1)
                    dve.wait_ge(s_k, 4)
                    dve.tensor_copy(hi_f[:, :], hi_i[:, :]).then_inc(s_k, 1)
                    dve.tensor_copy(lo_f[:, :], lo_i[:, :]).then_inc(s_k, 1)
                    dve.wait_ge(s_k, 6)
                    for b in range(2):
                        dve.tensor_scalar(hot_hi[:, b, :], cols[:, :], hi_f[:, b:b + 1], None, ALU.is_equal).then_inc(s_hot, 1)
                        dve.tensor_scalar(hot_lo[:, b, :], cols[:, 0:P], lo_f[:, b:b + 1], None, ALU.is_equal).then_inc(s_hot, 1)
                    with dve.Fori(1, ET // 2) as i:
                        for b in range(2):
                            dve.wait_ge(s_cnt, i * 2 + b - 1)
                            dve.tensor_scalar(hot_hi[:, b, :], cols[:, :], hi_f[:, bass.ds(i * 2 + b, 1)], None, ALU.is_equal).then_inc(s_hot, 1)
                            dve.tensor_scalar(hot_lo[:, b, :], cols[:, 0:P], lo_f[:, bass.ds(i * 2 + b, 1)], None, ALU.is_equal).then_inc(s_hot, 1)

            @block.tensor
            def _(pe):
                with pe.If(e.slow(pe)):
                    for t in range(2):
                        pe.wait_ge(s_hot, 2 * t + 2)
                        pe.matmul(deg[:, :], hot_lo[:, t, :], hot_hi[:, t, :], start=(t == 0), stop=False, skip_group_check=True).then_inc(s_cnt, 1)
                    with pe.Fori(1, ET // 2) as i:
                        for b in range(2):
                            pe.wait_ge(s_hot, i * 4 + 2 * b + 2)
                            pe.matmul(deg[:, :], hot_lo[:, b, :], hot_hi[:, b, :], start=False, stop=(b == 1), skip_group_check=True).then_inc(s_cnt, 1)

            @block.scalar
            def _(act):
                with act.If(e.slow(act)):
                    act.preload_act_table_set(ACT_SET)
                    act.wait_ge(s_cnt, ET)
                    act.activation(logdeg[:, :], deg[:, :], ACT.Ln, bias=ones[:, 0:1]).then_inc(s_log, 1)
                    act.wait_ge(s_log, 1)
                    act.activation(dinv[:, :], logdeg[:, :], ACT.Exp, scale=-0.5).then_inc(s_log, 1)
                    act.wait_ge(s_log, 2)

        with ExitStack() as c3:
            def tsb(name, shape, dt=F32):
                return c3.enter_context(nc.sbuf_tensor(name, shape, dt))

            def bank(name):
                return c3.enter_context(nc.psum_tensor(name, [P, 512], F32))

            gs = tsb("e_gs", [P, 1], I32)
            gd = tsb("e_gd", [P, 1], I32)
            key = tsb("e_key", [P, 1])
            off = tsb("e_off", [P, 1])
            tidx = tsb("e_tidx", [P, 1], I32)
            rank = tsb("e_rank", [P, 1])
            move = tsb("e_move", [P, 1])
            rows = tsb("e_rows", [P, 2, D])
            rowsT = tsb("e_rowsT", [D, 2, P])
            same = tsb("e_same", [P, P])
            junk = tsb("e_junk", [P, P])
            q_sb = tsb("e_q", [P, D])
            prod = tsb("e_prod", [P, D])
            score = tsb("e_score", [P, H])
            contrib = tsb("e_contrib", [P, A])
            total = tsb("e_total", [P, A])
            pT = bank("e_pT")[:, 0:2 * P].rearrange("p (a b) -> p a b", a=2)
            pkey = bank("e_pkey")[:, 0:P]
            pq = bank("e_pq")[:, 0:D]
            pkv = bank("e_pkv")[:, 0:2 * D]
            ptot = bank("e_ptot")[:, 0:A]

            for layer in range(2):
                W = A if layer == 0 else D
                table = e.sums0 if layer == 0 else e.sums1
                key_all = src_f if layer == 0 else dst_f
                with ExitStack() as c4:
                    L = f"l{layer}_"
                    s_st = sem(L + "s_staged")
                    s_rows = sem(L + "s_rows")
                    s_T = sem(L + "s_transposed")
                    s_Tc = sem(L + "s_transposed_copied")
                    s_qkv = sem(L + "s_qkv")
                    s_q = sem(L + "s_q_copied")
                    s_dve = sem(L + "s_dve_steps")
                    s_sc = sem(L + "s_scores")
                    s_e = sem(L + "s_exp")
                    s_con = sem(L + "s_contrib")
                    s_tot = sem(L + "s_totals")
                    s_totc = sem(L + "s_totals_copied")
                    s_add = sem(L + "s_added")
                    s_carry = sem(L + "s_carry")
                    block = c4.enter_context(nc.Block())
                    DVE_STEPS = 13 if layer == 0 else 8

                    @block.vector
                    def _(dve):
                        with dve.If(e.slow(dve)):
                            with dve.Fori(0, ET) as i:
                                st = Steps(dve, s_dve, DVE_STEPS, i)
                                dve.wait_ge(s_add, i * 16)
                                dve.tensor_copy(gs[:, :], src_i[:, bass.ds(i, 1)]).then_inc(s_st, 1)
                                dve.tensor_copy(gd[:, :], dst_i[:, bass.ds(i, 1)]).then_inc(s_st, 1)
                                dve.tensor_copy(key[:, :], key_all[:, bass.ds(i, 1)]).then_inc(s_st, 1)
                                dve.wait_ge(s_st, i * 3 + 3)
                                st.done(dve.tensor_tensor(off[:, :], dump[:, :], key[:, :], ALU.subtract))
                                dve.wait_ge(s_T, i + 1)
                                st.done(dve.tensor_scalar(same[:, :], pkey[:, :], key[:, 0:1], None, ALU.is_equal))
                                st.done(dve.tensor_tensor(junk[:, :], same[:, :], below[:, :], ALU.mult))
                                st.done(dve.tensor_reduce(rank[:, :], junk[:, :], AX, ALU.add))
                                st.done(dve.tensor_scalar(rank[:, :], rank[:, :], 0.0, None, ALU.is_gt))
                                st.done(dve.tensor_tensor(move[:, :], rank[:, :], off[:, :], ALU.mult))
                                st.done(dve.tensor_tensor(tidx[:, :], key[:, :], move[:, :], ALU.add))
                                if layer == 0:
                                    dve.wait_ge(s_qkv, i + 1)
                                    dve.wait_ge(s_q, i + 1)
                                    st.done(dve.tensor_tensor(prod[:, :], q_sb[:, :], pkv[:, 0:D], ALU.mult))
                                    st.done(dve.tensor_reduce(score[:, :], prod[:, :].rearrange("p (h d) -> p h d", h=H), AX, ALU.add))
                                    st.done(dve.tensor_scalar(score[:, :], score[:, :], 10.0, -10.0, ALU.min, ALU.max))
                                    dve.sem_inc(s_sc, 1)
                                    dve.wait_ge(s_e, i + 1)
                                    e_b = contrib[:, D:A].unsqueeze(2).to_broadcast([P, H, DH])
                                    st.done(dve.tensor_tensor(contrib[:, 0:D].rearrange("p (h d) -> p h d", h=H),
                                                              pkv[:, D:2 * D].rearrange("p (h d) -> p h d", h=H), e_b, ALU.mult))
                                    st.done(dve.tensor_copy(junk[:, 0:1], rank[:, :]))
                                dve.sem_inc(s_con, 1)
                                dve.wait_ge(s_tot, i + 1)
                                st.done(dve.tensor_copy(total[:, 0:W], ptot[:, 0:W]))
                                dve.sem_inc(s_totc, 1)
                                st.end()

                    @block.gpsimd
                    def _(pool):
                        with pool.If(e.slow(pool)):
                            with pool.Fori(0, ET) as i:
                                pool.wait_ge(s_st, i * 3 + 3)
                                pool.sem_inc(s_carry, 1)
                                if layer == 0:
                                    pool.indirect_dma_start(rows[:, 0, :], None, e.x[:, :],
                                                            bass.IndirectOffsetOnAxis(ap=gs[:, 0:1], axis=0)).then_inc(s_rows, 16)
                                    pool.indirect_dma_start(rows[:, 1, :], None, e.x[:, :],
                                                            bass.IndirectOffsetOnAxis(ap=gd[:, 0:1], axis=0)).then_inc(s_rows, 16)
                                else:
                                    pool.indirect_dma_start(rows[:, 0, :], None, e.x1s_plain[:, :],
                                                            bass.IndirectOffsetOnAxis(ap=gs[:, 0:1], axis=0)).then_inc(s_rows, 16)
                                pool.wait_ge(s_totc, i + 1)
                                pool.sem_inc(s_carry, 1)
                                pool.indirect_dma_start(table[:, :], bass.IndirectOffsetOnAxis(ap=tidx[:, 0:1], axis=0),
                                                        total[:, 0:W], None, compute_op=ALU.add).then_inc(s_add, 16)
                            pool.wait_ge(s_add, 16 * ET)

                    @block.tensor
                    def _(pe):
                        with pe.If(e.slow(pe)):
                            with pe.Fori(0, ET) as i:
                                pe.wait_ge(s_st, i * 3 + 3)
                                t = pe.transpose(pkey[:, :], key[:, 0:1].to_broadcast([P, P]), ident[:, :])
                                if layer == 0:
                                    pe.wait_ge(s_rows, i * 32 + 32)
                                    pe.sem_inc(s_carry, 1)
                                    pe.transpose(pT[0:D, 0, :], rows[:, 0, :], ident[:, :])
                                    t = pe.transpose(pT[0:D, 1, :], rows[:, 1, :], ident[:, :])
                                t.then_inc(s_T, 1)
                                if layer == 0:
                                    pe.wait_ge(s_Tc, i + 1)
                                    pe.sem_inc(s_carry, 1)
                                    pe.matmul(pq[:, :], rowsT[:, 0, :], e.q_w[:, :], start=True, stop=True)
                                    pe.matmul(pkv[:, :], rowsT[:, 1, :], e.kv_w[:, :], start=True, stop=True).then_inc(s_qkv, 1)
                                pe.wait_ge(s_con, i + 1)
                                if layer == 1:
                                    pe.wait_ge(s_rows, i * 16 + 16)
                                pe.sem_inc(s_carry, 1)
                                pe.matmul(ptot[:, 0:W], same[:, :], contrib[:, 0:W] if layer == 0 else rows[:, 0, :],
                                          start=True, stop=True).then_inc(s_tot, 1)

                    if layer == 0:
                        @block.scalar
                        def _(act):
                            with act.If(e.slow(act)):
                                act.preload_act_table_set(ACT_SET)
                                with act.Fori(0, ET) as i:
                                    act.wait_ge(s_T, i + 1)
                                    act.activation(rowsT[:, :, :], pT[0:D, 0:2, :], ACT.Copy).then_inc(s_Tc, 1)
                                    act.wait_ge(s_qkv, i + 1)
                                    act.activation(q_sb[:, :], pq[:, :], ACT.Copy).then_inc(s_q, 1)
                                    act.wait_ge(s_sc, i + 1)
                                    act.activation(contrib[:, D:A], score[:, :], ACT.Exp).then_inc(s_e, 1)

                if layer == 0:
                    dense(nc, e, dinv, 0)
        dense(nc, e, dinv, 1)



def dense(nc, e, dinv, layer):
    N, D, H, DH, NT, A, LASTN = e.N, e.D, e.H, e.DH, e.NT, e.A, e.LASTN
    ident, ones, eps, bias2 = e.ident, e.ones, e.eps, e.bias2
    with ExitStack() as c:
        L = f"d{layer}_"

        def tsb(name, shape, dt=F32):
            return c.enter_context(nc.sbuf_tensor(L + name, shape, dt))

        def sem(name):
            return c.enter_context(nc.semaphore(L + name, num=e.spare.pop()))

        xin = tsb("xin", [P, D])
        acc = tsb("acc", [P, A])
        agg = tsb("agg", [P, D])
        own = tsb("own", [P, D])
        rec = tsb("rec", [P, H])
        h = tsb("h", [P, D])
        stats = tsb("stats", [P, 6])
        mv = tsb("mv", [P, 2])
        lnv = tsb("lnv", [P, 1])
        rstd = tsb("rstd", [P, 1])
        y1 = tsb("y1", [P, D])
        y2 = tsb("y2", [P, D])
        rT = tsb("rT", [D, 2, P])
        num = tsb("num", [P, D])
        den = tsb("den", [P, D])
        pT = c.enter_context(nc.psum_tensor(L + "pT", [P, 512], F32))[0:D, 0:2 * P].rearrange("p (a b) -> p a b", a=2)
        py = c.enter_context(nc.psum_tensor(L + "py", [P, 512], F32))[:, 0:D]
        s_in = sem("s_in")
        s_dve = sem("s_dve_steps")
        s_var = sem("s_var")
        s_rstd = sem("s_rstd")
        s_y = sem("s_y")
        s_out = sem("s_out")
        s_act = sem("s_act_steps")
        s_agg = sem("s_agg")
        s_T = sem("s_T")
        s_Tc = sem("s_Tc")
        s_lin = sem("s_lin")
        s_e = sem("s_exp")
        s_cap = sem("s_cap")
        s_carry = sem("s_carry")
        s_bn = sem("s_bn")
        block = c.enter_context(nc.Block())
        full = NT - 1
        INS = 2 if layer == 0 else 3
        OUTS = 2 if layer == 0 else 1
        DVE_STEPS = 9 if layer == 0 else 12

        def loop(eng, body):
            with eng.Fori(0, full) as i:
                body(i, P)
            body(full, LASTN)

        @block.sync
        def _(sp):
            with sp.If(e.slow(sp)):
                def body(i, n):
                    at = bass.ds(i * P, n)
                    sp.wait_ge(s_out, i * OUTS * 16)
                    if layer == 0:
                        sp.dma_start(xin[0:n, :], e.x[at, :]).then_inc(s_in, 16)
                        sp.dma_start(acc[0:n, :], e.sums0[at, :]).then_inc(s_in, 16)
                    else:
                        sp.dma_start(xin[0:n, :], e.x1_plain[at, :]).then_inc(s_in, 16)
                        sp.dma_start(own[0:n, :], e.x1s_plain[at, :]).then_inc(s_in, 16)
                        sp.dma_start(acc[0:n, 0:D], e.sums1[at, :]).then_inc(s_in, 16)
                    sp.wait_ge(s_y, i + 1)
                    if layer == 0:
                        sp.dma_start(e.x1_plain[at, :], y1[0:n, :]).then_inc(s_out, 16)
                        sp.dma_start(e.x1s_plain[at, :], y2[0:n, :]).then_inc(s_out, 16)
                    else:
                        sp.dma_start(e.out[at, :], y1[0:n, :]).then_inc(s_out, 16)
                loop(sp, body)
                sp.wait_ge(s_out, NT * OUTS * 16)

        @block.vector
        def _(dve):
            with dve.If(e.slow(dve)):
                def body(i, n):
                    st = Steps(dve, s_dve, DVE_STEPS, i)
                    dve.wait_ge(s_in, (i + 1) * INS * 16)
                    if layer == 0:
                        st.done(dve.tensor_scalar(rec[0:n, :], acc[0:n, D:A], 1e-8, None, ALU.add))
                        st.done(dve.reciprocal(rec[0:n, :], rec[0:n, :]))
                        st.done(dve.tensor_tensor(h[0:n, :].rearrange("p (h d) -> p h d", h=H),
                                                  acc[0:n, 0:D].rearrange("p (h d) -> p h d", h=H),
                                                  rec[0:n, :].unsqueeze(2).to_broadcast([n, H, DH]), ALU.mult))
                        st.done(dve.scalar_tensor_tensor(h[0:n, :], xin[0:n, :], 2.0, h[0:n, :], ALU.mult, ALU.add))
                    else:
                        st.done(dve.tensor_tensor(agg[0:n, :], acc[0:n, 0:D], own[0:n, :], ALU.add))
                        st.done(dve.tensor_scalar(agg[0:n, :], agg[0:n, :], dinv[0:n, bass.ds(i, 1)], None, ALU.mult))
                        dve.sem_inc(s_agg, 1)
                        dve.wait_ge(s_lin, i + 1)
                        st.done(dve.tensor_scalar(h[0:n, :], py[0:n, :], 20.0, None, ALU.min))
                        dve.sem_inc(s_cap, 1)
                        dve.wait_ge(s_e, i + 1)
                        st.done(dve.scalar_tensor_tensor(num[0:n, :], y2[0:n, :], 2.0, y2[0:n, :], ALU.add, ALU.mult))
                        st.done(dve.tensor_scalar(den[0:n, :], num[0:n, :], 2.0, None, ALU.add))
                        st.done(dve.reciprocal(den[0:n, :], den[0:n, :]))
                        st.done(dve.tensor_tensor(num[0:n, :], num[0:n, :], den[0:n, :], ALU.mult))
                        st.done(dve.tensor_tensor(num[0:n, :], num[0:n, :], py[0:n, :], ALU.mult))
                        st.done(dve.tensor_tensor(h[0:n, :], num[0:n, :], xin[0:n, :], ALU.add))
                    st.done(dve.bn_stats(stats[0:n, :], h[0:n, :]))
                    dve.sem_inc(s_bn, 1)
                    st.done(dve.bn_aggr(mv[0:n, :], stats[0:n, :]))
                    dve.sem_inc(s_var, 1)
                    dve.wait_ge(s_rstd, i + 1)
                    st.done(dve.tensor_scalar(y1[0:n, :], h[0:n, :], mv[0:n, 0:1], rstd[0:n, :], ALU.subtract, ALU.mult))
                    if layer == 0:
                        st.done(dve.tensor_scalar(y2[0:n, :], y1[0:n, :], dinv[0:n, bass.ds(i, 1)], None, ALU.mult))
                        st.done(dve.tensor_copy(lnv[0:n, :], rstd[0:n, :]))
                    dve.sem_inc(s_y, 1)
                    st.end()
                loop(dve, body)

        if layer == 1:
            @block.tensor
            def _(pe):
                with pe.If(e.slow(pe)):
                    def body(i, n):
                        pe.wait_ge(s_agg, i + 1)
                        pe.sem_inc(s_carry, 1)
                        pe.transpose(pT[:, 0, 0:n], agg[0:n, :], ident[0:n, 0:n])
                        pe.transpose(pT[:, 1, 0:n], xin[0:n, :], ident[0:n, 0:n]).then_inc(s_T, 1)
                        pe.wait_ge(s_Tc, i + 1)
                        pe.sem_inc(s_carry, 1)
                        pe.matmul(py[0:n, :], rT[:, 0, 0:n], e.g_w[:, :], start=True, stop=False)
                        pe.matmul(py[0:n, :], rT[:, 1, 0:n], e.lin_w[0:D, :], start=False, stop=False)
                        pe.matmul(py[0:n, :], ones[0:2, 0:n], bias2[:, :], start=False, stop=True).then_inc(s_lin, 1)
                    loop(pe, body)

        @block.scalar
        def _(act):
            with act.If(e.slow(act)):
                def body(i, n):
                    if layer == 1:
                        act.wait_ge(s_T, i + 1)
                        act.activation(rT[:, :, 0:n], pT[:, :, 0:n], ACT.Copy).then_inc(s_Tc, 1)
                        act.wait_ge(s_cap, i + 1)
                        act.activation(y2[0:n, :], h[0:n, :], ACT.Exp).then_inc(s_e, 1)
                    act.wait_ge(s_var, i + 1)
                    act.activation(lnv[0:n, :], mv[0:n, 1:2], ACT.Ln, bias=eps[0:n, :]).then_inc(s_act, 1)
                    act.wait_ge(s_act, i + 1)
                    act.activation(rstd[0:n, :], lnv[0:n, :], ACT.Exp, scale=-0.5).then_inc(s_rstd, 1)
                act.preload_act_table_set(ACT_SET)
                loop(act, body)


def gnn(nc, x, src, dst, qW, kW, vW, gW, gb, lW, lb, out):
    N, D = x.shape
    E = src.shape[0]
    H = 4
    NPB = 108
    NQ = -(-N // (QUAD * NPB))
    NB = NQ * QUAD
    ET = -(-E // P)
    ET += -ET % 28
    LASTE = E - (P - 1) * ET
    NT = -(-N // P)
    A = D + H
    R1 = D + 4
    DUMP = N
    ROWS = N + P + (-(N + P)) % P
    assert NB + 2 <= 512 and ET <= 512 and N < 2 ** 16 and NPB < P and NQ % 4 == 0
    assert (N - (NQ - 1) * QUAD * NPB) % QUAD == 0

    with ExitStack() as ctx:
        def sb(name, shape, dt=F32):
            return ctx.enter_context(nc.sbuf_tensor(name, shape, dt))

        def sem(name):
            return ctx.enter_context(nc.semaphore(name))

        e = Shared()
        e.N, e.D, e.H, e.DH, e.A, e.R1 = N, D, H, D // H, A, R1
        e.NB, e.NPB, e.NQ, e.ET, e.NT, e.LASTN, e.DUMP, e.ROWS = NB, NPB, NQ, ET, NT, N - (NT - 1) * P, DUMP, ROWS
        e.x, e.out, e.spare = x, out, []
        e.steps, e.steps_done = sem("s_steps"), 0
        e.carry = sem("s_carry")
        e.sums0 = nc.dram_tensor("sums0", (ROWS, A), F32).ap()
        e.sums1 = nc.dram_tensor("sums1", (ROWS, D), F32).ap()
        e.x1_plain = nc.dram_tensor("x1_plain", (N, D), F32).ap()
        e.x1s_plain = nc.dram_tensor("x1s_plain", (N, D), F32).ap()
        e.x1_rows = nc.dram_tensor("x1_rows", (N, R1), F32).ap()
        e.dinv_rows = nc.dram_tensor("dinv_rows", (NB, NPB), F32).ap()

        e.src_i = sb("src_i", [P, ET], I32)
        e.dst_i = sb("dst_i", [P, ET], I32)
        e.src_f = sb("src_f", [P, ET])
        e.dst_f = sb("dst_f", [P, ET])
        e.q_w = sb("q_w", [D, D])
        e.kv_w = sb("kv_w", [D, 2 * D])
        e.g_w = sb("g_w", [D, D])
        e.lin_w = sb("lin_w", [R1, D])
        e.bias2 = sb("bias2", [2, D])
        e.ones = sb("ones", [P, P])
        e.ones16 = sb("ones16", [P, P], F16)
        e.ident = sb("ident", [P, P])
        e.ident16 = sb("ident16", [P, P], F16)
        e.below = sb("below", [P, P])
        e.earlier16 = sb("earlier16", [P, P], F16)
        e.not_before = sb("not_before", [P, P], F16)
        e.dump = sb("dump", [P, 1])
        e.iota = sb("iota", [P, P])
        e.iota16 = sb("iota16", [P, NB + 2], F16)
        e.quad_rows = sb("quad_rows", [P, QUAD, NPB])
        e.quad_start = sb("quad_start", [P, NQ])
        e.eps, e.minus_one, e.two, e.twenty = [sb(n, [P, 1]) for n in ("eps", "minus_one", "two", "twenty")]
        e.over = sb("over", [P, 2])
        e.flag = sb("flag", [P, 1], I32)
        e.dinv_b = sb("dinv_b", [NPB, NB])
        tables = []
        for t in ("src", "dst"):
            v = Shared()
            v.oth, v.lo = sb(t + "_oth", [P, NB + 1]), sb(t + "_lo", [P, NB + 1])
            v.ov_b, v.ov_key, v.ov_row = sb(t + "_ov_b", [P, 1]), sb(t + "_ov_key", [P, 1]), sb(t + "_ov_row", [P, NQ])
            tables.append(v)
        e.fast = lambda eng: eng.value_load(e.flag[0:1, 0:1], min_val=0, max_val=1) < 1
        e.slow = lambda eng: eng.value_load(e.flag[0:1, 0:1], min_val=0, max_val=1) > 0

        with ExitStack() as c1:
            s_ld, s_w, s_pad, s_c, s_d, s_lin = [c1.enter_context(nc.semaphore(n)) for n in
                                                 ("s_edges", "s_weights", "s_pads_set", "s_pool_constants", "s_dve_constants", "s_lin")]
            ints = c1.enter_context(nc.sbuf_tensor("ints", [P, 512], I32))
            ints_q = c1.enter_context(nc.sbuf_tensor("ints_q", [P, QUAD, NPB], I32))
            ints_s = c1.enter_context(nc.sbuf_tensor("ints_s", [P, NQ], I32))
            ints_d = c1.enter_context(nc.sbuf_tensor("ints_d", [P, 1], I32))
            block = c1.enter_context(nc.Block())

            @block.sync
            def _(sp):
                sp.wait_ge(s_pad, 2)
                for t, s in ((e.src_i, src), (e.dst_i, dst)):
                    sp.dma_start(t[0:P - 1, :], s[0:(P - 1) * ET].rearrange("(p t) -> p t", t=ET)).then_inc(s_ld, 16)
                    sp.dma_start(t[P - 1:P, 0:LASTE], s[(P - 1) * ET:E].rearrange("(p t) -> p t", p=1)).then_inc(s_ld, 16)
                sp.wait_ge(s_lin, 1)
                for t, s in ((e.q_w[:, :], qW), (e.kv_w[:, 0:D], kW), (e.kv_w[:, D:2 * D], vW), (e.g_w[:, :], gW), (e.lin_w[0:D, :], lW)):
                    sp.dma_start(t, s).then_inc(s_w, 16)
                for r, s in enumerate((gb, lb)):
                    sp.dma_start(e.bias2[r:r + 1, :], s.rearrange("(a n) -> a n", a=1)).then_inc(s_w, 16)
                    sp.dma_start(e.lin_w[D + 1 + r:D + 2 + r, :], s.rearrange("(a n) -> a n", a=1)).then_inc(s_w, 16)
                sp.wait_ge(s_w, 16 * 9)
                sp.wait_ge(s_ld, 16 * 4)

            @block.gpsimd
            def _(pool):
                pool.iota(ints[:, :], pattern=[[1, 512]], base=0, channel_multiplier=0).then_inc(s_c, 1)
                pool.iota(ints_q[:, :, :], pattern=[[1, QUAD], [QUAD, NPB]], base=0, channel_multiplier=0).then_inc(s_c, 1)
                pool.iota(ints_s[:, :], pattern=[[QUAD * NPB, NQ]], base=0, channel_multiplier=0).then_inc(s_c, 1)
                pool.iota(ints_d[:, :], pattern=[[0, 1]], base=DUMP, channel_multiplier=1).then_inc(s_c, 1)
                for t in (e.ident, e.ident16, e.below, e.not_before):
                    pool.memset(t[:, :], 0.0).then_inc(s_c, 1)
                pool.memset(e.earlier16[:, :], 1.0).then_inc(s_c, 1)
                pool.wait_ge(s_c, 9)
                for t in (e.ident, e.ident16):
                    pool.affine_select(out=t[:, :], in_=t[:, :], compare_op=ALU.not_equal, fill=1.0,
                                       base=0, pattern=[[-1, P]], channel_multiplier=1).then_inc(s_c, 1)
                pool.affine_select(out=e.below[:, :], in_=e.below[:, :], compare_op=ALU.is_ge, fill=1.0,
                                   base=0, pattern=[[1, P]], channel_multiplier=-1).then_inc(s_c, 1)
                pool.affine_select(out=e.not_before[:, :], in_=e.not_before[:, :], compare_op=ALU.is_gt, fill=-2.0,
                                   base=0, pattern=[[-1, P]], channel_multiplier=1).then_inc(s_c, 1)
                pool.affine_select(out=e.earlier16[:, :], in_=e.earlier16[:, :], compare_op=ALU.is_gt, fill=0.0,
                                   base=0, pattern=[[1, P]], channel_multiplier=-1).then_inc(s_c, 1)
                pool.wait_ge(s_c, 14)

            @block.vector
            def _(dve):
                dve.memset(e.src_i[:, :], DUMP + P - 1).then_inc(s_pad, 1)
                dve.memset(e.dst_i[:, :], DUMP + P - 1).then_inc(s_pad, 1)
                dve.memset(e.lin_w[:, :], 0.0).then_inc(s_lin, 1)
                for t, v in ((e.ones, 1.0), (e.ones16, 1.0), (e.eps, EPS_LN), (e.minus_one, -1.0), (e.two, 2.0), (e.twenty, 20.0)):
                    dve.memset(t[:, :], v).then_inc(s_d, 1)
                dve.wait_ge(s_c, 4)
                dve.tensor_copy(e.dump[:, :], ints_d[:, :]).then_inc(s_d, 1)
                dve.tensor_copy(e.iota[:, :], ints[:, 0:P]).then_inc(s_d, 1)
                dve.tensor_copy(e.iota16[:, :], ints[:, 0:NB + 2]).then_inc(s_d, 1)
                dve.tensor_copy(e.quad_rows[:, :, :], ints_q[:, :, :]).then_inc(s_d, 1)
                dve.tensor_copy(e.quad_start[:, :], ints_s[:, :]).then_inc(s_d, 1)
                dve.wait_ge(s_ld, 16 * 4)
                dve.tensor_copy(e.src_f[:, :], e.src_i[:, :]).then_inc(s_pad, 1)
                dve.tensor_copy(e.dst_f[:, :], e.dst_i[:, :]).then_inc(s_pad, 1)
                dve.wait_ge(s_pad, 4)
                dve.tensor_scalar_min(e.src_i[:, :], e.src_f[:, :], float(N - 1)).then_inc(s_pad, 1)
                dve.tensor_scalar_min(e.dst_i[:, :], e.dst_f[:, :], float(N - 1)).then_inc(s_pad, 1)
                dve.wait_ge(s_pad, 6)
                dve.wait_ge(s_d, 11)

        for k, (t, key, other) in enumerate((("src", e.src_f, e.dst_f), ("dst", e.dst_f, e.src_f))):
            v = tables[k]
            e.oth, e.lo, e.ov_b, e.ov_key, e.ov_row, e.over_at = v.oth, v.lo, v.ov_b, v.ov_key, v.ov_row, k
            slots_by_block(nc, e, t + "_", key[:, :], other[:, :])
        with ExitStack() as c1:
            block = c1.enter_context(nc.Block())

            @block.vector
            def _(dve):
                ch = Chain(dve, e)
                ch.done(dve.tensor_tensor(e.over[:, 0:1], e.over[:, 0:1], e.over[:, 1:2], ALU.max))
                ch.done(dve.tensor_scalar(e.flag[:, :], e.over[:, 0:1], float(P), None, ALU.is_gt))

        degrees(nc, e, tables[1])
        attention(nc, e, tables[0])
        convolution(nc, e, tables[1])
        general(nc, e)


def kernel(**inputs):
    import numpy as np
    import concourse.bacc as bacc
    from concourse.bass_utils import run_bass_kernel_spmd
    nc = bacc.Bacc("TRN2", target_bir_lowering=False, num_devices=1)
    names = ("x", "src", "dst", "L0_gnn_qW", "L0_gnn_kW", "L0_gnn_vW",
             "L1_gnn_W_gcn", "L1_gnn_b_gcn", "L1_gnn_W_lin", "L1_gnn_b_lin")
    arrays, aps = {}, []
    for n in names:
        a = np.ascontiguousarray(inputs[n])
        arrays["in_" + n] = a
        aps.append(nc.dram_tensor("in_" + n, a.shape, mybir.dt.from_np(a.dtype), kind="ExternalInput").ap())
    out = nc.dram_tensor("out", inputs["x"].shape, F32, kind="ExternalOutput").ap()
    gnn(nc, *aps, out)
    r = run_bass_kernel_spmd(nc, [arrays], core_ids=[0])
    return r.results[0]["out"]
```
